# Optimizing a Trainium2 kernel written in Bass

```python
import numpy as np
import jax
import jax.numpy as jnp

def _softmax(x, axis=-1):
    return jax.nn.softmax(x, axis=axis)

def _gelu(x):
    return jax.nn.gelu(x, approximate=True)

def _silu(x):
    return jax.nn.silu(x)

def _sigmoid(x):
    return jax.nn.sigmoid(x)

def _layernorm(x, axis=-1, eps=1e-05):
    m = jnp.mean(x, axis=axis, keepdims=True)
    v = jnp.var(x, axis=axis, keepdims=True)
    return (x - m) / jnp.sqrt(v + eps)

def _scatter_add(tgt, idx, src, axis=0):
    return tgt.at[idx].add(src)

def _segment_sum(src, seg, n):
    return jax.ops.segment_sum(src, seg, n)
kernel_name = 'mk_early_fusion_d1_tok_img768_r4_517c34'

def setup_inputs(seed: int=0):
    np.random.seed(seed)
    _w = jnp.asarray

    def _rec_inputs():
        import jax
        import jax.numpy as jnp
        _rk = jax.random.key(seed)
        x = -0.000356955 + 1 * jax.random.normal(jax.random.fold_in(_rk, 1), (8, 3, 128, 128), jnp.float32)
        txt = 0.000273629 + 0.577477 * jax.random.normal(jax.random.fold_in(_rk, 2), (8, 128, 192), jnp.float32)
        return (x, txt)
    x, txt = _rec_inputs()

    def _L0_tok_setup():
        import jax, jax.numpy as jnp
        import numpy as np
        IMAGE_SIZE = 224
        PATCH = 16
        HIDDEN = 192
        C = 3
        key = jax.random.key(seed)
        k1, k2, k3 = jax.random.split(key, 3)
        img = jax.random.normal(k1, (128, C, IMAGE_SIZE, IMAGE_SIZE), dtype=jnp.float32)
        d_in = C * PATCH * PATCH
        bound = 1.0 / np.sqrt(d_in)
        W = jax.random.uniform(k2, (HIDDEN, d_in), jnp.float32, -bound, bound)
        b = jax.random.uniform(k3, (HIDDEN,), jnp.float32, -bound, bound)
        return {'img': img, 'W': W, 'b': b}
    _L0_tok_all = _L0_tok_setup()
    _L0_tok_in = {k: v for k, v in _L0_tok_all.items() if k in ('W', 'b')}
    del _L0_tok_all

    def _L0_attn_setup():
        import jax, jax.numpy as jnp
        import numpy as np
        NUM_HEADS = 12
        WINDOW = 64
        LN_EPS = 1e-05

        def _ln(x, g, b):
            m = x.mean(-1, keepdims=True)
            v = x.var(-1, keepdims=True)
            return (x - m) / jnp.sqrt(v + LN_EPS) * g + b
        key = jax.random.key(seed)
        ks = jax.random.split(key, 10)
        B, L, D = (1, 512, 192)
        s = 0.02

        def w(k, shape):
            return jax.random.normal(k, shape, jnp.float32) * s
        return {'x': jax.random.normal(ks[0], (B, L, D), jnp.float32), 'ln1_g': jnp.ones((D,), jnp.float32), 'ln1_b': jnp.zeros((D,), jnp.float32), 'attn_qkv_w': w(ks[1], (D, 3 * D)), 'attn_qkv_b': jnp.zeros((3 * D,), jnp.float32), 'attn_proj_w': w(ks[2], (D, D)), 'attn_proj_b': jnp.zeros((D,), jnp.float32), 'ssm_qkv_w': w(ks[3], (D, 3 * D)), 'ssm_qkv_b': jnp.zeros((3 * D,), jnp.float32), 'ssm_out_w': w(ks[4], (D, D)), 'ssm_out_b': jnp.zeros((D,), jnp.float32), 'ssm_ln_g': jnp.ones((D,), jnp.float32), 'ssm_ln_b': jnp.zeros((D,), jnp.float32), 'out_w': w(ks[5], (D, D)), 'out_b': jnp.zeros((D,), jnp.float32), 'mlp_w1': w(ks[6], (D, 4 * D)), 'mlp_b1': jnp.zeros((4 * D,), jnp.float32), 'mlp_w2': w(ks[7], (4 * D, D)), 'mlp_b2': jnp.zeros((D,), jnp.float32), 'lnm_g': jnp.ones((D,), jnp.float32), 'lnm_b': jnp.zeros((D,), jnp.float32)}
    _L0_attn_all = _L0_attn_setup()
    _L0_attn_in = {k: v for k, v in _L0_attn_all.items() if k in ('ln1_g', 'ln1_b', 'attn_qkv_w', 'attn_qkv_b', 'attn_proj_w', 'attn_proj_b', 'ssm_qkv_w', 'ssm_qkv_b', 'ssm_out_w', 'ssm_out_b', 'ssm_ln_g', 'ssm_ln_b', 'out_w', 'out_b', 'mlp_w1', 'mlp_b1', 'mlp_w2', 'mlp_b2', 'lnm_g', 'lnm_b')}
    del _L0_attn_all

    def _L0_ffn_setup():
        import math
        import jax, jax.numpy as jnp
        import numpy as np
        N_HEAD = 12
        N_EXP = 8
        TOP_K = 2
        TRAIN_CAPACITY = 1.25
        MIN_CAPACITY = 4
        LN_EPS = 1e-05
        NEG_INF = -1e+30

        def _layer_norm(x, w, b):
            mu = jnp.mean(x, axis=-1, keepdims=True)
            var = jnp.var(x, axis=-1, keepdims=True)
            return (x - mu) * jax.lax.rsqrt(var + LN_EPS) * w + b

        def _attention(x, qkv_w, qkv_b, proj_w, proj_b):
            B, T, C = x.shape
            H, D = (N_HEAD, C // N_HEAD)
            qkv = x @ qkv_w + qkv_b
            q, k, v = jnp.split(qkv, 3, axis=-1)
            q = q.reshape(B, T, H, D).transpose(0, 2, 1, 3)
            k = k.reshape(B, T, H, D).transpose(0, 2, 1, 3)
            v = v.reshape(B, T, H, D).transpose(0, 2, 1, 3)
            scores = jnp.einsum('bhqd,bhkd->bhqk', q, k) / math.sqrt(D)
            causal = jnp.tril(jnp.ones((T, T), bool))
            scores = jnp.where(causal, scores, NEG_INF)
            attn = jax.nn.softmax(scores, axis=-1)
            y = jnp.einsum('bhqk,bhkd->bhqd', attn, v)
            y = y.transpose(0, 2, 1, 3).reshape(B, T, C)
            return y @ proj_w + proj_b

        def _moe(x, w_g, fc_w, fc_b, pj_w, pj_b):
            B, T, C = x.shape
            N, E, K = (B * T, N_EXP, TOP_K)
            cap = int(math.floor(K * TRAIN_CAPACITY * N / E))
            cap += cap % 2
            cap = max(cap, MIN_CAPACITY)
            logits = (x @ w_g).reshape(N, E)
            _, topk_idx = jax.lax.top_k(logits, K)
            hot = jax.nn.one_hot(topk_idx, E, dtype=jnp.int32)
            sel = hot.sum(axis=1) > 0
            router_probs = jax.nn.softmax(jnp.where(sel, logits, NEG_INF), axis=-1)
            exp_mask = hot.transpose(1, 0, 2)
            exp_rank = jnp.cumsum(exp_mask.reshape(K * N, E), axis=0) - 1
            exp_rank = exp_rank.reshape(K, N, E)
            exp_mask = exp_mask * (exp_rank < cap).astype(jnp.int32)
            exp_rank = jnp.sum(exp_mask * exp_rank, axis=-1)
            exp_weights = exp_mask.astype(x.dtype) * router_probs[None]
            rank_sc = jax.nn.one_hot(exp_rank, cap, dtype=x.dtype)
            cb_weight = jnp.einsum('kne,knc->nec', exp_weights, rank_sc)
            sec_mask = (cb_weight != 0).astype(x.dtype)
            xf = x.reshape(N, C)
            xb = jnp.einsum('nec,nd->ecd', sec_mask, xf)
            h = jax.nn.gelu(jnp.einsum('ecd,edf->ecf', xb, fc_w) + fc_b, approximate=False)
            out = jnp.einsum('ecf,efd->ecd', h, pj_w) + pj_b
            y = jnp.einsum('nec,ecd->nd', cb_weight, out)
            return y.reshape(B, T, C)
        key = jax.random.key(seed)
        ks = jax.random.split(key, 12)
        B, T, C = (4, 256, 192)
        E, F = (N_EXP, 4 * C)
        s = 0.02
        return {'x': jax.random.normal(ks[0], (B, T, C), jnp.float32), 'ln1_w': jnp.ones((C,), jnp.float32), 'ln1_b': jnp.zeros((C,), jnp.float32), 'ln2_w': jnp.ones((C,), jnp.float32), 'ln2_b': jnp.zeros((C,), jnp.float32), 'attn_qkv_w': jax.random.normal(ks[1], (C, 3 * C), jnp.float32) * s, 'attn_qkv_b': jnp.zeros((3 * C,), jnp.float32), 'attn_proj_w': jax.random.normal(ks[2], (C, C), jnp.float32) * s, 'attn_proj_b': jnp.zeros((C,), jnp.float32), 'w_g': jax.random.normal(ks[3], (C, E), jnp.float32) * s, 'exp_fc_w': jax.random.normal(ks[4], (E, C, F), jnp.float32) * s, 'exp_fc_b': jnp.zeros((E, 1, F), jnp.float32), 'exp_proj_w': jax.random.normal(ks[5], (E, F, C), jnp.float32) * s, 'exp_proj_b': jnp.zeros((E, 1, C), jnp.float32)}
    _L0_ffn_all = _L0_ffn_setup()
    _L0_ffn_in = {k: v for k, v in _L0_ffn_all.items() if k in ('ln1_w', 'ln1_b', 'ln2_w', 'ln2_b', 'attn_qkv_w', 'attn_qkv_b', 'attn_proj_w', 'attn_proj_b', 'w_g', 'exp_fc_w', 'exp_fc_b', 'exp_proj_w', 'exp_proj_b')}
    del _L0_ffn_all
    return {'x': x, 'txt': txt, 'L0_tok_W': _L0_tok_in['W'], 'L0_tok_b': _L0_tok_in['b'], 'L0_attn_ln1_g': _L0_attn_in['ln1_g'], 'L0_attn_ln1_b': _L0_attn_in['ln1_b'], 'L0_attn_attn_qkv_w': _L0_attn_in['attn_qkv_w'], 'L0_attn_attn_qkv_b': _L0_attn_in['attn_qkv_b'], 'L0_attn_attn_proj_w': _L0_attn_in['attn_proj_w'], 'L0_attn_attn_proj_b': _L0_attn_in['attn_proj_b'], 'L0_attn_ssm_qkv_w': _L0_attn_in['ssm_qkv_w'], 'L0_attn_ssm_qkv_b': _L0_attn_in['ssm_qkv_b'], 'L0_attn_ssm_out_w': _L0_attn_in['ssm_out_w'], 'L0_attn_ssm_out_b': _L0_attn_in['ssm_out_b'], 'L0_attn_ssm_ln_g': _L0_attn_in['ssm_ln_g'], 'L0_attn_ssm_ln_b': _L0_attn_in['ssm_ln_b'], 'L0_attn_out_w': _L0_attn_in['out_w'], 'L0_attn_out_b': _L0_attn_in['out_b'], 'L0_attn_mlp_w1': _L0_attn_in['mlp_w1'], 'L0_attn_mlp_b1': _L0_attn_in['mlp_b1'], 'L0_attn_mlp_w2': _L0_attn_in['mlp_w2'], 'L0_attn_mlp_b2': _L0_attn_in['mlp_b2'], 'L0_attn_lnm_g': _L0_attn_in['lnm_g'], 'L0_attn_lnm_b': _L0_attn_in['lnm_b'], 'L0_ffn_ln1_w': _L0_ffn_in['ln1_w'], 'L0_ffn_ln1_b': _L0_ffn_in['ln1_b'], 'L0_ffn_ln2_w': _L0_ffn_in['ln2_w'], 'L0_ffn_ln2_b': _L0_ffn_in['ln2_b'], 'L0_ffn_attn_qkv_w': _L0_ffn_in['attn_qkv_w'], 'L0_ffn_attn_qkv_b': _L0_ffn_in['attn_qkv_b'], 'L0_ffn_attn_proj_w': _L0_ffn_in['attn_proj_w'], 'L0_ffn_attn_proj_b': _L0_ffn_in['attn_proj_b'], 'L0_ffn_w_g': _L0_ffn_in['w_g'], 'L0_ffn_exp_fc_w': _L0_ffn_in['exp_fc_w'], 'L0_ffn_exp_fc_b': _L0_ffn_in['exp_fc_b'], 'L0_ffn_exp_proj_w': _L0_ffn_in['exp_proj_w'], 'L0_ffn_exp_proj_b': _L0_ffn_in['exp_proj_b']}

def reference(x, txt, L0_tok_W, L0_tok_b, L0_attn_ln1_g, L0_attn_ln1_b, L0_attn_attn_qkv_w, L0_attn_attn_qkv_b, L0_attn_attn_proj_w, L0_attn_attn_proj_b, L0_attn_ssm_qkv_w, L0_attn_ssm_qkv_b, L0_attn_ssm_out_w, L0_attn_ssm_out_b, L0_attn_ssm_ln_g, L0_attn_ssm_ln_b, L0_attn_out_w, L0_attn_out_b, L0_attn_mlp_w1, L0_attn_mlp_b1, L0_attn_mlp_w2, L0_attn_mlp_b2, L0_attn_lnm_g, L0_attn_lnm_b, L0_ffn_ln1_w, L0_ffn_ln1_b, L0_ffn_ln2_w, L0_ffn_ln2_b, L0_ffn_attn_qkv_w, L0_ffn_attn_qkv_b, L0_ffn_attn_proj_w, L0_ffn_attn_proj_b, L0_ffn_w_g, L0_ffn_exp_fc_w, L0_ffn_exp_fc_b, L0_ffn_exp_proj_w, L0_ffn_exp_proj_b):
    import jax
    import jax.numpy as jnp

    def _L0_tok_ref(img, W, b):
        import jax, jax.numpy as jnp
        import numpy as np
        IMAGE_SIZE = 224
        PATCH = 16
        HIDDEN = 192
        C = 3
        B, Cc, H, Wd = img.shape
        hp, wp = (H // PATCH, W // PATCH if False else Wd // PATCH)
        hp = H // PATCH
        x = img.reshape(B, Cc, hp, PATCH, wp, PATCH)
        x = x.transpose(0, 2, 4, 1, 3, 5)
        x = x.reshape(B, hp * wp, Cc * PATCH * PATCH)
        return jnp.einsum('bld,hd->blh', x, W) + b

    def _L0_attn_ref(x, ln1_g, ln1_b, attn_qkv_w, attn_qkv_b, attn_proj_w, attn_proj_b, ssm_qkv_w, ssm_qkv_b, ssm_out_w, ssm_out_b, ssm_ln_g, ssm_ln_b, out_w, out_b, mlp_w1, mlp_b1, mlp_w2, mlp_b2, lnm_g, lnm_b):
        import jax, jax.numpy as jnp
        import numpy as np
        NUM_HEADS = 12
        WINDOW = 64
        LN_EPS = 1e-05

        def _ln(x, g, b):
            m = x.mean(-1, keepdims=True)
            v = x.var(-1, keepdims=True)
            return (x - m) / jnp.sqrt(v + LN_EPS) * g + b
        B, L, D = x.shape
        H = NUM_HEADS
        E = D // H
        xn = _ln(x, ln1_g, ln1_b)
        qkv = (xn @ attn_qkv_w + attn_qkv_b).reshape(B, L, 3, H, E)
        q = jnp.transpose(qkv[:, :, 0], (0, 2, 1, 3))
        k = jnp.transpose(qkv[:, :, 1], (0, 2, 1, 3))
        v = jnp.transpose(qkv[:, :, 2], (0, 2, 1, 3))
        scale = 1.0 / jnp.sqrt(jnp.float32(E))
        scores = jnp.einsum('bhqe,bhke->bhqk', q, k) * scale
        i = jnp.arange(L)[:, None]
        j = jnp.arange(L)[None, :]
        mask = (j > i) | (j <= i - WINDOW)
        scores = jnp.where(mask, jnp.float32(-10000.0), scores)
        attn = jax.nn.softmax(scores, axis=-1)
        ao = jnp.einsum('bhqk,bhke->bhqe', attn, v)
        ao = jnp.transpose(ao, (0, 2, 1, 3)).reshape(B, L, D)
        ao = ao @ attn_proj_w + attn_proj_b
        qkv2 = xn @ ssm_qkv_w + ssm_qkv_b
        q2, k2, v2 = jnp.split(qkv2, 3, axis=-1)
        q2 = q2.reshape(B, L, H, E)
        k2 = k2.reshape(B, L, H, E)
        v2 = v2.reshape(B, L, H, E)
        q2 = jax.nn.elu(q2) + (1.0 + 0.0001)
        k2 = jax.nn.elu(k2) + (1.0 + 0.0001)
        q2 = q2 * scale
        kv = jnp.einsum('blhe,blhf->blhef', k2, v2)
        kv_cumsum = jnp.cumsum(kv, axis=1)
        k_cumsum = jnp.cumsum(k2, axis=1)
        num = jnp.einsum('blhe,blhef->blhf', q2, kv_cumsum)
        den = jnp.einsum('blhe,blhe->blh', q2, k_cumsum)[..., None] + 0.0001
        so = (num / den).reshape(B, L, D)
        so = so @ ssm_out_w + ssm_out_b
        so = _ln(so, ssm_ln_g, ssm_ln_b)
        x2 = x + (ao + so) @ out_w + out_b
        h = _ln(x2, lnm_g, lnm_b)
        h = jax.nn.gelu(h @ mlp_w1 + mlp_b1, approximate=False)
        return x2 + (h @ mlp_w2 + mlp_b2)

    def _L0_ffn_ref(x, ln1_w, ln1_b, ln2_w, ln2_b, attn_qkv_w, attn_qkv_b, attn_proj_w, attn_proj_b, w_g, exp_fc_w, exp_fc_b, exp_proj_w, exp_proj_b):
        import math
        import jax, jax.numpy as jnp
        import numpy as np
        N_HEAD = 12
        N_EXP = 8
        TOP_K = 2
        TRAIN_CAPACITY = 1.25
        MIN_CAPACITY = 4
        LN_EPS = 1e-05
        NEG_INF = -1e+30

        def _layer_norm(x, w, b):
            mu = jnp.mean(x, axis=-1, keepdims=True)
            var = jnp.var(x, axis=-1, keepdims=True)
            return (x - mu) * jax.lax.rsqrt(var + LN_EPS) * w + b

        def _attention(x, qkv_w, qkv_b, proj_w, proj_b):
            B, T, C = x.shape
            H, D = (N_HEAD, C // N_HEAD)
            qkv = x @ qkv_w + qkv_b
            q, k, v = jnp.split(qkv, 3, axis=-1)
            q = q.reshape(B, T, H, D).transpose(0, 2, 1, 3)
            k = k.reshape(B, T, H, D).transpose(0, 2, 1, 3)
            v = v.reshape(B, T, H, D).transpose(0, 2, 1, 3)
            scores = jnp.einsum('bhqd,bhkd->bhqk', q, k) / math.sqrt(D)
            causal = jnp.tril(jnp.ones((T, T), bool))
            scores = jnp.where(causal, scores, NEG_INF)
            attn = jax.nn.softmax(scores, axis=-1)
            y = jnp.einsum('bhqk,bhkd->bhqd', attn, v)
            y = y.transpose(0, 2, 1, 3).reshape(B, T, C)
            return y @ proj_w + proj_b

        def _moe(x, w_g, fc_w, fc_b, pj_w, pj_b):
            B, T, C = x.shape
            N, E, K = (B * T, N_EXP, TOP_K)
            cap = int(math.floor(K * TRAIN_CAPACITY * N / E))
            cap += cap % 2
            cap = max(cap, MIN_CAPACITY)
            logits = (x @ w_g).reshape(N, E)
            _, topk_idx = jax.lax.top_k(logits, K)
            hot = jax.nn.one_hot(topk_idx, E, dtype=jnp.int32)
            sel = hot.sum(axis=1) > 0
            router_probs = jax.nn.softmax(jnp.where(sel, logits, NEG_INF), axis=-1)
            exp_mask = hot.transpose(1, 0, 2)
            exp_rank = jnp.cumsum(exp_mask.reshape(K * N, E), axis=0) - 1
            exp_rank = exp_rank.reshape(K, N, E)
            exp_mask = exp_mask * (exp_rank < cap).astype(jnp.int32)
            exp_rank = jnp.sum(exp_mask * exp_rank, axis=-1)
            exp_weights = exp_mask.astype(x.dtype) * router_probs[None]
            rank_sc = jax.nn.one_hot(exp_rank, cap, dtype=x.dtype)
            cb_weight = jnp.einsum('kne,knc->nec', exp_weights, rank_sc)
            sec_mask = (cb_weight != 0).astype(x.dtype)
            xf = x.reshape(N, C)
            xb = jnp.einsum('nec,nd->ecd', sec_mask, xf)
            h = jax.nn.gelu(jnp.einsum('ecd,edf->ecf', xb, fc_w) + fc_b, approximate=False)
            out = jnp.einsum('ecf,efd->ecd', h, pj_w) + pj_b
            y = jnp.einsum('nec,ecd->nd', cb_weight, out)
            return y.reshape(B, T, C)
        x = x + _attention(_layer_norm(x, ln1_w, ln1_b), attn_qkv_w, attn_qkv_b, attn_proj_w, attn_proj_b)
        x = x + _moe(_layer_norm(x, ln2_w, ln2_b), w_g, exp_fc_w, exp_fc_b, exp_proj_w, exp_proj_b)
        return x
    h = _L0_tok_ref(x, L0_tok_W, L0_tok_b)
    h = jnp.concatenate([h, txt], axis=1)
    h = h + _L0_attn_ref(_layernorm(h, axis=-1), L0_attn_ln1_g, L0_attn_ln1_b, L0_attn_attn_qkv_w, L0_attn_attn_qkv_b, L0_attn_attn_proj_w, L0_attn_attn_proj_b, L0_attn_ssm_qkv_w, L0_attn_ssm_qkv_b, L0_attn_ssm_out_w, L0_attn_ssm_out_b, L0_attn_ssm_ln_g, L0_attn_ssm_ln_b, L0_attn_out_w, L0_attn_out_b, L0_attn_mlp_w1, L0_attn_mlp_b1, L0_attn_mlp_w2, L0_attn_mlp_b2, L0_attn_lnm_g, L0_attn_lnm_b)
    h = h + _L0_ffn_ref(_layernorm(h, axis=-1), L0_ffn_ln1_w, L0_ffn_ln1_b, L0_ffn_ln2_w, L0_ffn_ln2_b, L0_ffn_attn_qkv_w, L0_ffn_attn_qkv_b, L0_ffn_attn_proj_w, L0_ffn_attn_proj_b, L0_ffn_w_g, L0_ffn_exp_fc_w, L0_ffn_exp_fc_b, L0_ffn_exp_proj_w, L0_ffn_exp_proj_b)
    return h

_drawn_inputs = setup_inputs


def setup_inputs(seed=0):
    import zlib

    import numpy as np

    out = dict(_drawn_inputs(seed))
    spreads = {'L0_attn_ln1_g': (1.0, 0.6),
     'L0_attn_ln1_b': (0.0, 0.569),
     'L0_attn_attn_qkv_b': (0.0, 0.8),
     'L0_attn_attn_proj_b': (0.0, 0.403),
     'L0_attn_ssm_qkv_b': (0.0, 0.1),
     'L0_attn_ssm_out_b': (0.0, 0.1),
     'L0_attn_ssm_ln_g': (1.0, 0.2),
     'L0_attn_ssm_ln_b': (0.0, 0.437),
     'L0_attn_out_b': (0.0, 0.1),
     'L0_attn_mlp_b1': (0.0, 0.436),
     'L0_attn_mlp_b2': (0.0, 0.1),
     'L0_attn_lnm_g': (1.0, 0.6),
     'L0_attn_lnm_b': (0.0, 0.8),
     'L0_ffn_ln1_w': (1.0, 0.6),
     'L0_ffn_ln1_b': (0.0, 0.8),
     'L0_ffn_ln2_w': (1.0, 0.6),
     'L0_ffn_ln2_b': (0.0, 0.726),
     'L0_ffn_attn_qkv_b': (0.0, 0.633),
     'L0_ffn_attn_proj_b': (0.0, 0.303),
     'L0_ffn_exp_fc_b': (0.0, 0.8),
     'L0_ffn_exp_proj_b': (0.0, 0.301)}
    factors = {'L0_tok_b': 2.685,
     'L0_attn_attn_qkv_w': 8.0,
     'L0_attn_attn_proj_w': 8.0,
     'L0_ffn_attn_qkv_w': 5.829,
     'L0_ffn_attn_proj_w': 3.46}
    for name, (base, spread) in spreads.items():
        noise = np.random.default_rng([zlib.crc32(name.encode()), seed]).standard_normal(out[name].shape)
        drawn = base * np.exp(spread * noise) if base else spread * noise
        out[name] = jnp.asarray(drawn.astype(out[name].dtype))
    for name, factor in factors.items():
        out[name] = (out[name] * factor).astype(out[name].dtype)
    return out
```

```python
from contextlib import ExitStack

import concourse.bass as bass
from concourse import mybir

ALU = mybir.AluOpType
ACT = mybir.ActivationFunctionType
F32 = mybir.dt.float32
BF16 = mybir.dt.bfloat16
I32 = mybir.dt.int32
AX = mybir.AxisListType.X

P = 128
D = 192
HALF = 96
HEADS, HD = 12, 16
GROUPS, GH = 3, 4
BATCH, IMG, TXT = 8, 64, 128
SEQ = IMG + TXT
PAIRS, TILES = BATCH // 2, 3
COLS = 2 * SEQ
TOKENS = BATCH * SEQ
KT = 768 // P
HID = 4 * D
MT = HID // P
WINDOW = 64
EXPERTS = 8
CAP = 2 * 5 * TOKENS // (4 * EXPERTS)
CAP += CAP % 2
SLOT_TILES = 4
SLOTS = CAP // SLOT_TILES
EPS = 1e-5
SCALE = HD ** -0.5
ELU_EPS = 1e-4
DUMP = EXPERTS * CAP
ROWS = DUMP + 2 * TOKENS
W_FULL = SEQ + TXT + TXT
W_WIN = 2 * IMG + TXT + TXT
assert SLOTS <= P and CAP <= 512


class Named(dict):

    def __getattr__(self, name):
        return self[name]


TILE_AT = (P, 0, 2 * P)
IMG_COLS = (slice(TXT, SEQ), slice(SEQ, SEQ + IMG))
TXT_COLS = (slice(0, TXT), slice(SEQ + IMG, COLS))


def tile_cols(ap, t):
    return ap[:, TILE_AT[t]:TILE_AT[t] + P]


def seen_by_image(ap, s, kind, at=0):
    if kind == "full":
        return ap[:, s * SEQ - at:(s + 1) * SEQ - at]
    if s == 1:
        return ap[:, SEQ - at:SEQ + 2 * IMG - at]
    return ap[:, 0:2 * TXT].rearrange("p (a b) -> p a b", a=2)[:, :, 0:IMG]


def build(nc, d, out):
    ctx = ExitStack()
    with ctx:
        def sb(name, shape, dt=F32):
            return ctx.enter_context(nc.sbuf_tensor(name, shape, dt))

        SEM, PER = {}, {}

        def sem(name, per=1):
            SEM[name] = ctx.enter_context(nc.semaphore(name))
            PER[name] = per
            return SEM[name]

        def need(eng, name, i, k=None):
            eng.wait_ge(SEM[name], i * PER[name] + (PER[name] if k is None else k))

        def need_last(eng, name, i):
            if isinstance(i, int) and i == 0:
                return
            eng.wait_ge(SEM[name], i * PER[name])

        def apart(eng):
            eng.wait_ge(SEM["setup_pool"], FILLS)

        identf = sb("identf", [P, P])
        identb = sb("identb", [P, P], BF16)
        mask = {"win": sb("mask_win", [P, 448], BF16), "full": sb("mask_full", [P, 448], BF16)}
        maskT = {"win": sb("maskT_win", [P, W_WIN], BF16), "full": sb("maskT_full", [P, W_FULL], BF16)}
        keep01 = sb("keep01", [P, W_FULL])
        order = sb("order", [P, 9, P], BF16)
        onesb = sb("onesb", [P, P], BF16)
        ones_row = sb("ones_row", [1, P])
        neghalf = sb("neghalf", [P, TILES])
        carrier = sb("carrier", [P, 1])
        eps = sb("eps", [P, TILES])
        w_tok = sb("w_tok", [P, KT, D])
        b_tok = sb("b_tok", [1, D])
        w_qk = {n: sb(f"w_qk_{n}", [HALF + 1, 2, 6, P]) for n in ("attn", "ssm", "ffn")}
        w_v = {n: sb(f"w_v_{n}", [HALF + 1, 2, D]) for n in ("attn", "ssm", "ffn")}
        w_proj = {n: sb(f"w_proj_{n}", [P, GROUPS, D]) for n in ("attn", "ssm", "ffn")}
        b_so = sb("b_so", [1, D])
        w_out = sb("w_out", [HALF + 1, 2, D])
        w_m1 = sb("w_m1", [HALF + 1, 2, HID])
        w_m2 = sb("w_m2", [P, MT, D])
        b_m2 = sb("b_m2", [P, D])
        w_g = sb("w_g", [HALF, 2, EXPERTS])
        affine = sb("affine", [HALF, 5, 2, 2])
        LN1, LNS, LNM, LNF1, LNF2 = range(5)

        def cut(buf, at, a, b):
            return buf[:, at:at + a * b].rearrange("p (a b) -> p a b", a=a)

        def stream(n):
            c = Named(n=n)
            c.ps = ctx.enter_context(nc.psum_tensor(f"ps_{n}", [P, 4, 512], F32))
            c.work = sb(f"work_{n}", [P, 2 * GROUPS * COLS + GH * W_FULL])
            c.qT = cut(c.work, 0, GROUPS, COLS)
            c.kT = cut(c.work, GROUPS * COLS, GROUPS, COLS)
            c.PT = cut(c.work, 2 * GROUPS * COLS, GH, W_FULL)
            for name, shape in (("V", [P, TILES, HEADS, 32]),
                                ("negm", [P, TILES, P]), ("rec", [P, COLS]), ("OT", [P, GROUPS, COLS]),
                                ("xln", [P, TILES, D]), ("xhat", [P, TILES, D]),
                                ("xnT", [HALF + 1, 2, COLS])):
                c[name] = sb(f"{name}_{n}", shape)
            return c

        A, F = stream("a"), stream("f")
        A.kind, F.kind = "win", "full"
        A.w, F.w = "attn", "ffn"
        hA = sb("hA", [P, TILES, D])
        hF = sb("hF", [P, TILES, D])
        xT_in = sb("xT_in", [P, KT, P])
        e_ssm = sb("e_ssm", [P, 2, COLS])
        r_ssm = sb("r_ssm", [P, COLS])
        aoT = sb("aoT", [HALF, 2, COLS])
        uT = sb("uT", [HALF + 1, 2, COLS])
        sohat = sb("sohat", [P, TILES, D])
        x2 = sb("x2", [P, TILES, D])
        hs = sb("hs", [P, TILES, D])
        g_work = sb("g_work", [P, MT * COLS])
        gT = cut(g_work, 0, MT, COLS)
        x1 = sb("x1", [P, TILES, D])
        hx_all = sb("hx_all", [P, PAIRS, TILES, D])
        xh_all = sb("xh_all", [P, PAIRS, TILES, D])
        logits = sb("logits", [P, PAIRS, TILES, EXPERTS])

        def ln(name, src, dst):
            L = Named(name=name, src=src, dst=dst)
            L.st = sb(f"{name}_st", [P, TILES, 6])
            L.mv = sb(f"{name}_mv", [P, TILES, 2])
            L.ve = sb(f"{name}_ve", [P, TILES])
            L.rs = sb(f"{name}_rs", [P, TILES])
            for s, per in (("stats", TILES), ("aggr", TILES), ("var", 1), ("rstd", 1), ("out", TILES)):
                sem(f"{name}_{s}", per)
            return L

        a0 = ln("a0", lambda t: hA[:, t, :], lambda t: A.xln[:, t, :])
        a1 = ln("a1", lambda t: A.xln[:, t, :], lambda t: A.xhat[:, t, :])
        so = ln("so", lambda t: A.ps[:, 1 + t, 0:D], lambda t: sohat[:, t, :])
        am = ln("am", lambda t: x2[:, t, :], lambda t: A.xhat[:, t, :])
        f0 = ln("f0", lambda t: hF[:, t, :], lambda t: F.xln[:, t, :])
        f1 = ln("f1", lambda t: F.xln[:, t, :], lambda t: F.xhat[:, t, :])
        f2 = ln("f2", lambda t: x1[:, t, :], lambda t: F.xhat[:, t, :])

        for n in ("a", "f"):
            for s, per in (("xT_ps", 2), ("xT", 2), ("S_ps", GROUPS), ("negm", 2 * GROUPS),
                           ("M_ps", GROUPS), ("qa", GROUPS), ("ST_ps", GROUPS), ("PT", GROUPS),
                           ("PV_ps", GROUPS), ("shuf", GROUPS), ("rec", GROUPS), ("OT", GROUPS),
                           ("qkv_ps", 9), ("q", 3), ("k", 3), ("v", 3)):
                sem(f"{n}_{s}", per)
        for s, per in (("x_in", 16), ("txt_in", 16), ("h0_ps", 1), ("h0", 1), ("ao_ps", 2), ("ao", 2),
                       ("s_qkv_ps", 9), ("s_exp", 6), ("s_relu", 6), ("s_phi", 6), ("s_v", 3),
                       ("s_ST_ps", 3), ("s_PT", 3), ("s_PV_ps", 3), ("s_shuf", 3), ("s_eps", 3),
                       ("s_rec", 3), ("s_OT", 3),
                       ("so_ps", 3), ("soT_ps", 2), ("u", 2), ("out_ps", 3), ("x2", 3),
                       ("hx2", 1), ("hs", 1), ("mT_ps", 2), ("mT", 2), ("m1_ps", 6), ("gelu", 6),
                       ("m2_ps", 3), ("hF", 3),
                       ("fp_ps", 3), ("x1", 3), ("hx", 1), ("xh", 1), ("x2T_ps", 2), ("x2T", 2),
                       ("lg_ps", 1), ("lg", 1)):
            sem(s, per)
        FILLS = 15
        ready = sem("setup_pool")
        loads = ["const", "tok", "attn", "ssm", "mlp", "ffn"]
        LOADED = {n: 0 for n in loads}
        for n in loads:
            sem("ld_" + n)

        xb_dram = nc.dram_tensor("xb_rows", [ROWS, D], F32, kind="Internal").ap()
        ob_dram = nc.dram_tensor("ob_rows", [EXPERTS * CAP, D], F32, kind="Internal").ap()
        zrow = g_work[:, 0:EXPERTS * CAP // P * D // 10]
        R = Named()
        NT = PAIRS * TILES
        for name, shape, dt in (("m", [P, 2, NT], F32), ("eq", [P, NT, EXPERTS], F32),
                                ("cand", [P, NT, EXPERTS], F32), ("mc", [P, NT], F32),
                                ("first", [P, 2, NT, EXPERTS], F32), ("l2", [P, NT, EXPERTS], F32),
                                ("fb", [P, PAIRS, TILES, 2, EXPERTS], BF16), ("dm", [P, NT], F32), ("ex", [P, NT], F32),
                                ("den", [P, NT], F32), ("p", [P, 2, NT], F32),
                                ("base", [P, PAIRS + 1, 2, EXPERTS], F32),
                                ("tot", [P, PAIRS, 2, EXPERTS], F32),
                                ("rank", [P, PAIRS, TILES, 2, EXPERTS], F32),
                                ("kept", [P, PAIRS, TILES, 2, EXPERTS], F32),
                                ("slotv", [P, PAIRS, TILES, 2, EXPERTS], F32),
                                ("ks", [P, PAIRS, TILES, 2], F32), ("slot", [P, PAIRS, TILES, 2], F32),
                                ("dumpv", [P, PAIRS, TILES, 2], F32),
                                ("wgt", [P, PAIRS, TILES, 2], F32),
                                ("gidx", [P, PAIRS, TILES, 2], I32), ("sidx", [P, PAIRS, TILES, 2], I32)):
            R[name] = sb("r_" + name, shape, dt)
        desc = sb("desc", [P, EXPERTS])
        ebase = sb("ebase", [P, EXPERTS])
        dump_id = sb("dump_id", [P, PAIRS, TILES, 2])
        w_fc = [sb("w_fc0", [HALF + 1, 2, HID]), w_m1]
        w_pj = [w_m2, w_tok]
        b_pj = [sb(f"b_pj{j}", [P, D]) for j in range(2)]
        xbT = [sb(f"xbT{j}", [HALF + 1, 2, CAP]) for j in range(2)]
        heT = cut(A.work, 0, MT, CAP)
        xb = [cut(F.work[0:SLOTS, :], j * SLOT_TILES * D, SLOT_TILES, D) for j in range(2)]
        ob = [cut(F.work[0:SLOTS, :], (2 + j) * SLOT_TILES * D, SLOT_TILES, D) for j in range(2)]
        g_rows = g_work[:, 0:8 * D].rearrange("p (a b n) -> p a b n", a=4, b=2)
        y_mid = cut(g_work, 8 * D, 2, D)
        y_out = cut(g_work, 10 * D, 2, D)
        for s in ("route", "dm", "exp_d", "rank_ps", "slots", "zero", "zfill", "fbcast"):
            sem(s)
        for j in range(2):
            for s, per in (("fc_in", 16), ("pj_in", 16), ("xb_in", 16), ("xbT_ps", 2), ("xbT", 2),
                           ("bp_in", 16), ("fc_ps", 6), ("he", 6), ("pj_ps", 4), ("ob", 4), ("st", 16)):
                sem(f"e{j}_{s}", per)
        scat = sem("scattered", 16)
        gat = [sem(f"gathered{j}") for j in range(4)]
        sem("ymid")
        sem("yout")
        ysto = [sem(f"ystored{j}") for j in range(2)]

        a_steps = ([("h0", 0), ("ln0", 0), ("ln1", 0), ("xT", 0), ("qkv", 0)]
                   + [(s, g) for g in range(GROUPS) for s in ("S", "M", "ST", "PV")]
                   + [("aproj", 0), ("sqkv", 0)] + [(s, g) for g in range(GROUPS) for s in ("sST", "sPV")]
                   + [("so", 0), ("soT", 0), ("out", 0), ("lnm", 0), ("mT", 0), ("m1", 0), ("m2", 0)])
        f_steps = ([("ln0", 0), ("ln1", 0), ("xT", 0), ("qkv", 0)]
                   + [(s, g) for g in range(GROUPS) for s in ("S", "M", "ST", "PV")]
                   + [("fproj", 0), ("ln2", 0), ("x2T", 0), ("logit", 0)])

        def steps(parts, ia, jf):
            na = len(a_steps) if ia is not None else 0
            nf = len(f_steps) if jf is not None else 0
            turns = sorted([((k + 0.5) / na, 0, k) for k in range(na)] + [((k + 0.5) / nf, 1, k) for k in range(nf)])
            for _, which, k in turns:
                name, g = (a_steps, f_steps)[which][k]
                part = parts.get(("af"[which], name))
                if part:
                    part((ia, jf)[which], g)

        def all_pairs(eng, parts):
            steps(parts, 0, None)
            steps(parts, 1, 0)
            with eng.Fori(1, PAIRS - 1) as j:
                steps(parts, j + 1, j)
            steps(parts, None, PAIRS - 1)

        block = ctx.enter_context(nc.Block())

        def stored(n, j):
            return sum(16 * (2 if m % TILES == 0 else 1) for m in range(n) if m % 2 == j)

        @block.sync
        def _(sp):
            def load(n, dst, src):
                LOADED[n] += 16
                sp.dma_start(dst, src).then_inc(SEM["ld_" + n], 16)

            def a_in(i):
                need_last(sp, "h0_ps", i)
                sp.dma_start(xT_in[:], d.xT[i]).then_inc(SEM["x_in"], 16)
                need_last(sp, "hs", i)
                need_last(sp, "a0_out", i)
                sp.dma_start(hA[:, 1:3, :], d.txt[i]).then_inc(SEM["txt_in"], 16)

            load("tok", w_tok[:], d.w_tok)
            load("tok", b_tok[:], d.b_tok)
            a_in(0)
            load("const", identf[:], d.identf)
            load("const", identb[:], d.identb)
            load("const", affine[:], d.affine)
            for n in ("win", "full"):
                load("const", mask[n][:], d["mask_" + n])
                load("const", maskT[n][:], d["maskT_" + n])
            load("const", keep01[:], d.keep01)
            load("const", order[:], d.order)
            load("const", desc[:], d.desc)
            load("const", ebase[:], d.ebase)
            load("const", dump_id[:], d.dump_id)
            load("attn", w_qk["attn"][:], d.wqk_attn)
            load("attn", w_v["attn"][:], d.wv_attn)
            load("attn", w_proj["attn"][:], d.wp_attn)
            load("ssm", w_qk["ssm"][:], d.wqk_ssm)
            load("ssm", w_v["ssm"][:], d.wv_ssm)
            load("ssm", w_proj["ssm"][:], d.wp_ssm)
            load("ssm", b_so[:], d.b_so)
            load("ssm", w_out[:], d.w_out)
            load("mlp", w_m1[:], d.w_m1)
            load("mlp", w_m2[:], d.w_m2)
            load("mlp", b_m2[:], d.b_m2.to_broadcast([P, D]))
            load("ffn", w_qk["ffn"][:], d.wqk_ffn)
            load("ffn", w_v["ffn"][:], d.wv_ffn)
            load("ffn", w_proj["ffn"][:], d.wp_ffn)
            load("ffn", w_g[:], d.w_g)
            sp.wait_ge(SEM["zero"], 1)
            zr = xb_dram[0:EXPERTS * CAP, :].rearrange("(k p r) n -> k p (r n)", p=P, k=10)
            for k in range(10):
                sp.dma_start(zr[k], zrow).then_inc(SEM["zfill"], 16)

            for i in range(1, PAIRS):
                a_in(i)

            def expert_in(u, j):
                need_last(sp, f"e{j}_fc_ps", u)
                sp.dma_start(w_fc[j][:], d.e_fc[2 * u + j]).then_inc(SEM[f"e{j}_fc_in"], 16)
                need_last(sp, f"e{j}_pj_ps", u)
                sp.dma_start(w_pj[j][:], d.e_pj[2 * u + j]).then_inc(SEM[f"e{j}_pj_in"], 16)
                need_last(sp, f"e{j}_ob", u)
                sp.dma_start(b_pj[j][:], d.e_bpj[2 * u + j].to_broadcast([P, D])).then_inc(SEM[f"e{j}_bp_in"], 16)

            def rows_in(u, j):
                need_last(sp, f"e{j}_xbT_ps", u)
                rows = xb_dram[0:EXPERTS * CAP, :].rearrange("(e t s) n -> e s t n", e=EXPERTS, s=SLOTS)
                sp.dma_start(xb[j], rows[2 * u + j]).then_inc(SEM[f"e{j}_xb_in"], 16)

            def rows_out(u, j):
                need(sp, f"e{j}_ob", u)
                rows = ob_dram.rearrange("(e t s) n -> e s t n", e=EXPERTS, s=SLOTS)
                sp.dma_start(rows[2 * u + j], ob[j]).then_inc(SEM[f"e{j}_st"], 16)

            sp.wait_ge(SEM["m1_ps"], PAIRS * PER["m1_ps"])
            sp.wait_ge(SEM["m2_ps"], PAIRS * PER["m2_ps"])
            expert_in(0, 0)
            expert_in(0, 1)
            sp.wait_ge(scat, 16 * 2 * NT)
            rows_in(0, 0)
            rows_in(0, 1)
            with sp.Fori(0, EXPERTS // 2 - 1) as u:
                for j in range(2):
                    rows_out(u, j)
                    expert_in(u + 1, j)
                    rows_in(u + 1, j)
            for j in range(2):
                rows_out(EXPERTS // 2 - 1, j)
            for n in range(NT):
                p, t = n // TILES, n % TILES
                sp.wait_ge(SEM["yout"], n + 1)
                if t == 0:
                    for b in range(2):
                        sp.dma_start(out[2 * p + b, 0:IMG, :], y_out[b * IMG:(b + 1) * IMG, n % 2, :]).then_inc(ysto[n % 2], 16)
                else:
                    sp.dma_start(out[2 * p + t - 1, IMG:SEQ, :], y_out[:, n % 2, :]).then_inc(ysto[n % 2], 16)
            for j in range(2):
                sp.wait_ge(ysto[j], stored(NT, j))

        @block.tensor
        def _(pe):
            def mm(out_, lhsT, rhs, start=True, stop=True, skip=False):
                return pe.matmul(out_, lhsT, rhs, start=start, stop=stop, skip_group_check=skip)

            def wait_loads(*names):
                for n in names:
                    pe.wait_ge(SEM["ld_" + n], LOADED[n])

            def turn(c, src, sem_in, done, i):
                for s in range(2):
                    for t in range(TILES):
                        need(pe, sem_in, i, t + 1)
                        last = pe.transpose(tile_cols(c.ps[0:HALF, s, 0:COLS], t), src[:, t, s * HALF:(s + 1) * HALF],
                                            identf[:])
                    last.then_inc(SEM[done], 1)

            def halves(out_, w, xT, stop=True):
                mm(out_, w(0, HALF), xT(0, HALF), True, False)
                return mm(out_, w(1, HALF + 1), xT(1, HALF + 1), False, stop)

            def a_h0(i, g):
                if isinstance(i, int):
                    wait_loads("tok")
                    pe.wait_ge(ready, FILLS)
                need(pe, "x_in", i)
                need_last(pe, "hF", i)
                for k in range(KT):
                    mm(A.ps[:, 0, 0:D], xT_in[:, k, :], w_tok[:, k, :], k == 0, False)
                mm(A.ps[:, 0, 0:D], ones_row[:], b_tok[:], False, True).then_inc(SEM["h0_ps"], 1)

            def xT(c):
                n = c.n
                def part(i, g):
                    if c is A:
                        if isinstance(i, int):
                            wait_loads("const")
                        need(pe, "h0", i)
                    else:
                        need_last(pe, "lg", i)
                    turn(c, c.xhat, f"{n}1_out", f"{n}_xT_ps", i)
                return part

            def qkv(c, w, done, free):
                def part(i, g):
                    if isinstance(i, int):
                        wait_loads(w)
                    if w != "ssm":
                        need(pe, f"{c.n}_xT", i)
                    for m in range(6):
                        free(i, m)
                        j = (m % 2) * GROUPS + m // 2
                        halves(c.ps[:, m % 4, 0:COLS], lambda s, k: w_qk[w][0:k, s, j, :],
                               lambda s, k: c.xnT[0:k, s, :]).then_inc(SEM[done], 1)
                    for t in range(TILES):
                        free(i, 6 + t)
                        halves(c.ps[:, (6 + t) % 4, 0:D], lambda s, k: tile_cols(c.xnT[0:k, s, :], t),
                               lambda s, k: w_v[w][0:k, s, :]).then_inc(SEM[done], 1)
                return part

            def free_soft(c):
                def free(i, m):
                    if m >= 4:
                        need(pe, f"{c.n}_{'qk'[m % 2]}", i, (m - 4) // 2 + 1)
                return free

            def free_ssm(i, m):
                if m == 1 or m == 2:
                    need(pe, "ao", i)
                if m >= 4:
                    need(pe, "s_exp", i, m - 3)
                    need(pe, "s_relu", i, m - 3)

            def S(c):
                n = c.n
                def part(i, g):
                    if g == 0:
                        need(pe, f"{n}_q", i)
                        need(pe, f"{n}_k", i)
                        need(pe, f"{n}_v", i)
                    else:
                        need(pe, f"{n}_OT", i, g)
                    for b in range(GH):
                        mm(c.ps[:, b, 0:448], identb[:], mask[c.kind][:], True, True)
                    for b in range(GH):
                        r = slice(32 * b, 32 * b + HD)
                        q, k = c.qT[r, g, :], c.kT[r, g, :]
                        for s in range(2):
                            mm(c.ps[IMG * s:IMG * (s + 1), b, 0:IMG], q[:, IMG_COLS[s]], k[:, IMG_COLS[s]],
                               False, True, True)
                        for s in range(2):
                            last = mm(c.ps[:, b, IMG + s * SEQ:IMG + (s + 1) * SEQ], q[:, TXT_COLS[s]],
                                      k[:, s * SEQ:(s + 1) * SEQ], False, True, True)
                    last.then_inc(SEM[f"{n}_S_ps"], 1)
                return part

            def M(c):
                n = c.n
                def part(i, g):
                    need(pe, f"{n}_negm", i, 2 * g + 2)
                    for t in range(TILES):
                        last = pe.transpose(tile_cols(c.ps[:, 0, 0:COLS], t), c.negm[:, t, :], identf[:])
                    last.then_inc(SEM[f"{n}_M_ps"], 1)
                return part

            def scoresT(c, rows, kind, i, g, masked):
                w0 = 2 * IMG if kind == "win" else SEQ
                if masked:
                    for b in range(GH):
                        mm(c.ps[:, b, 0:w0 + 2 * TXT], identb[:], maskT[kind][:], True, True)
                for b in range(GH):
                    r = slice(32 * b, 32 * b + rows)
                    q, k = c.qT[r, g, :], c.kT[r, g, :]
                    st = not masked
                    for s in range(2):
                        mm(c.ps[IMG * s:IMG * (s + 1), b, 0:w0], k[:, IMG_COLS[s]], seen_by_image(q, s, kind),
                           st, True, True)
                    for s in range(2):
                        last = mm(c.ps[:, b, w0 + s * TXT:w0 + (s + 1) * TXT], k[:, TXT_COLS[s]], q[:, TXT_COLS[s]],
                                  st, True, True)
                return last

            def ST(c):
                n = c.n
                def part(i, g):
                    need(pe, f"{n}_qa", i, g + 1)
                    scoresT(c, HD + 1, c.kind, i, g, True).then_inc(SEM[f"{n}_ST_ps"], 1)
                return part

            def values(c, kind, g):
                w0 = 2 * IMG if kind == "win" else SEQ
                for b in range(GH):
                    h = GH * g + b
                    for s in range(2):
                        o = c.ps[32 * b:32 * b + 32, s, :]
                        r = slice(IMG * s, IMG * s + IMG)
                        mm(o[:, TXT_COLS[s].start - s * SEQ:TXT_COLS[s].stop - s * SEQ], c.V[:, 1 + s, h, :],
                           c.PT[:, b, w0 + s * TXT:w0 + (s + 1) * TXT], True, False, True)
                        last = mm(seen_by_image(o, s, kind, s * SEQ), c.V[r, 0, h, :], c.PT[r, b, 0:w0], False, True, True)
                return last

            def PV(c):
                n = c.n
                def part(i, g):
                    need(pe, f"{n}_PT", i, g + 1)
                    values(c, c.kind, g).then_inc(SEM[f"{n}_PV_ps"], 1)
                return part

            def a_proj(i, g):
                need(pe, "a_OT", i)
                for s in range(2):
                    for k in range(GROUPS):
                        last = mm(A.ps[0:HALF, 1 + s, 0:COLS], w_proj["attn"][:, k, s * HALF:(s + 1) * HALF],
                                  A.OT[:, k, :], k == 0, k == GROUPS - 1)
                    last.then_inc(SEM["ao_ps"], 1)

            def a_sST(i, g):
                if g == 0:
                    need(pe, "s_phi", i)
                    need(pe, "s_v", i)
                else:
                    need(pe, "s_OT", i, g)
                scoresT(A, HD, "full", i, g, False).then_inc(SEM["s_ST_ps"], 1)

            def a_sPV(i, g):
                need(pe, "s_PT", i, g + 1)
                values(A, "full", g).then_inc(SEM["s_PV_ps"], 1)

            def a_so(i, g):
                need(pe, "s_OT", i)
                for t in range(TILES):
                    for k in range(GROUPS):
                        mm(A.ps[:, 1 + t, 0:D], tile_cols(A.OT[:, k, :], t), w_proj["ssm"][:, k, :], k == 0, False)
                    mm(A.ps[:, 1 + t, 0:D], ones_row[:], b_so[:], False, True).then_inc(SEM["so_ps"], 1)

            def a_soT(i, g):
                need(pe, "so_out", i)
                turn(A, sohat, "so_out", "soT_ps", i)

            def a_out(i, g):
                need(pe, "u", i)
                for t in range(TILES):
                    halves(A.ps[:, 1 + t, 0:D], lambda s, k: tile_cols(uT[0:k, s, :], t),
                           lambda s, k: w_out[0:k, s, :]).then_inc(SEM["out_ps"], 1)

            def a_mT(i, g):
                if isinstance(i, int):
                    wait_loads("mlp")
                turn(A, A.xhat, "am_out", "mT_ps", i)

            def a_m1(i, g):
                need(pe, "mT", i)
                for m in range(MT):
                    if m >= 4:
                        need(pe, "gelu", i, m - 3)
                    halves(A.ps[:, (m + 2) % 4, 0:COLS], lambda s, k: w_m1[0:k, s, m * P:(m + 1) * P],
                           lambda s, k: A.xnT[0:k, s, :]).then_inc(SEM["m1_ps"], 1)

            def a_m2(i, g):
                need(pe, "gelu", i)
                for t in range(TILES):
                    for m in range(MT):
                        last = mm(A.ps[:, t, 0:D], tile_cols(gT[:, m, :], t), w_m2[:, m, :], m == 0, m == MT - 1)
                    last.then_inc(SEM["m2_ps"], 1)

            def f_proj(i, g):
                need(pe, "f_OT", i)
                for t in range(TILES):
                    for k in range(GROUPS):
                        last = mm(F.ps[:, 1 + t, 0:D], tile_cols(F.OT[:, k, :], t), w_proj["ffn"][:, k, :],
                                  k == 0, k == GROUPS - 1)
                    last.then_inc(SEM["fp_ps"], 1)

            def f_x2T(i, g):
                turn(F, F.xhat, "f2_out", "x2T_ps", i)

            def f_logit(i, g):
                need(pe, "x2T", i)
                for t in range(TILES):
                    o = F.ps[:, 2, t * EXPERTS:(t + 1) * EXPERTS]
                    for s in range(2):
                        last = mm(o, tile_cols(F.xnT[0:HALF, s, :], t), w_g[:, s, :], s == 0, s == 1)
                last.then_inc(SEM["lg_ps"], 1)

            all_pairs(pe, {
                ("a", "h0"): a_h0, ("a", "xT"): xT(A), ("a", "qkv"): qkv(A, "attn", "a_qkv_ps", free_soft(A)),
                ("a", "S"): S(A), ("a", "M"): M(A), ("a", "ST"): ST(A), ("a", "PV"): PV(A),
                ("a", "aproj"): a_proj, ("a", "sqkv"): qkv(A, "ssm", "s_qkv_ps", free_ssm),
                ("a", "sST"): a_sST, ("a", "sPV"): a_sPV, ("a", "so"): a_so, ("a", "soT"): a_soT,
                ("a", "out"): a_out, ("a", "mT"): a_mT, ("a", "m1"): a_m1, ("a", "m2"): a_m2,
                ("f", "xT"): xT(F), ("f", "qkv"): qkv(F, "ffn", "f_qkv_ps", free_soft(F)),
                ("f", "S"): S(F), ("f", "M"): M(F), ("f", "ST"): ST(F), ("f", "PV"): PV(F),
                ("f", "fproj"): f_proj, ("f", "x2T"): f_x2T, ("f", "logit"): f_logit,
            })

            pe.wait_ge(SEM["fbcast"], 1)
            for t in range(TILES):
                for s in range(TILES):
                    mm(A.ps[:, t, 0:64], order[:, 3 * s + t, :], R.fb[:, :, s, :, :], s == 0, s == TILES - 1)
            for s in range(TILES):
                last = mm(A.ps[:, 3, 0:64], onesb[:], R.fb[:, :, s, :, :], s == 0, s == TILES - 1)
            last.then_inc(SEM["rank_ps"], 1)

            def expert(u, j):
                n = f"e{j}_"
                need(pe, n + "xb_in", u)
                if j == 0:
                    need_last(pe, "e1_xbT", u)
                else:
                    need(pe, "e0_xbT", u)
                for s in range(2):
                    for t in range(SLOT_TILES):
                        last = pe.transpose(A.ps[0:HALF, s, t * SLOTS:(t + 1) * SLOTS],
                                            xb[j][:, t, s * HALF:(s + 1) * HALF], identf[0:SLOTS, 0:SLOTS])
                    last.then_inc(SEM[n + "xbT_ps"], 1)
                need(pe, n + "xbT", u)
                need(pe, n + "fc_in", u)
                for m in range(MT):
                    if m >= 4:
                        need(pe, n + "he", u, m - 3)
                    ps = (A.ps[:, 2 + m % 4, :] if m % 4 < 2 else F.ps[:, m % 4 - 2, :])
                    halves(ps[:, 0:CAP], lambda s, k: w_fc[j][0:k, s, m * P:(m + 1) * P],
                           lambda s, k: xbT[j][0:k, s, :]).then_inc(SEM[n + "fc_ps"], 1)
                need(pe, n + "he", u)
                need(pe, n + "pj_in", u)
                if j == 1:
                    need(pe, "e0_ob", u)
                else:
                    need_last(pe, "e1_ob", u)
                for t in range(SLOT_TILES):
                    if t >= 2:
                        need(pe, n + "ob", u, t - 1)
                    for m in range(MT):
                        last = mm(F.ps[0:SLOTS, 2 + t % 2, 0:D], heT[:, m, t * SLOTS:(t + 1) * SLOTS],
                                  w_pj[j][:, m, :], m == 0, m == MT - 1)
                    last.then_inc(SEM[n + "pj_ps"], 1)

            pe.wait_ge(SEM["slots"], 1)
            for j in range(2):
                expert(0, j)
            with pe.Fori(1, EXPERTS // 2) as u:
                for j in range(2):
                    expert(u, j)

        @block.scalar
        def _(act):
            def copy(dst, src):
                return act.activation(dst, src, ACT.Copy)

            def scaled(c, which, ps_name, done, i, dst):
                if isinstance(i, int):
                    act.wait_ge(SEM["ld_const"], LOADED["const"])
                for s in range(2):
                    need(act, ps_name, i, s + 1)
                    act.activation(dst[0:HALF, s, :], c.ps[0:HALF, s, 0:COLS], ACT.Identity,
                                   bias=affine[:, which, 1, s:s + 1], scale=affine[:, which, 0, s:s + 1])\
                       .then_inc(SEM[done], 1)

            def a_h0(i, g):
                need(act, "h0_ps", i)
                need_last(act, "hs", i)
                need_last(act, "a0_out", i)
                copy(hA[:, 0, :], A.ps[:, 0, 0:D]).then_inc(SEM["h0"], 1)

            def xT(c, which):
                def part(i, g):
                    if c is A:
                        need_last(act, "m1_ps", i)
                    else:
                        need_last(act, "lg_ps", i)
                    scaled(c, which, f"{c.n}_xT_ps", f"{c.n}_xT", i, c.xnT)
                return part

            def qkv(c):
                n = c.n
                def part(i, g):
                    for m in range(3):
                        need(act, f"{n}_qkv_ps", i, 2 * m + 1)
                        copy(c.qT[:, m, :], c.ps[:, (2 * m) % 4, 0:COLS]).then_inc(SEM[f"{n}_q"], 1)
                    for t in range(TILES):
                        need(act, f"{n}_qkv_ps", i, 7 + t)
                        copy(c.V[:, t, :, 0:HD], c.ps[:, (6 + t) % 4, 0:D].rearrange("p (h e) -> p h e", e=HD))\
                            .then_inc(SEM[f"{n}_v"], 1)
                return part

            def ST(c):
                n = c.n
                w = W_WIN if c.kind == "win" else W_FULL
                def part(i, g):
                    need(act, f"{n}_ST_ps", i, g + 1)
                    if g:
                        need(act, f"{n}_PV_ps", i, g)
                    act.activation(c.PT[:, :, 0:w], c.ps[:, :, 0:w], ACT.Exp, scale=SCALE)\
                       .then_inc(SEM[f"{n}_PT"], 1)
                return part

            def a_proj(i, g):
                for s in range(2):
                    need(act, "ao_ps", i, s + 1)
                    act.activation(aoT[:, s, :], A.ps[0:HALF, 1 + s, 0:COLS], ACT.Identity,
                                   bias=affine[:, LNS, 1, s:s + 1]).then_inc(SEM["ao"], 1)

            def a_sqkv(i, g):
                for m in range(6):
                    need(act, "s_qkv_ps", i, m + 1)
                    if m >= 2:
                        need(act, "s_phi", i, m - 1)
                    act.activation(e_ssm[:, m % 2, :], A.ps[:, m % 4, 0:COLS], ACT.Exp).then_inc(SEM["s_exp"], 1)
                for t in range(TILES):
                    need(act, "s_qkv_ps", i, 7 + t)
                    copy(A.V[:, t, :, 0:HD], A.ps[:, (6 + t) % 4, 0:D].rearrange("p (h e) -> p h e", e=HD))\
                        .then_inc(SEM["s_v"], 1)

            def a_mT(i, g):
                scaled(A, LNM, "mT_ps", "mT", i, A.xnT)

            def a_m1(i, g):
                if isinstance(i, int):
                    act.wait_ge(SEM["zfill"], 160)
                for m in range(MT):
                    need(act, "m1_ps", i, m + 1)
                    act.activation(gT[:, m, :], A.ps[:, (m + 2) % 4, 0:COLS], ACT.Gelu).then_inc(SEM["gelu"], 1)

            def f_x2T(i, g):
                scaled(F, LNF2, "x2T_ps", "x2T", i, F.xnT)

            all_pairs(act, {
                ("a", "h0"): a_h0, ("a", "xT"): xT(A, LN1), ("a", "qkv"): qkv(A), ("a", "ST"): ST(A),
                ("a", "aproj"): a_proj, ("a", "sqkv"): a_sqkv, ("a", "mT"): a_mT, ("a", "m1"): a_m1,
                ("f", "xT"): xT(F, LNF1), ("f", "qkv"): qkv(F), ("f", "ST"): ST(F), ("f", "x2T"): f_x2T,
            })
            act.wait_ge(SEM["dm"], 1)
            act.activation(R.ex[:], R.dm[:], ACT.Exp).then_inc(SEM["exp_d"], 1)

            def expert(u, j):
                n = f"e{j}_"
                for s in range(2):
                    need(act, n + "xbT_ps", u, s + 1)
                    act.activation(xbT[j][0:HALF, s, :], A.ps[0:HALF, s, 0:CAP], ACT.Identity,
                                   bias=affine[:, LNF2, 1, s:s + 1], scale=affine[:, LNF2, 0, s:s + 1])\
                       .then_inc(SEM[n + "xbT"], 1)
                if j == 1:
                    need(act, "e0_pj_ps", u)
                else:
                    need_last(act, "e1_pj_ps", u)
                for m in range(MT):
                    need(act, n + "fc_ps", u, m + 1)
                    ps = (A.ps[:, 2 + m % 4, :] if m % 4 < 2 else F.ps[:, m % 4 - 2, :])
                    act.activation(heT[:, m, :], ps[:, 0:CAP], ACT.Gelu).then_inc(SEM[n + "he"], 1)

            for j in range(2):
                expert(0, j)
            with act.Fori(1, EXPERTS // 2) as u:
                for j in range(2):
                    expert(u, j)

        @block.vector
        def _(dve):
            def norm(L, i):
                for t in range(TILES):
                    dve.bn_stats(L.st[:, t, :], L.src(t)).then_inc(SEM[L.name + "_stats"], 1)
                need(dve, L.name + "_stats", i)
                dve.memset(carrier[:], 0.0)
                for t in range(TILES):
                    dve.bn_aggr(L.mv[:, t, :], L.st[:, t, :]).then_inc(SEM[L.name + "_aggr"], 1)
                need(dve, L.name + "_rstd", i)
                for t in range(TILES):
                    dve.tensor_scalar(L.dst(t), L.src(t), L.mv[:, t, 0:1], L.rs[:, t:t + 1],
                                      ALU.subtract, ALU.mult).then_inc(SEM[L.name + "_out"], 1)

            def a_ln0(i, g):
                need(dve, "h0", i)
                need(dve, "txt_in", i)
                norm(a0, i)

            def a_ln1(i, g):
                need(dve, "a0_out", i)
                norm(a1, i)

            def f_ln0(i, g):
                need(dve, "hF", i)
                norm(f0, i)

            def f_ln1(i, g):
                need(dve, "f0_out", i)
                norm(f1, i)

            def qkv(c):
                n = c.n
                def part(i, g):
                    for m in range(3):
                        need(dve, f"{n}_qkv_ps", i, 2 * m + 2)
                        dve.tensor_copy(c.kT[:, m, :], c.ps[:, (2 * m + 1) % 4, 0:COLS]).then_inc(SEM[f"{n}_k"], 1)
                return part

            def S(c):
                n = c.n
                def part(i, g):
                    need(dve, f"{n}_S_ps", i, g + 1)
                    if g:
                        need(dve, f"{n}_M_ps", i, g)
                    m = c.negm[:].rearrange("p t (h e) -> p h t e", e=32)
                    dve.tensor_reduce(m[:, :, 0, HD], c.ps[:, :, 0:IMG], AX, ALU.max, negate=True)\
                       .then_inc(SEM[f"{n}_negm"], 1)
                    dve.tensor_reduce(m[:, :, 1:3, HD],
                                      c.ps[:, :, IMG:IMG + 2 * SEQ].rearrange("p h (t k) -> p h t k", t=2),
                                      AX, ALU.max, negate=True).then_inc(SEM[f"{n}_negm"], 1)
                return part

            def M(c):
                n = c.n
                def part(i, g):
                    need(dve, f"{n}_M_ps", i, g + 1)
                    dve.tensor_tensor(c.qT[:, g, :], c.ps[:, 0, 0:COLS], c.qT[:, g, :], ALU.add)\
                       .then_inc(SEM[f"{n}_qa"], 1)
                return part

            def divide(c, pre, i, g, eps):
                need(dve, pre + "PV_ps", i, g + 1)
                dve.memset(carrier[:], 0.0)
                rec = c.rec[:].rearrange("p (s k) -> p s k", s=2)
                o = c.ps[:, 0:2, 0:SEQ]
                dve.stream_shuffle(rec, o, [HD] * 32).then_inc(SEM[pre + "shuf"], 1)
                need(dve, pre + "shuf", i, g + 1)
                if eps:
                    dve.tensor_scalar(c.rec[:], c.rec[:], eps, None, ALU.add).then_inc(SEM[pre + "eps"], 1)
                    need(dve, pre + "eps", i, g + 1)
                dve.reciprocal(c.rec[:], c.rec[:]).then_inc(SEM[pre + "rec"], 1)
                need(dve, pre + "rec", i, g + 1)
                dve.tensor_tensor(c.OT[:, g, :].rearrange("p (s k) -> p s k", s=2), o, rec, ALU.mult)\
                   .then_inc(SEM[pre + "OT"], 1)

            def PV(c):
                return lambda i, g: divide(c, c.n + "_", i, g, 0.0)

            def a_sqkv(i, g):
                for m in range(6):
                    dst = (A.qT if m % 2 == 0 else A.kT)[:, m // 2, :]
                    need(dve, "s_exp", i, m + 1)
                    if m:
                        need(dve, "s_phi", i, m)
                    dve.tensor_scalar(r_ssm[:], A.ps[:, m % 4, 0:COLS], 0.0, ELU_EPS, ALU.max, ALU.add)\
                       .then_inc(SEM["s_relu"], 1)
                    need(dve, "s_relu", i, m + 1)
                    dve.scalar_tensor_tensor(out=dst, in0=e_ssm[:, m % 2, :], scalar=1.0, in1=r_ssm[:],
                                             op0=ALU.min, op1=ALU.add).then_inc(SEM["s_phi"], 1)

            def a_sST(i, g):
                need(dve, "s_ST_ps", i, g + 1)
                if g:
                    need(dve, "s_PV_ps", i, g)
                dve.tensor_tensor(A.PT, A.ps[:, :, 0:W_FULL],
                                  keep01[:].unsqueeze(1).to_broadcast([P, GH, W_FULL]), ALU.mult)\
                   .then_inc(SEM["s_PT"], 1)

            def a_sPV(i, g):
                if g == 0:
                    need(dve, "ao", i)
                divide(A, "s_", i, g, 1e-4 / SCALE)

            def a_so(i, g):
                need(dve, "so_ps", i)
                norm(so, i)

            def a_soT(i, g):
                need(dve, "ao", i)
                for s in range(2):
                    need(dve, "soT_ps", i, s + 1)
                    dve.scalar_tensor_tensor(out=uT[0:HALF, s, :], in0=A.ps[0:HALF, s, 0:COLS],
                                             scalar=affine[:, LNS, 0, s:s + 1], in1=aoT[:, s, :],
                                             op0=ALU.mult, op1=ALU.add).then_inc(SEM["u"], 1)

            def a_out(i, g):
                need_last(dve, "hx2", i)
                for t in range(TILES):
                    need(dve, "out_ps", i, t + 1)
                    dve.tensor_tensor(x2[:, t, :], A.ps[:, 1 + t, 0:D], A.xln[:, t, :], ALU.add)\
                       .then_inc(SEM["x2"], 1)

            def a_lnm(i, g):
                need(dve, "x2", i)
                norm(am, i)

            def a_m2(i, g):
                need(dve, "hs", i)
                need_last(dve, "hx", i)
                for t in range(TILES):
                    need(dve, "m2_ps", i, t + 1)
                    dve.tensor_tensor(hF[:, t, :], A.ps[:, t, 0:D], hs[:, t, :], ALU.add)\
                       .then_inc(SEM["hF"], 1)

            def f_proj(i, g):
                need_last(dve, "hx", i)
                for t in range(TILES):
                    need(dve, "fp_ps", i, t + 1)
                    dve.tensor_tensor(x1[:, t, :], F.ps[:, 1 + t, 0:D], F.xln[:, t, :], ALU.add)\
                       .then_inc(SEM["x1"], 1)

            def f_ln2(i, g):
                need(dve, "x1", i)
                norm(f2, i)

            def f_ln1_guarded(i, g):
                need_last(dve, "xh", i)
                f_ln1(i, g)

            def f_logit(i, g):
                need(dve, "lg_ps", i)
                dve.tensor_copy(logits[:, i, :, :], F.ps[:, 2, 0:TILES * EXPERTS]
                                .rearrange("p (t e) -> p t e", t=TILES)).then_inc(SEM["lg"], 1)

            dve.wait_ge(ready, FILLS)
            dve.wait_ge(SEM["ld_const"], LOADED["const"])
            all_pairs(dve, {
                ("a", "ln0"): a_ln0, ("a", "ln1"): a_ln1, ("a", "qkv"): qkv(A), ("a", "S"): S(A),
                ("a", "M"): M(A), ("a", "PV"): PV(A), ("a", "sqkv"): a_sqkv, ("a", "sST"): a_sST,
                ("a", "sPV"): a_sPV, ("a", "so"): a_so, ("a", "soT"): a_soT, ("a", "out"): a_out,
                ("a", "lnm"): a_lnm, ("a", "m2"): a_m2,
                ("f", "ln0"): f_ln0, ("f", "ln1"): f_ln1_guarded, ("f", "qkv"): qkv(F), ("f", "S"): S(F),
                ("f", "M"): M(F), ("f", "PV"): PV(F), ("f", "fproj"): f_proj, ("f", "ln2"): f_ln2,
                ("f", "logit"): f_logit,
            })

            done = [0]

            def link(ins):
                done[0] += 1
                ins.then_inc(SEM["route"], 1)
                dve.wait_ge(SEM["route"], done[0])

            lg = logits[:].rearrange("p a t e -> p (a t) e")
            dve.wait_ge(SEM["lg"], PAIRS)
            src = lg
            desc_b = desc[:].unsqueeze(1).to_broadcast([P, NT, EXPERTS])

            def per_expert(ap):
                return ap.unsqueeze(2).to_broadcast([P, NT, EXPERTS])

            for k in range(2):
                link(dve.tensor_reduce(R.m[:, k, :], src, AX, ALU.max))
                link(dve.tensor_tensor(R.eq[:], src, per_expert(R.m[:, k, :]), ALU.is_equal))
                link(dve.tensor_tensor(R.cand[:], R.eq[:], desc_b, ALU.mult))
                link(dve.tensor_reduce(R.mc[:], R.cand[:], AX, ALU.max))
                link(dve.tensor_tensor(R.first[:, k, :, :], R.cand[:], per_expert(R.mc[:]), ALU.is_equal))
                if k == 0:
                    link(dve.scalar_tensor_tensor(out=R.l2[:], in0=R.first[:, 0, :, :], scalar=-3.0e38, in1=lg,
                                                  op0=ALU.mult, op1=ALU.add))
                    src = R.l2[:]
                else:
                    for kk in range(2):
                        last = dve.tensor_copy(R.fb[:, :, :, kk, :],
                                               R.first[:, kk, :, :].rearrange("p (a t) e -> p a t e", t=TILES))
                        if kk == 0:
                            link(last)
                    last.then_inc(SEM["fbcast"], 1)
            dve.tensor_tensor(R.dm[:], R.m[:, 1, :], R.m[:, 0, :], ALU.subtract).then_inc(SEM["dm"], 1)
            dve.wait_ge(SEM["exp_d"], 1)
            link(dve.tensor_scalar(R.den[:], R.ex[:], 1.0, None, ALU.add))
            link(dve.reciprocal(R.p[:, 0, :], R.den[:]))
            link(dve.tensor_tensor(R.p[:, 1, :], R.ex[:], R.p[:, 0, :], ALU.mult))
            dve.wait_ge(SEM["rank_ps"], 1)
            link(dve.tensor_copy(R.tot[:], A.ps[:, 3, 0:64].rearrange("p (a k e) -> p a k e", a=PAIRS, k=2)))
            link(dve.memset(R.base[:, 0, 0, :], 0.0))
            for p in range(PAIRS):
                link(dve.tensor_tensor(R.base[:, p + 1, 0, :], R.base[:, p, 0, :], R.tot[:, p, 0, :], ALU.add))
            link(dve.tensor_copy(R.base[:, 0, 1, :], R.base[:, PAIRS, 0, :]))
            for p in range(PAIRS - 1):
                link(dve.tensor_tensor(R.base[:, p + 1, 1, :], R.base[:, p, 1, :], R.tot[:, p, 1, :], ALU.add))
            for t in range(TILES):
                link(dve.tensor_tensor(R.rank[:, :, t, :, :],
                                       A.ps[:, t, 0:64].rearrange("p (a k e) -> p a k e", a=PAIRS, k=2),
                                       R.base[:, 0:PAIRS, :, :], ALU.add))
            flat = "p a t k e -> p (a t k) e"
            fl4 = "p a t k -> p (a t k)"
            for k in range(2):
                link(dve.scalar_tensor_tensor(out=R.kept[:, :, :, k, :], in0=R.rank[:, :, :, k, :], scalar=float(CAP),
                                              in1=R.first[:, k, :, :].rearrange("p (a t) e -> p a t e", t=TILES),
                                              op0=ALU.is_lt, op1=ALU.mult))
            link(dve.tensor_tensor(R.slotv[:].rearrange(flat), R.rank[:].rearrange(flat),
                                   ebase[:].unsqueeze(1).to_broadcast([P, 2 * NT, EXPERTS]), ALU.add))
            link(dve.tensor_tensor(R.slotv[:].rearrange(flat), R.slotv[:].rearrange(flat),
                                   R.kept[:].rearrange(flat), ALU.mult))
            link(dve.tensor_reduce(R.slot[:].rearrange(fl4), R.slotv[:].rearrange(flat), AX, ALU.add))
            link(dve.tensor_reduce(R.ks[:].rearrange(fl4), R.kept[:].rearrange(flat), AX, ALU.add))
            for k in range(2):
                link(dve.tensor_tensor(R.wgt[:, :, :, k], R.ks[:, :, :, k],
                                       R.p[:, k, :].rearrange("p (a t) -> p a t", t=TILES), ALU.mult))
            link(dve.tensor_scalar(R.ks[:], R.ks[:], -1.0, 1.0, ALU.mult, ALU.add))
            link(dve.tensor_tensor(R.dumpv[:], R.ks[:], dump_id[:], ALU.mult))
            link(dve.tensor_tensor(R.dumpv[:], R.dumpv[:], R.slot[:], ALU.add))
            link(dve.tensor_copy(R.gidx[:], R.slot[:]))
            dve.tensor_copy(R.sidx[:], R.dumpv[:]).then_inc(SEM["slots"], 1)

            def expert(u, j):
                n = f"e{j}_"
                need(dve, n + "bp_in", u)
                need_last(dve, n + "st", u)
                for t in range(SLOT_TILES):
                    need(dve, n + "pj_ps", u, t + 1)
                    dve.tensor_tensor(ob[j][:, t, :], F.ps[0:SLOTS, 2 + t % 2, 0:D], b_pj[j][0:SLOTS, :], ALU.add)\
                       .then_inc(SEM[n + "ob"], 1)

            for j in range(2):
                expert(0, j)
            with dve.Fori(1, EXPERTS // 2) as u:
                for j in range(2):
                    expert(u, j)

            for n in range(NT):
                p, t = n // TILES, n % TILES
                dve.wait_ge(gat[n % 4], 32 * (n // 4 + 1))
                dve.scalar_tensor_tensor(out=y_mid[:, n % 2, :], in0=g_rows[:, n % 4, 0, :], scalar=R.wgt[:, p, t, 0:1],
                                         in1=hx_all[:, p, t, :], op0=ALU.mult, op1=ALU.add).then_inc(SEM["ymid"], 1)
                dve.wait_ge(SEM["ymid"], n + 1)
                if n >= 2:
                    dve.wait_ge(ysto[n % 2], stored(n, n % 2))
                dve.scalar_tensor_tensor(out=y_out[:, n % 2, :], in0=g_rows[:, n % 4, 1, :], scalar=R.wgt[:, p, t, 1:2],
                                         in1=y_mid[:, n % 2, :], op0=ALU.mult, op1=ALU.add).then_inc(SEM["yout"], 1)

        @block.gpsimd
        def _(pool):
            fills = [(ones_row[:], 1.0), (onesb[:], 1.0), (neghalf[:], -0.5), (eps[:], EPS)]
            fills += [(b[:], 0.0) for c in (A, F) for b in (c.V, c.negm)]
            fills += [(c.V[:, :, :, HD:HD + 1], 1.0) for c in (A, F)]
            fills += [(b[HALF:HALF + 1, :, :], 1.0) for b in (A.xnT, F.xnT, uT, xbT[0], xbT[1])]
            pool.memset(zrow, 0.0).then_inc(SEM["zero"], 1)
            pool.wait_ge(SEM["zero"], 1)
            assert len(fills) == FILLS
            for n, (buf, value) in enumerate(fills):
                pool.memset(buf, value).then_inc(ready, 1)
                pool.wait_ge(ready, n + 1)

            def rstd(L):
                def part(i, g):
                    need(pool, L.name + "_aggr", i)
                    pool.tensor_tensor(L.ve[:], L.mv[:, :, 1], eps[:], ALU.add)\
                        .then_inc(SEM[L.name + "_var"], 1)
                    need(pool, L.name + "_var", i)
                    pool.tensor_tensor(L.rs[:], L.ve[:], neghalf[:], ALU.pow).then_inc(SEM[L.name + "_rstd"], 1)
                return part

            def a_lnm(i, g):
                rstd(am)(i, g)
                if isinstance(i, int):
                    pool.wait_ge(SEM["ld_mlp"], LOADED["mlp"])
                need(pool, "x2", i)
                need_last(pool, "hF", i)
                pool.tensor_tensor(hs[:], x2[:], hA[:], ALU.add).then_inc(SEM["hx2"], 1)
                need(pool, "hx2", i)
                pool.tensor_tensor(hs[:], hs[:], b_m2[:].unsqueeze(1).to_broadcast([P, TILES, D]), ALU.add)\
                    .then_inc(SEM["hs"], 1)

            def f_ln2(i, g):
                rstd(f2)(i, g)
                need(pool, "x1", i)
                apart(pool)
                pool.tensor_tensor(hx_all[:, i, :, :], x1[:], hF[:], ALU.add).then_inc(SEM["hx"], 1)
                need(pool, "f2_out", i)
                apart(pool)
                pool.tensor_copy(xh_all[:, i, :, :], F.xhat[:]).then_inc(SEM["xh"], 1)

            all_pairs(pool, {
                ("a", "ln0"): rstd(a0), ("a", "ln1"): rstd(a1), ("a", "so"): rstd(so), ("a", "lnm"): a_lnm,
                ("f", "ln0"): rstd(f0), ("f", "ln1"): rstd(f1), ("f", "ln2"): f_ln2,
            })
            pool.wait_ge(SEM["slots"], 1)
            pool.wait_ge(SEM["xh"], PAIRS)
            pool.wait_ge(SEM["zfill"], 160)
            for n in range(NT):
                p, t = n // TILES, n % TILES
                for k in range(2):
                    pool.indirect_dma_start(out=xb_dram, out_offset=bass.IndirectOffsetOnAxis(ap=R.sidx[:, p, t, k:k + 1], axis=0),
                                            in_=xh_all[:, p, t, :], in_offset=None).then_inc(scat, 16)
            for j in range(2):
                pool.wait_ge(SEM[f"e{j}_st"], 16 * (EXPERTS // 2))
            for n in range(NT):
                p, t = n // TILES, n % TILES
                if n >= 4:
                    pool.wait_ge(SEM["yout"], n - 3)
                for k in range(2):
                    pool.indirect_dma_start(out=g_rows[:, n % 4, k, :], out_offset=None, in_=ob_dram,
                                            in_offset=bass.IndirectOffsetOnAxis(ap=R.gidx[:, p, t, k:k + 1], axis=0))\
                        .then_inc(gat[n % 4], 16)


def constants(np):
    bf = np.dtype("bfloat16")
    i_txt, j_txt = np.arange(IMG, SEQ), np.arange(IMG, SEQ)
    c = {}
    pos = np.stack([np.concatenate([np.arange(IMG), SEQ + np.arange(IMG)]),
                    IMG + np.arange(TXT), SEQ + IMG + np.arange(TXT)])
    seq = [np.concatenate([i_txt, np.arange(IMG)]), np.arange(SEQ)]
    for kind, off in (("win", -40960.0), ("full", -1e30)):
        def valid(i, j):
            ok = j <= i
            return ok & (j > i - WINDOW) if kind == "win" else ok
        img_q = np.arange(P)[:, None] % IMG
        txt_q = IMG + np.arange(P)[:, None]
        m = np.concatenate([valid(img_q, np.arange(IMG)[None])] + [valid(txt_q, s[None]) for s in seq], 1)
        c["mask_" + kind] = np.where(m, 0.0, off).astype(bf)
        w0 = 2 * IMG if kind == "win" else SEQ
        t = valid(i_txt[None], j_txt[:, None])
        q0 = seq if kind == "full" else [s[s < 2 * IMG] for s in seq]
        q0 = np.repeat(np.stack(q0), IMG, axis=0)
        mT = np.concatenate([valid(q0, np.arange(P)[:, None] % IMG), t, t], 1)
        c["maskT_" + kind] = np.where(mT, 0.0, off).astype(bf)
        if kind == "full":
            c["keep01"] = mT.astype(np.float32)
    c["identf"] = np.eye(P, dtype=np.float32)
    c["identb"] = np.eye(P).astype(bf)
    c["order"] = np.stack([pos[s][:, None] < pos[t][None] for s in range(TILES) for t in range(TILES)], 1).astype(bf)
    c["desc"] = np.tile(np.arange(EXPERTS, 0, -1, dtype=np.float32), (P, 1))
    c["ebase"] = np.tile(CAP * np.arange(EXPERTS, dtype=np.float32), (P, 1))
    n = np.arange(PAIRS * TILES).reshape(PAIRS, TILES)[None, :, :, None] * P + np.arange(P)[:, None, None, None]
    c["dump_id"] = (DUMP + TOKENS * np.arange(2)[None, None, None, :] + n).astype(np.float32)
    return c


def layout(np, x):
    f = {k: np.asarray(v) for k, v in x.items()}
    z = np.zeros
    o = {}
    patches = f["x"].reshape(BATCH, 3, 2 * 4, 16, 8, 16)
    patches = patches.transpose(1, 3, 5, 0, 2, 4).reshape(KT, P, PAIRS, P)
    o["xT"] = patches.transpose(2, 1, 0, 3)
    o["txt"] = f["txt"].reshape(PAIRS, 2, TXT, D).transpose(0, 2, 1, 3)
    o["w_tok"] = f["L0_tok_W"].T.reshape(KT, P, D).transpose(1, 0, 2)
    o["b_tok"] = f["L0_tok_b"].reshape(1, D)

    def biased(w, b):
        r = z((HALF + 1, 2, w.shape[1]), np.float32)
        r[0:HALF] = w.reshape(2, HALF, -1).transpose(1, 0, 2)
        r[HALF, 1] = b
        return r

    for n, key in (("attn", "L0_attn_attn_qkv"), ("ssm", "L0_attn_ssm_qkv"), ("ffn", "L0_ffn_attn_qkv")):
        w, b = f[key + "_w"], f[key + "_b"]
        full = biased(w, b)
        r = z((HALF + 1, 2, 6, GH, 32), np.float32)
        r[..., 0:HD] = full[:, :, 0:2 * D].reshape(HALF + 1, 2, 6, GH, HD)
        if n != "ssm":
            r[HALF, 1, GROUPS:, :, HD] = 1.0
        o["wqk_" + n] = r.reshape(HALF + 1, 2, 6, P)
        o["wv_" + n] = full[:, :, 2 * D:]
    for n, wk, bk in (("attn", "L0_attn_attn_proj_w", "L0_attn_attn_proj_b"), ("ssm", "L0_attn_ssm_out_w", None),
                      ("ffn", "L0_ffn_attn_proj_w", "L0_ffn_attn_proj_b")):
        r = z((GROUPS, GH, 32, D), np.float32)
        r[:, :, 0:HD] = f[wk].reshape(GROUPS, GH, HD, D)
        if bk:
            r[0, 0, HD] = f[bk]
        o["wp_" + n] = r.reshape(GROUPS, P, D).transpose(1, 0, 2)
    o["b_so"] = f["L0_attn_ssm_out_b"].reshape(1, D)
    o["w_out"] = biased(f["L0_attn_out_w"], f["L0_attn_out_b"])
    o["w_m1"] = biased(f["L0_attn_mlp_w1"], f["L0_attn_mlp_b1"])
    o["w_m2"] = f["L0_attn_mlp_w2"].reshape(MT, P, D).transpose(1, 0, 2)
    o["b_m2"] = f["L0_attn_mlp_b2"].reshape(1, D)
    o["w_g"] = f["L0_ffn_w_g"].reshape(2, HALF, EXPERTS).transpose(1, 0, 2)
    norms = (("L0_attn_ln1_g", "L0_attn_ln1_b"), ("L0_attn_ssm_ln_g", "L0_attn_ssm_ln_b"),
             ("L0_attn_lnm_g", "L0_attn_lnm_b"), ("L0_ffn_ln1_w", "L0_ffn_ln1_b"), ("L0_ffn_ln2_w", "L0_ffn_ln2_b"))
    o["affine"] = np.stack([np.stack([f[k].reshape(2, HALF) for k in ab]) for ab in norms]).transpose(3, 0, 1, 2)
    o["e_fc"] = np.stack([biased(f["L0_ffn_exp_fc_w"][e], f["L0_ffn_exp_fc_b"][e, 0]) for e in range(EXPERTS)])
    o["e_pj"] = f["L0_ffn_exp_proj_w"].reshape(EXPERTS, MT, P, D).transpose(0, 2, 1, 3)
    o["e_bpj"] = f["L0_ffn_exp_proj_b"].reshape(EXPERTS, 1, D)
    return o


def kernel(**inputs):
    import numpy as np
    import concourse.bacc as bacc
    from concourse.bass_utils import run_bass_kernel_spmd as run

    nc = bacc.Bacc("TRN2", target_bir_lowering=False, num_devices=1)
    arrays = {k: np.ascontiguousarray(v) for k, v in {**constants(np), **layout(np, inputs)}.items()}
    d = Named({k: nc.dram_tensor(k + "_dram", a.shape, mybir.dt.from_np(a.dtype), kind="ExternalInput").ap()
               for k, a in arrays.items()})
    out = nc.dram_tensor("out_dram", (BATCH, SEQ, D), F32, kind="ExternalOutput").ap()
    build(nc, d, out)
    r = run(nc, [{k + "_dram": a for k, a in arrays.items()}], core_ids=[0])
    return r.results[0]["out_dram"]
```

```python
from contextlib import ExitStack

import concourse.bass as bass
from concourse import mybir

ALU = mybir.AluOpType
ACT = mybir.ActivationFunctionType
F32 = mybir.dt.float32
BF16 = mybir.dt.bfloat16
I32 = mybir.dt.int32
AX = mybir.AxisListType.X

P = 128
D = 192
HALF = 96
HEADS, HD = 12, 16
GROUPS, GH = 3, 4
BATCH, IMG, TXT = 8, 64, 128
SEQ = IMG + TXT
PAIRS, TILES = BATCH // 2, 3
STREAMS = 2
TURNS = PAIRS // STREAMS
COLS = 2 * SEQ
TOKENS = BATCH * SEQ
KT = 768 // P
HID = 4 * D
MT = HID // P
WINDOW = 64
EXPERTS = 8
CAP = 2 * 5 * TOKENS // (4 * EXPERTS)
CAP += CAP % 2
SLOT_TILES = 4
SLOTS = CAP // SLOT_TILES
EPS = 1e-5
SCALE = HD ** -0.5
ELU_EPS = 1e-4
DUMP = EXPERTS * CAP
ROWS = DUMP + 2 * TOKENS
W_FULL = SEQ + TXT + TXT
SEG = (slice(0, P), slice(P, P + SEQ), slice(P + SEQ, P + 2 * SEQ))
W_Q = P + 2 * SEQ
TURNED = (P, 2 * P, 0, 3 * P)
assert W_Q == 512
assert SLOTS <= P and CAP <= 512


class Named(dict):

    def __getattr__(self, name):
        return self[name]


TILE_AT = (P, 0, 2 * P)
IMG_COLS = (slice(TXT, SEQ), slice(SEQ, SEQ + IMG))
TXT_COLS = (slice(0, TXT), slice(SEQ + IMG, COLS))


def tile_cols(ap, t):
    return ap[:, TILE_AT[t]:TILE_AT[t] + P]


def build(nc, d, out):
    ctx = ExitStack()
    with ctx:
        def sb(name, shape, dt=F32):
            return ctx.enter_context(nc.sbuf_tensor(name, shape, dt))

        SEM, PER = {}, {}

        def sem(name, per=1):
            SEM[name] = ctx.enter_context(nc.semaphore(name))
            PER[name] = per
            return SEM[name]

        def need(eng, name, i, k=None):
            eng.wait_ge(SEM[name], i * PER[name] + (PER[name] if k is None else k))

        def need_last(eng, name, i):
            if isinstance(i, int) and i == 0:
                return
            eng.wait_ge(SEM[name], i * PER[name])

        def apart(eng):
            eng.wait_ge(SEM["setup_pool"], FILLS)

        identf = sb("identf", [P, P])
        identb = sb("identb", [P, P], BF16)
        mask = {n: sb(f"mask_{n}", [P, W_Q], BF16) for n in ("win", "full")}
        keep01 = sb("keep01", [P, W_FULL])
        order = sb("order", [P, 9, P], BF16)
        onesb = sb("onesb", [P, P], BF16)
        ones_row = sb("ones_row", [1, P])
        neghalf = sb("neghalf", [P, TILES])
        eps = sb("eps", [P, TILES])
        w_tok = sb("w_tok", [P, KT, D])
        b_tok = sb("b_tok", [1, D])
        w_qk = {n: sb(f"w_qk_{n}", [HALF + 1, 2, GROUPS, P]) for n in ("attn", "ssm", "ffn")}
        w_v = {n: sb(f"w_v_{n}", [HALF + 1, 2, D]) for n in ("attn", "ssm", "ffn")}
        w_proj = {n: sb(f"w_proj_{n}", [P, GROUPS, D]) for n in ("attn", "ssm", "ffn")}
        b_so = sb("b_so", [1, D])
        w_out = sb("w_out", [HALF + 1, 2, D])
        w_m1 = sb("w_m1", [HALF + 1, 2, HID])
        w_m2 = sb("w_m2", [P, MT, D])
        b_m2 = sb("b_m2", [P, D])
        w_g = sb("w_g", [HALF, 2, EXPERTS])
        affine = sb("affine", [HALF, 5, 2, 2])
        AFFINE = {"a1": 0, "so": 1, "am": 2, "f1": 3, "f2": 4}

        def cut(buf, at, a, b):
            return buf[:, at:at + a * b].rearrange("p (a b) -> p a b", a=a)

        SOFT = (("turned", 2), ("scaled", 2), ("S_ps", GROUPS), ("negm", 2 * GROUPS),
                ("P", GROUPS * GH * TILES), ("T_ps", GROUPS * GH), ("PTd", GROUPS * GH // 2),
                ("PTa", GROUPS * GH // 2), ("rr", GROUPS), ("recb", GROUPS), ("R_ps", GROUPS), ("R", GROUPS),
                ("PV_ps", GROUPS), ("OT", GROUPS), ("qkv_ps", 2 * GROUPS), ("q", 3), ("k", 3), ("v", 3))
        SINGLE = (("x_in", 16), ("txt_in", 16), ("h0_ps", 1), ("h0", 1), ("ao_ps", 2), ("ao", 2),
                  ("s_exp", 3), ("s_relu", 3), ("s_phi", 3),
                  ("s_PT", 3), ("s_div", 3 * GROUPS),
                  ("tok_ps", 3), ("u", 2), ("x2", 3),
                  ("hx2", 1), ("hs", 1), ("m1_ps", 6), ("gelu", 6),
                  ("m2_ps", 3), ("hF", 3),
                  ("hx", 1), ("xh", 1),
                  ("lg_ps", 1), ("lg", 1))
        LAYERS = ("attn", "ssm", "ffn")
        TURNED_X = ("a1", "so", "am", "f1", "f2")
        SCALED_X = ("a1", "am", "f1", "f2")
        TOKENS_X = ("so", "out", "ffn")
        NORMS = ("a0", "a1", "so", "am", "f0", "f1", "f2")

        def stream(n, index):
            c = Named(n=n, index=index)
            c["ps"] = ctx.enter_context(nc.psum_tensor(f"ps_{n}", [P, 4, 512], F32))
            c["work"] = sb(f"work_{n}", [P, 2 * GROUPS * COLS + GH * W_Q])
            c["qT"] = cut(c.work, 0, GROUPS, COLS)
            c["kT"] = cut(c.work, GROUPS * COLS, GROUPS, COLS)
            c["PT"] = cut(c.work, 2 * GROUPS * COLS, GH, W_Q)
            c["g_work"] = sb(f"g_work_{n}", [P, MT * COLS])
            c["Pq"] = cut(c.g_work, 0, GH, W_Q)
            c["e_ssm"] = cut(c.g_work, 0, 2, COLS)
            c["r_ssm"] = c.g_work[:, 2 * COLS:3 * COLS]
            c["aoT"] = cut(c.g_work[0:HALF, :], 3 * COLS, 2, COLS)
            c["gT"] = cut(c.g_work, 0, MT, COLS)
            for name, shape in (("V", [P, TILES, HEADS, 32]),
                                ("negm", [P, GH, TILES]), ("rsum", [P, GH, TILES]), ("rr", [P, GH, TILES]),
                                ("recb", [P, TILES, GH, 32]), ("rec", [P, COLS]), ("OT", [P, GROUPS, COLS]),
                                ("xln", [P, TILES, D]), ("xhat", [P, TILES, D]),
                                ("xnT", [HALF + 1, 2, COLS]), ("xT_in", [P, KT, P]),
                                ("h", [P, TILES, D]),
                                ("x2", [P, TILES, D]),
                                ("st", [P, TILES, 6]), ("mv", [P, TILES, 2]), ("ve", [P, TILES]), ("rs", [P, TILES]), ("carrier", [P, 1])):
                c[name] = sb(f"{name}_{n}", shape)
            for s, per in SOFT + SINGLE:
                sem(f"{n}_{s}", per)
            for s, per in (("stats", TILES), ("aggr", TILES), ("rstd", 2), ("out", TILES)):
                sem(f"{n}_ln_{s}", per)
            return c

        def norms(c):
            where = {"a0": (lambda t: c.h[:, t, :], lambda t: c.xln[:, t, :]),
                     "a1": (lambda t: c.xln[:, t, :], lambda t: c.xhat[:, t, :]),
                     "so": (lambda t: c.ps[:, 1 + t, 0:D], lambda t: c.xhat[:, t, :]),
                     "am": (lambda t: c.x2[:, t, :], lambda t: c.xhat[:, t, :]),
                     "f0": (lambda t: c.h[:, t, :], lambda t: c.xln[:, t, :]),
                     "f1": (lambda t: c.xln[:, t, :], lambda t: c.xhat[:, t, :]),
                     "f2": (lambda t: c.x2[:, t, :], lambda t: c.xhat[:, t, :])}
            return {name: Named(src=where[name][0], dst=where[name][1]) for name in NORMS}

        X, Y = stream("x", 0), stream("y", 1)
        for c in (X, Y):
            c["norms"] = norms(c)
        phases = {w + ph: Named(c, phase=k, kind=("win", "full")[k], w=("attn", "ffn")[k], norm=("a1", "f1")[k])
                  for w, c in (("x", X), ("y", Y)) for k, ph in enumerate("af")}

        def use(c, u):
            return 2 * u + c.phase

        def nth(uses, which, u):
            return len(uses) * u + uses.index(which)

        def norm_use(name, u):
            return nth(NORMS, name, u)

        def pair(c, u):
            return STREAMS * u + c.index

        hx_all = sb("hx_all", [P, PAIRS, TILES, D])
        xh_all = sb("xh_all", [P, PAIRS, TILES, D])
        logits = sb("logits", [P, PAIRS, TILES, EXPERTS])

        FILLS = 10
        ready = sem("setup_pool")
        loads = ["const", "tok", "attn", "ssm", "mlp", "ffn"]
        LOADED = {n: 0 for n in loads}
        for n in loads:
            sem("ld_" + n)

        xb_dram = nc.dram_tensor("xb_rows", [ROWS, D], F32, kind="Internal").ap()
        ob_dram = nc.dram_tensor("ob_rows", [EXPERTS * CAP, D], F32, kind="Internal").ap()
        zrow = X.g_work[:, 0:EXPERTS * CAP // P * D // 10]
        R = Named()
        NT = PAIRS * TILES
        for name, shape, dt in (("m", [P, 2, NT], F32), ("eq", [P, NT, EXPERTS], F32),
                                ("cand", [P, NT, EXPERTS], F32), ("mc", [P, NT], F32),
                                ("first", [P, 2, NT, EXPERTS], F32), ("l2", [P, NT, EXPERTS], F32),
                                ("fb", [P, PAIRS, TILES, 2, EXPERTS], BF16), ("dm", [P, NT], F32), ("ex", [P, NT], F32),
                                ("den", [P, NT], F32), ("p", [P, 2, NT], F32),
                                ("base", [P, PAIRS + 1, 2, EXPERTS], F32),
                                ("tot", [P, PAIRS, 2, EXPERTS], F32),
                                ("rank", [P, PAIRS, TILES, 2, EXPERTS], F32),
                                ("kept", [P, PAIRS, TILES, 2, EXPERTS], F32),
                                ("slotv", [P, PAIRS, TILES, 2, EXPERTS], F32),
                                ("ks", [P, PAIRS, TILES, 2], F32), ("slot", [P, PAIRS, TILES, 2], F32),
                                ("dumpv", [P, PAIRS, TILES, 2], F32),
                                ("wgt", [P, PAIRS, TILES, 2], F32),
                                ("gidx", [P, PAIRS, TILES, 2], I32), ("sidx", [P, PAIRS, TILES, 2], I32)):
            R[name] = sb("r_" + name, shape, dt)
        desc = sb("desc", [P, EXPERTS])
        ebase = sb("ebase", [P, EXPERTS])
        dump_id = sb("dump_id", [P, PAIRS, TILES, 2])
        w_fc = [sb("w_fc0", [HALF + 1, 2, HID]), w_m1]
        w_pj = [w_m2, w_tok]
        b_pj = [sb(f"b_pj{j}", [P, D]) for j in range(2)]
        xbT = [cut(Y.g_work[0:HALF + 1, :], j * 2 * CAP, 2, CAP) for j in range(2)]
        heT = cut(X.work, 0, MT, CAP)
        xb = [cut(Y.work[0:SLOTS, :], j * SLOT_TILES * D, SLOT_TILES, D) for j in range(2)]
        ob = [cut(Y.work[0:SLOTS, :], (2 + j) * SLOT_TILES * D, SLOT_TILES, D) for j in range(2)]
        g_rows = X.g_work[:, 0:8 * D].rearrange("p (a b n) -> p a b n", a=4, b=2)
        y_mid = cut(X.g_work, 8 * D, 2, D)
        y_out = cut(X.g_work, 10 * D, 2, D)
        for s in ("xb_ones", "route", "dm", "exp_d", "rank_ps", "slots", "zero", "zfill", "fbcast"):
            sem(s)
        for j in range(2):
            for s, per in (("fc_in", 16), ("pj_in", 16), ("xb_in", 16), ("xbT_ps", 2), ("xbT", 2),
                           ("bp_in", 16), ("fc_ps", 6), ("he", 6), ("pj_ps", 4), ("ob", 4), ("st", 16)):
                sem(f"e{j}_{s}", per)
        scat = sem("scattered", 16)
        gat = [sem(f"gathered{j}") for j in range(4)]
        sem("ymid")
        sem("yout")
        ysto = [sem(f"ystored{j}") for j in range(2)]

        def times(names, n):
            return [(name, g) for g in range(n) for name in names]

        def named(ph, some):
            return [(ph, *x) for x in some]

        soft = times(("S", "T", "PV"), GROUPS)
        turn_steps = (
            named("a", times(("h0", "ln0", "ln0x", "ln1", "ln1x", "xT"), 1) + times(("qkv",), 3) + soft
                  + times(("aproj",), 1) + times(("sqkv",), 3) + times(("sST", "sPV", "sdiv"), GROUPS)
                  + times(("so", "sox", "soT", "out", "lnm", "lnmx", "mT"), 1) + times(("m1",), 3) + times(("m2",), 3))
            + named("f", times(("ln0", "ln0x", "ln1", "ln1x", "xT"), 1) + times(("qkv",), 3) + soft
                    + times(("fproj", "ln2", "ln2x", "x2T", "logit"), 1)))
        WOVEN = "xxxxyyxxyyyxxxyxyxyyxyxyxyxyxyxyxyxyxyxyxyxyyxxyxyyxxyxyxyxyxxyxyxxxyxyxyxxyyyxxyxyyxxxxyyyyyyyyxxxxyyyyxyxyxyxyxyxyxyxyxyxxyyxyxyxy"
        assert WOVEN.count("x") == len(turn_steps) and WOVEN.count("y") == len(turn_steps)

        def steps(parts, u):
            at = {w: iter(turn_steps) for w in "xy"}
            for w in WOVEN:
                ph, name, g = next(at[w])
                if (ph, name) in parts:
                    parts[ph, name](phases[w + ph], u, g)

        def all_turns(eng, parts):
            steps(parts, 0)
            with eng.Fori(1, TURNS) as u:
                steps(parts, u)

        block = ctx.enter_context(nc.Block())

        def stored(n, j):
            return sum(16 * (2 if m % TILES == 0 else 1) for m in range(n) if m % 2 == j)

        @block.sync
        def _(sp):
            def load(n, dst, src):
                LOADED[n] += 16
                sp.dma_start(dst, src).then_inc(SEM["ld_" + n], 16)

            def tokens_in(u):
                for c in (X, Y):
                    need_last(sp, f"{c.n}_h0_ps", u)
                    sp.dma_start(c.xT_in[:], d.xT[pair(c, u)]).then_inc(SEM[f"{c.n}_x_in"], 16)
                for c in (X, Y):
                    need_last(sp, f"{c.n}_hx", u)
                    sp.dma_start(c.h[:, 1:3, :], d.txt[pair(c, u)]).then_inc(SEM[f"{c.n}_txt_in"], 16)

            load("tok", w_tok[:], d.w_tok)
            load("tok", b_tok[:], d.b_tok)
            tokens_in(0)
            load("const", identf[:], d.identf)
            load("const", identb[:], d.identb)
            load("const", affine[:], d.affine)
            for n in ("win", "full"):
                load("const", mask[n][:], d["mask_" + n])
            load("const", keep01[:], d.keep01)
            load("const", order[:], d.order)
            load("const", desc[:], d.desc)
            load("const", ebase[:], d.ebase)
            load("const", dump_id[:], d.dump_id)
            load("attn", w_qk["attn"][:], d.wqk_attn)
            load("attn", w_v["attn"][:], d.wv_attn)
            load("attn", w_proj["attn"][:], d.wp_attn)
            load("ssm", w_qk["ssm"][:], d.wqk_ssm)
            load("ssm", w_v["ssm"][:], d.wv_ssm)
            load("ssm", w_proj["ssm"][:], d.wp_ssm)
            load("ssm", b_so[:], d.b_so)
            load("ssm", w_out[:], d.w_out)
            load("mlp", w_m1[:], d.w_m1)
            load("mlp", w_m2[:], d.w_m2)
            load("mlp", b_m2[:], d.b_m2.to_broadcast([P, D]))
            load("ffn", w_qk["ffn"][:], d.wqk_ffn)
            load("ffn", w_v["ffn"][:], d.wv_ffn)
            load("ffn", w_proj["ffn"][:], d.wp_ffn)
            load("ffn", w_g[:], d.w_g)
            sp.wait_ge(SEM["zero"], 1)
            zr = xb_dram[0:EXPERTS * CAP, :].rearrange("(k p r) n -> k p (r n)", p=P, k=10)
            for k in range(10):
                sp.dma_start(zr[k], zrow).then_inc(SEM["zfill"], 16)

            for u in range(1, TURNS):
                tokens_in(u)

            def expert_in(u, j):
                need_last(sp, f"e{j}_fc_ps", u)
                sp.dma_start(w_fc[j][:], d.e_fc[2 * u + j]).then_inc(SEM[f"e{j}_fc_in"], 16)
                need_last(sp, f"e{j}_pj_ps", u)
                sp.dma_start(w_pj[j][:], d.e_pj[2 * u + j]).then_inc(SEM[f"e{j}_pj_in"], 16)
                need_last(sp, f"e{j}_ob", u)
                sp.dma_start(b_pj[j][:], d.e_bpj[2 * u + j].to_broadcast([P, D])).then_inc(SEM[f"e{j}_bp_in"], 16)

            def rows_in(u, j):
                need_last(sp, f"e{j}_xbT_ps", u)
                rows = xb_dram[0:EXPERTS * CAP, :].rearrange("(e t s) n -> e s t n", e=EXPERTS, s=SLOTS)
                sp.dma_start(xb[j], rows[2 * u + j]).then_inc(SEM[f"e{j}_xb_in"], 16)

            def rows_out(u, j):
                need(sp, f"e{j}_ob", u)
                rows = ob_dram.rearrange("(e t s) n -> e s t n", e=EXPERTS, s=SLOTS)
                sp.dma_start(rows[2 * u + j], ob[j]).then_inc(SEM[f"e{j}_st"], 16)

            for c in (X, Y):
                for n in ("m1_ps", "m2_ps"):
                    need(sp, f"{c.n}_{n}", TURNS - 1)
            expert_in(0, 0)
            expert_in(0, 1)
            sp.wait_ge(scat, 16 * 2 * NT)
            rows_in(0, 0)
            rows_in(0, 1)
            with sp.Fori(0, EXPERTS // 2 - 1) as u:
                for j in range(2):
                    rows_out(u, j)
                    expert_in(u + 1, j)
                    rows_in(u + 1, j)
            for j in range(2):
                rows_out(EXPERTS // 2 - 1, j)
            for n in range(NT):
                p, t = n // TILES, n % TILES
                sp.wait_ge(SEM["yout"], n + 1)
                if t == 0:
                    for b in range(2):
                        sp.dma_start(out[2 * p + b, 0:IMG, :], y_out[b * IMG:(b + 1) * IMG, n % 2, :]).then_inc(ysto[n % 2], 16)
                else:
                    sp.dma_start(out[2 * p + t - 1, IMG:SEQ, :], y_out[:, n % 2, :]).then_inc(ysto[n % 2], 16)
            for j in range(2):
                sp.wait_ge(ysto[j], stored(NT, j))

        @block.tensor
        def _(pe):
            def mm(out_, lhsT, rhs, start=True, stop=True, skip=False):
                return pe.matmul(out_, lhsT, rhs, start=start, stop=stop, skip_group_check=skip)

            def wait_loads(*names):
                for n in names:
                    pe.wait_ge(SEM["ld_" + n], LOADED[n])

            def turn(c, norm, u):
                for s in range(2):
                    for t in range(TILES):
                        need(pe, f"{c.n}_ln_out", norm_use(norm, u), t + 1)
                        last = pe.transpose(tile_cols(c.ps[0:HALF, s, 0:COLS], t), c.xhat[:, t, s * HALF:(s + 1) * HALF],
                                            identf[:])
                    last.then_inc(SEM[f"{c.n}_turned"], 1)

            def halves(out_, w, xT, stop=True):
                mm(out_, w(0, HALF), xT(0, HALF), True, False)
                return mm(out_, w(1, HALF + 1), xT(1, HALF + 1), False, stop)

            def a_h0(c, u, g):
                if isinstance(u, int):
                    wait_loads("tok")
                    pe.wait_ge(ready, FILLS)
                need(pe, f"{c.n}_x_in", u)
                need_last(pe, f"{c.n}_lg", u)
                for k in range(KT):
                    mm(c.ps[:, 0, 0:D], c.xT_in[:, k, :], w_tok[:, k, :], k == 0, False)
                mm(c.ps[:, 0, 0:D], ones_row[:], b_tok[:], False, True).then_inc(SEM[f"{c.n}_h0_ps"], 1)

            def xT(c, u, g):
                if c.phase == 0:
                    if isinstance(u, int):
                        wait_loads("const")
                    need(pe, f"{c.n}_h0", u)
                turn(c, c.norm, u)

            def qkv(c, w, free, u, g):
                if g == 0 and isinstance(u, int):
                    wait_loads(w)
                free(2 * g)
                halves(c.ps[:, 2 * g % 4, 0:COLS], lambda s, k: w_qk[w][0:k, s, g, :],
                       lambda s, k: c.xnT[0:k, s, :]).then_inc(SEM[f"{c.n}_qkv_ps"], 1)
                free(2 * g + 1)
                halves(c.ps[:, (2 * g + 1) % 4, 0:D], lambda s, k: tile_cols(c.xnT[0:k, s, :], g),
                       lambda s, k: w_v[w][0:k, s, :]).then_inc(SEM[f"{c.n}_qkv_ps"], 1)

            def soft_qkv(c, u, g):
                i = use(c, u)
                def free(n):
                    if n == 4:
                        need(pe, f"{c.n}_q", i, 1)
                    if n == 5:
                        need(pe, f"{c.n}_v", nth(LAYERS, c.w, u), 1)
                if g == 0:
                    need(pe, f"{c.n}_scaled", nth(SCALED_X, c.norm, u))
                qkv(c, c.w, free, u, g)

            def a_sqkv(c, u, g):
                def free(n):
                    if n == 1 or n == 2:
                        need(pe, f"{c.n}_ao", u)
                    if n == 4:
                        need(pe, f"{c.n}_s_relu", u, 1)
                    if n == 5:
                        need(pe, f"{c.n}_v", nth(LAYERS, "ssm", u), 1)
                qkv(c, "ssm", free, u, g)

            def S(c, u, g):
                n = c.n
                i = use(c, u)
                if g == 0:
                    need(pe, f"{n}_q", i)
                    need(pe, f"{n}_k", nth(LAYERS, c.w, u))
                    need(pe, f"{n}_v", nth(LAYERS, c.w, u))
                else:
                    need(pe, f"{n}_OT", nth(LAYERS, c.w, u), g)
                for b in range(GH):
                    mm(c.ps[:, b, :], identb[:], mask[c.kind][:], True, True)
                for t, keys in enumerate((slice(TXT, TXT + P), slice(0, SEQ), slice(SEQ, COLS))):
                    for b in range(GH):
                        r = slice(32 * b, 32 * b + HD)
                        last = mm(c.ps[:, b, SEG[t]], tile_cols(c.qT[r, g, :], t), c.kT[r, g, keys],
                                  False, True, True)
                last.then_inc(SEM[f"{n}_S_ps"], 1)

            def T(c, u, g):
                n = c.n
                i = use(c, u)
                for b in range(GH):
                    need(pe, f"{n}_P", i, (GH * g + b + 1) * TILES)
                    for m, at in enumerate(TURNED):
                        last = pe.transpose(c.ps[:, b, m * P:(m + 1) * P], c.Pq[:, b, at:at + P], identf[:])
                    last.then_inc(SEM[f"{n}_T_ps"], 1)

            def scoresT(c, g):
                heads = [slice(32 * b, 32 * b + HD) for b in range(GH)]
                for s in range(2):
                    for b, r in enumerate(heads):
                        mm(c.ps[IMG * s:IMG * (s + 1), b, 0:SEQ], c.kT[r, g, IMG_COLS[s]],
                           c.qT[r, g, s * SEQ:(s + 1) * SEQ], True, True, True)
                for s in range(2):
                    for b, r in enumerate(heads):
                        last = mm(c.ps[:, b, SEQ + s * TXT:SEQ + (s + 1) * TXT], c.kT[r, g, TXT_COLS[s]],
                                  c.qT[r, g, TXT_COLS[s]], True, True, True)
                return last

            def values(c, g, w):
                for b in range(GH):
                    for s in range(2):
                        for m, (o, rows, tile, cols) in enumerate(w[s]):
                            last = mm(c.ps[32 * b:32 * b + 32, s, o], c.V[rows, tile, GH * g + b, :],
                                      c.PT[rows, b, cols], m == 0, True, True)
                return last

            ALL, LOW, HIGH = slice(0, P), slice(0, IMG), slice(IMG, P)
            TXT_0, TXT_1, IMG_1 = slice(0, TXT), slice(IMG, SEQ), slice(0, IMG)
            soft_values = (((TXT_0, ALL, 1, slice(0, P)), (slice(0, SEQ), LOW, 0, slice(P, P + SEQ))),
                           ((TXT_1, ALL, 2, slice(3 * P, 4 * P)), (TXT_1, HIGH, 0, slice(P, 2 * P)),
                            (IMG_1, HIGH, 0, slice(P + SEQ, 3 * P))))
            ssm_values = (((TXT_0, ALL, 1, slice(SEQ, SEQ + P)), (slice(0, SEQ), LOW, 0, slice(0, SEQ))),
                          ((TXT_1, ALL, 2, slice(SEQ + P, SEQ + 2 * P)), (slice(0, SEQ), HIGH, 0, slice(0, SEQ))))

            def PV(c, u, g):
                n = c.n
                i = use(c, u)
                need(pe, f"{n}_PTd", i, 2 * g + 2)
                need(pe, f"{n}_PTa", i, 2 * g + 2)
                need(pe, f"{n}_recb", i, g + 1)
                for t in range(TILES):
                    last = pe.transpose(tile_cols(c.ps[:, 2, 0:COLS], t),
                                        c.recb[:, t, :, :].rearrange("p h e -> p (h e)"), identf[:])
                last.then_inc(SEM[f"{n}_R_ps"], 1)
                values(c, g, soft_values).then_inc(SEM[f"{n}_PV_ps"], 1)

            def a_proj(c, u, g):
                need(pe, f"{c.n}_OT", nth(LAYERS, c.w, u))
                for s in range(2):
                    for k in range(GROUPS):
                        last = mm(c.ps[0:HALF, 1 + s, 0:COLS], w_proj["attn"][:, k, s * HALF:(s + 1) * HALF],
                                  c.OT[:, k, :], k == 0, k == GROUPS - 1)
                    last.then_inc(SEM[f"{c.n}_ao_ps"], 1)

            def a_sST(c, u, g):
                if g == 0:
                    need(pe, f"{c.n}_s_phi", u)
                    need(pe, f"{c.n}_k", nth(LAYERS, "ssm", u))
                    need(pe, f"{c.n}_v", nth(LAYERS, "ssm", u))
                else:
                    need(pe, f"{c.n}_OT", nth(LAYERS, "ssm", u), g)
                scoresT(c, g).then_inc(SEM[f"{c.n}_S_ps"], 1)

            def a_sPV(c, u, g):
                need(pe, f"{c.n}_s_PT", u, g + 1)
                values(c, g, ssm_values).then_inc(SEM[f"{c.n}_PV_ps"], 1)

            def a_so(c, u, g):
                need(pe, f"{c.n}_OT", nth(LAYERS, "ssm", u))
                for t in range(TILES):
                    for k in range(GROUPS):
                        mm(c.ps[:, 1 + t, 0:D], tile_cols(c.OT[:, k, :], t), w_proj["ssm"][:, k, :], k == 0, False)
                    mm(c.ps[:, 1 + t, 0:D], ones_row[:], b_so[:], False, True).then_inc(SEM[f"{c.n}_tok_ps"], 1)

            def a_soT(c, u, g):
                need(pe, f"{c.n}_ln_out", norm_use("so", u))
                turn(c, "so", u)

            def a_out(c, u, g):
                need(pe, f"{c.n}_u", u)
                for t in range(TILES):
                    halves(c.ps[:, 1 + t, 0:D], lambda s, k: tile_cols(c.xnT[0:k, s, :], t),
                           lambda s, k: w_out[0:k, s, :]).then_inc(SEM[f"{c.n}_tok_ps"], 1)

            def a_mT(c, u, g):
                if isinstance(u, int):
                    wait_loads("mlp")
                turn(c, "am", u)

            def a_m1(c, u, g):
                need(pe, f"{c.n}_scaled", nth(SCALED_X, "am", u))
                for m in range(2 * g, 2 * g + 2):
                    if m >= 4:
                        need(pe, f"{c.n}_gelu", u, m - 3)
                    halves(c.ps[:, (m + 2) % 4, 0:COLS], lambda s, k: w_m1[0:k, s, m * P:(m + 1) * P],
                           lambda s, k: c.xnT[0:k, s, :]).then_inc(SEM[f"{c.n}_m1_ps"], 1)

            def a_m2(c, u, t):
                need(pe, f"{c.n}_gelu", u)
                for m in range(MT):
                    last = mm(c.ps[:, t, 0:D], tile_cols(c.gT[:, m, :], t), w_m2[:, m, :], m == 0, m == MT - 1)
                last.then_inc(SEM[f"{c.n}_m2_ps"], 1)

            def f_proj(c, u, g):
                need(pe, f"{c.n}_OT", nth(LAYERS, c.w, u))
                for t in range(TILES):
                    for k in range(GROUPS):
                        last = mm(c.ps[:, 1 + t, 0:D], tile_cols(c.OT[:, k, :], t), w_proj["ffn"][:, k, :],
                                  k == 0, k == GROUPS - 1)
                    last.then_inc(SEM[f"{c.n}_tok_ps"], 1)

            def f_x2T(c, u, g):
                turn(c, "f2", u)

            def f_logit(c, u, g):
                need(pe, f"{c.n}_scaled", nth(SCALED_X, "f2", u))
                for t in range(TILES):
                    o = c.ps[:, 2, t * EXPERTS:(t + 1) * EXPERTS]
                    for s in range(2):
                        last = mm(o, tile_cols(c.xnT[0:HALF, s, :], t), w_g[:, s, :], s == 0, s == 1)
                last.then_inc(SEM[f"{c.n}_lg_ps"], 1)

            soft_parts = {"xT": xT, "qkv": soft_qkv, "S": S, "T": T, "PV": PV}
            all_turns(pe, {**{(ph, n): part for ph in "af" for n, part in soft_parts.items()},
                ("a", "h0"): a_h0, ("a", "aproj"): a_proj, ("a", "sqkv"): a_sqkv,
                ("a", "sST"): a_sST, ("a", "sPV"): a_sPV, ("a", "so"): a_so, ("a", "soT"): a_soT,
                ("a", "out"): a_out, ("a", "mT"): a_mT, ("a", "m1"): a_m1, ("a", "m2"): a_m2,
                ("f", "fproj"): f_proj, ("f", "x2T"): f_x2T, ("f", "logit"): f_logit,
            })

            pe.wait_ge(SEM["fbcast"], 1)
            for t in range(TILES):
                for s in range(TILES):
                    mm(X.ps[:, t, 0:64], order[:, 3 * s + t, :], R.fb[:, :, s, :, :], s == 0, s == TILES - 1)
            for s in range(TILES):
                last = mm(X.ps[:, 3, 0:64], onesb[:], R.fb[:, :, s, :, :], s == 0, s == TILES - 1)
            last.then_inc(SEM["rank_ps"], 1)

            def turn_rows(u, j):
                n = f"e{j}_"
                need(pe, n + "xb_in", u)
                if j == 1:
                    need(pe, "e0_xbT", u)
                else:
                    need_last(pe, "e1_xbT", u)
                for s in range(2):
                    for t in range(SLOT_TILES):
                        last = pe.transpose(X.ps[0:HALF, s, t * SLOTS:(t + 1) * SLOTS],
                                            xb[j][:, t, s * HALF:(s + 1) * HALF], identf[0:SLOTS, 0:SLOTS])
                    last.then_inc(SEM[n + "xbT_ps"], 1)

            def first_product(u, j):
                n = f"e{j}_"
                need(pe, n + "xbT", u)
                need(pe, n + "fc_in", u)
                for m in range(MT):
                    if m >= 4:
                        need(pe, n + "he", u, m - 3)
                    ps = (X.ps[:, 2 + m % 4, :] if m % 4 < 2 else Y.ps[:, m % 4 - 2, :])
                    halves(ps[:, 0:CAP], lambda s, k: w_fc[j][0:k, s, m * P:(m + 1) * P],
                           lambda s, k: xbT[j][0:k, s, :]).then_inc(SEM[n + "fc_ps"], 1)

            def second_product(u, j):
                n = f"e{j}_"
                need(pe, n + "he", u)
                need(pe, n + "pj_in", u)
                if j == 1:
                    need(pe, "e0_ob", u)
                else:
                    need_last(pe, "e1_ob", u)
                for t in range(SLOT_TILES):
                    if t >= 2:
                        need(pe, n + "ob", u, t - 1)
                    for m in range(MT):
                        last = mm(Y.ps[0:SLOTS, 2 + t % 2, 0:D], heT[:, m, t * SLOTS:(t + 1) * SLOTS],
                                  w_pj[j][:, m, :], m == 0, m == MT - 1)
                    last.then_inc(SEM[n + "pj_ps"], 1)

            def experts(u, more=True):
                first_product(u, 0)
                turn_rows(u, 1)
                second_product(u, 0)
                first_product(u, 1)
                if more:
                    turn_rows(u + 1, 0)
                second_product(u, 1)

            pe.wait_ge(SEM["slots"], 1)
            pe.wait_ge(SEM["xb_ones"], 2)
            turn_rows(0, 0)
            experts(0)
            with pe.Fori(1, EXPERTS // 2 - 1) as u:
                experts(u)
            experts(EXPERTS // 2 - 1, more=False)

        @block.scalar
        def _(act):
            def copy(dst, src):
                return act.activation(dst, src, ACT.Copy)

            def scaled(c, norm, u):
                if isinstance(u, int):
                    act.wait_ge(SEM["ld_const"], LOADED["const"])
                which = AFFINE[norm]
                for s in range(2):
                    need(act, f"{c.n}_turned", nth(TURNED_X, norm, u), s + 1)
                    act.activation(c.xnT[0:HALF, s, :], c.ps[0:HALF, s, 0:COLS], ACT.Identity,
                                   bias=affine[:, which, 1, s:s + 1], scale=affine[:, which, 0, s:s + 1])\
                       .then_inc(SEM[f"{c.n}_scaled"], 1)

            def a_h0(c, u, g):
                need(act, f"{c.n}_h0_ps", u)
                need_last(act, f"{c.n}_hx", u)
                copy(c.h[:, 0, :], c.ps[:, 0, 0:D]).then_inc(SEM[f"{c.n}_h0"], 1)

            def xT(c, u, g):
                if c.phase == 0:
                    need_last(act, f"{c.n}_lg_ps", u)
                scaled(c, c.norm, u)

            def qkv(c, u, g):
                n = c.n
                i = use(c, u)
                need(act, f"{n}_qkv_ps", nth(LAYERS, c.w, u), 2 * g + 1)
                act.activation(c.qT[:, g, :], c.ps[:, 2 * g % 4, 0:COLS], ACT.Copy, scale=SCALE ** 0.5)\
                   .then_inc(SEM[f"{n}_q"], 1)
                need(act, f"{n}_qkv_ps", nth(LAYERS, c.w, u), 2 * g + 2)
                copy(c.V[:, g, :, 0:HD], c.ps[:, (2 * g + 1) % 4, 0:D].rearrange("p (h e) -> p h e", e=HD))\
                    .then_inc(SEM[f"{n}_v"], 1)

            def S(c, u, g):
                n = c.n
                i = use(c, u)
                if isinstance(i, int):
                    act.wait_ge(SEM["zfill"], 160)
                need(act, f"{n}_negm", i, 2 * g + 2)
                if g:
                    need(act, f"{n}_T_ps", i, GH * g)
                    need(act, f"{n}_rr", i, g)
                for b in range(GH):
                    for t in range(TILES):
                        act.activation(c.Pq[:, b, SEG[t]], c.ps[:, b, SEG[t]], ACT.Exp,
                                       bias=c.negm[:, b, t:t + 1], accum_out=c.rsum[:, b, t:t + 1])\
                           .then_inc(SEM[f"{n}_P"], 1)

            def T(c, u, g):
                n = c.n
                i = use(c, u)
                for b in (1, 3):
                    need(act, f"{n}_T_ps", i, GH * g + b + 1)
                    copy(c.PT[:, b, :], c.ps[:, b, :]).then_inc(SEM[f"{n}_PTa"], 1)

            def PV(c, u, g):
                n = c.n
                i = use(c, u)
                need(act, f"{n}_R_ps", i, g + 1)
                if g:
                    need(act, f"{n}_OT", nth(LAYERS, c.w, u), g)
                copy(c.rec[:], c.ps[:, 2, 0:COLS]).then_inc(SEM[f"{n}_R"], 1)

            def a_proj(c, u, g):
                for s in range(2):
                    need(act, f"{c.n}_ao_ps", u, s + 1)
                    act.activation(c.aoT[:, s, :], c.ps[0:HALF, 1 + s, 0:COLS], ACT.Identity,
                                   bias=affine[:, AFFINE["so"], 1, s:s + 1]).then_inc(SEM[f"{c.n}_ao"], 1)

            def a_sqkv(c, u, g):
                need(act, f"{c.n}_qkv_ps", nth(LAYERS, "ssm", u), 2 * g + 1)
                if g == 2:
                    need(act, f"{c.n}_s_phi", u, 1)
                act.activation(c.e_ssm[:, g % 2, :], c.ps[:, 2 * g % 4, 0:COLS], ACT.Exp).then_inc(SEM[f"{c.n}_s_exp"], 1)
                need(act, f"{c.n}_qkv_ps", nth(LAYERS, "ssm", u), 2 * g + 2)
                copy(c.V[:, g, :, 0:HD], c.ps[:, (2 * g + 1) % 4, 0:D].rearrange("p (h e) -> p h e", e=HD))\
                    .then_inc(SEM[f"{c.n}_v"], 1)

            def a_mT(c, u, g):
                scaled(c, "am", u)

            def a_m1(c, u, g):
                for m in range(2 * g, 2 * g + 2):
                    need(act, f"{c.n}_m1_ps", u, m + 1)
                    act.activation(c.gT[:, m, :], c.ps[:, (m + 2) % 4, 0:COLS], ACT.Gelu).then_inc(SEM[f"{c.n}_gelu"], 1)

            def f_x2T(c, u, g):
                scaled(c, "f2", u)

            soft_parts = {"xT": xT, "qkv": qkv, "S": S, "T": T, "PV": PV}
            all_turns(act, {**{(ph, n): part for ph in "af" for n, part in soft_parts.items()},
                ("a", "h0"): a_h0, ("a", "aproj"): a_proj, ("a", "sqkv"): a_sqkv, ("a", "mT"): a_mT,
                ("a", "m1"): a_m1, ("f", "x2T"): f_x2T,
            })
            act.wait_ge(SEM["dm"], 1)
            act.activation(R.ex[:], R.dm[:], ACT.Exp).then_inc(SEM["exp_d"], 1)

            def scaled_rows(u, j):
                n = f"e{j}_"
                for s in range(2):
                    need(act, n + "xbT_ps", u, s + 1)
                    act.activation(xbT[j][0:HALF, s, :], X.ps[0:HALF, s, 0:CAP], ACT.Identity,
                                   bias=affine[:, AFFINE["f2"], 1, s:s + 1], scale=affine[:, AFFINE["f2"], 0, s:s + 1])\
                       .then_inc(SEM[n + "xbT"], 1)

            def hidden(u, j):
                n = f"e{j}_"
                if j == 1:
                    need(act, "e0_pj_ps", u)
                else:
                    need_last(act, "e1_pj_ps", u)
                for m in range(MT):
                    need(act, n + "fc_ps", u, m + 1)
                    ps = (X.ps[:, 2 + m % 4, :] if m % 4 < 2 else Y.ps[:, m % 4 - 2, :])
                    act.activation(heT[:, m, :], ps[:, 0:CAP], ACT.Gelu).then_inc(SEM[n + "he"], 1)

            def experts(u, more=True):
                hidden(u, 0)
                scaled_rows(u, 1)
                hidden(u, 1)
                if more:
                    scaled_rows(u + 1, 0)

            scaled_rows(0, 0)
            experts(0)
            with act.Fori(1, EXPERTS // 2 - 1) as u:
                experts(u)
            experts(EXPERTS // 2 - 1, more=False)

        @block.vector
        def _(dve):
            def ln(name, src):
                def part(c, u, g):
                    if src == "x2":
                        need(dve, f"{c.n}_x2", 2 * u + (name == "f2"))
                    elif src == "tok_ps":
                        need(dve, f"{c.n}_tok_ps", nth(TOKENS_X, "so", u))
                    elif src:
                        need(dve, f"{c.n}_{src}", u)
                    else:
                        need(dve, f"{c.n}_ln_out", norm_use(name, u) - 1)
                    if name == "a0":
                        need(dve, f"{c.n}_txt_in", u)
                    for t in range(TILES):
                        dve.bn_stats(c.st[:, t, :], c.norms[name].src(t)).then_inc(SEM[f"{c.n}_ln_stats"], 1)
                    need(dve, f"{c.n}_ln_stats", norm_use(name, u))
                    dve.memset(c.carrier[:], 0.0)
                    for t in range(TILES):
                        dve.bn_aggr(c.mv[:, t, :], c.st[:, t, :]).then_inc(SEM[f"{c.n}_ln_aggr"], 1)
                return part

            def lnx(name):
                def part(c, u, g):
                    if name == "a1":
                        need_last(dve, f"{c.n}_xh", u)
                    need(dve, f"{c.n}_ln_rstd", norm_use(name, u))
                    for t in range(TILES):
                        dve.tensor_scalar(c.norms[name].dst(t), c.norms[name].src(t), c.mv[:, t, 0:1], c.rs[:, t:t + 1],
                                          ALU.subtract, ALU.mult).then_inc(SEM[f"{c.n}_ln_out"], 1)
                return part

            def k_under_q(c, g):
                dve.memset(c.carrier[:], 0.0)
                dve.stream_shuffle(c.kT[:, g, :], c.qT[:, g, :], list(range(HD, 2 * HD)) * 2)\
                   .then_inc(SEM[f"{c.n}_k"], 1)

            def qkv(c, u, g):
                if g:
                    need(dve, f"{c.n}_k", nth(LAYERS, c.w, u), g)
                need(dve, f"{c.n}_q", use(c, u), g + 1)
                k_under_q(c, g)

            def S(c, u, g):
                n = c.n
                i = use(c, u)
                need(dve, f"{n}_S_ps", nth(LAYERS, c.w, u), g + 1)
                if g:
                    need(dve, f"{n}_P", i, g * GH * TILES)
                dve.tensor_reduce(c.negm[:, :, 0], c.ps[:, :, SEG[0]], AX, ALU.max, negate=True)\
                   .then_inc(SEM[f"{n}_negm"], 1)
                dve.tensor_reduce(c.negm[:, :, 1:3],
                                  c.ps[:, :, P:W_Q].rearrange("p h (t k) -> p h t k", t=2),
                                  AX, ALU.max, negate=True).then_inc(SEM[f"{n}_negm"], 1)

            def T(c, u, g):
                n = c.n
                i = use(c, u)
                need(dve, f"{n}_T_ps", i, GH * g + 1)
                dve.tensor_copy(c.PT[:, 0, :], c.ps[:, 0, :]).then_inc(SEM[f"{n}_PTd"], 1)
                need(dve, f"{n}_P", i, (g + 1) * GH * TILES)
                dve.reciprocal(c.rr[:], c.rsum[:]).then_inc(SEM[f"{n}_rr"], 1)
                need(dve, f"{n}_rr", i, g + 1)
                if g:
                    need(dve, f"{n}_R_ps", i, g)
                dve.tensor_copy(c.recb[:], c.rr[:].rearrange("p h t -> p t h").unsqueeze(3)
                                .to_broadcast([P, TILES, GH, 32])).then_inc(SEM[f"{n}_recb"], 1)
                need(dve, f"{n}_T_ps", i, GH * g + 3)
                dve.tensor_copy(c.PT[:, 2, :], c.ps[:, 2, :]).then_inc(SEM[f"{n}_PTd"], 1)

            def PV(c, u, g):
                n = c.n
                i = use(c, u)
                need(dve, f"{n}_R", i, g + 1)
                need(dve, f"{n}_PV_ps", nth(LAYERS, c.w, u), g + 1)
                halves = "p (s k) -> p s k"
                dve.tensor_tensor(c.OT[:, g, :].rearrange(halves, s=2), c.ps[:, 0:2, 0:SEQ],
                                  c.rec[:].rearrange(halves, s=2), ALU.mult)\
                   .then_inc(SEM[f"{n}_OT"], 1)

            def a_sqkv(c, u, g):
                need(dve, f"{c.n}_s_exp", u, g + 1)
                if g:
                    need(dve, f"{c.n}_s_phi", u, g)
                dve.tensor_scalar(c.r_ssm, c.ps[:, 2 * g % 4, 0:COLS], 0.0, ELU_EPS, ALU.max, ALU.add)\
                   .then_inc(SEM[f"{c.n}_s_relu"], 1)
                need(dve, f"{c.n}_s_relu", u, g + 1)
                dve.scalar_tensor_tensor(out=c.qT[:, g, :], in0=c.e_ssm[:, g % 2, :], scalar=1.0, in1=c.r_ssm,
                                         op0=ALU.min, op1=ALU.add).then_inc(SEM[f"{c.n}_s_phi"], 1)
                need(dve, f"{c.n}_s_phi", u, g + 1)
                k_under_q(c, g)

            def a_sST(c, u, g):
                need(dve, f"{c.n}_S_ps", nth(LAYERS, "ssm", u), g + 1)
                if g:
                    need(dve, f"{c.n}_PV_ps", nth(LAYERS, "ssm", u), g)
                dve.tensor_tensor(c.PT[:, :, 0:W_FULL], c.ps[:, :, 0:W_FULL],
                                  keep01[:].unsqueeze(1).to_broadcast([P, GH, W_FULL]), ALU.mult)\
                   .then_inc(SEM[f"{c.n}_s_PT"], 1)

            def a_sdiv(c, u, g):
                if g == 0:
                    need(dve, f"{c.n}_ao", u)
                need(dve, f"{c.n}_PV_ps", nth(LAYERS, "ssm", u), g + 1)
                dve.memset(c.carrier[:], 0.0)
                rec = c.rec[:].rearrange("p (s k) -> p s k", s=2)
                o = c.ps[:, 0:2, 0:SEQ]
                dve.stream_shuffle(rec, o, [HD] * 32).then_inc(SEM[f"{c.n}_s_div"], 1)
                need(dve, f"{c.n}_s_div", u, 3 * g + 1)
                dve.tensor_scalar(c.rec[:], c.rec[:], 1e-4 / SCALE, None, ALU.add).then_inc(SEM[f"{c.n}_s_div"], 1)
                need(dve, f"{c.n}_s_div", u, 3 * g + 2)
                dve.reciprocal(c.rec[:], c.rec[:]).then_inc(SEM[f"{c.n}_s_div"], 1)
                need(dve, f"{c.n}_s_div", u, 3 * g + 3)
                dve.tensor_tensor(c.OT[:, g, :].rearrange("p (s k) -> p s k", s=2), o, rec, ALU.mult)\
                   .then_inc(SEM[f"{c.n}_OT"], 1)

            def a_soT(c, u, g):
                need(dve, f"{c.n}_ao", u)
                for s in range(2):
                    need(dve, f"{c.n}_turned", nth(TURNED_X, "so", u), s + 1)
                    dve.scalar_tensor_tensor(out=c.xnT[0:HALF, s, :], in0=c.ps[0:HALF, s, 0:COLS],
                                             scalar=affine[:, AFFINE["so"], 0, s:s + 1], in1=c.aoT[:, s, :],
                                             op0=ALU.mult, op1=ALU.add).then_inc(SEM[f"{c.n}_u"], 1)

            def a_out(c, u, g):
                for t in range(TILES):
                    need(dve, f"{c.n}_tok_ps", nth(TOKENS_X, "out", u), t + 1)
                    dve.tensor_tensor(c.x2[:, t, :], c.ps[:, 1 + t, 0:D], c.xln[:, t, :], ALU.add)\
                       .then_inc(SEM[f"{c.n}_x2"], 1)

            def a_m2(c, u, t):
                if t == 0:
                    need(dve, f"{c.n}_hs", u)
                need(dve, f"{c.n}_m2_ps", u, t + 1)
                dve.tensor_tensor(c.h[:, t, :], c.ps[:, t, 0:D], c.h[:, t, :], ALU.add).then_inc(SEM[f"{c.n}_hF"], 1)

            def f_proj(c, u, g):
                for t in range(TILES):
                    need(dve, f"{c.n}_tok_ps", nth(TOKENS_X, "ffn", u), t + 1)
                    dve.tensor_tensor(c.x2[:, t, :], c.ps[:, 1 + t, 0:D], c.xln[:, t, :], ALU.add)\
                       .then_inc(SEM[f"{c.n}_x2"], 1)

            def f_logit(c, u, g):
                need(dve, f"{c.n}_lg_ps", u)
                dve.tensor_copy(logits[:, pair(c, u), :, :], c.ps[:, 2, 0:TILES * EXPERTS]
                                .rearrange("p (t e) -> p t e", t=TILES)).then_inc(SEM[f"{c.n}_lg"], 1)

            dve.wait_ge(ready, FILLS)
            dve.wait_ge(SEM["ld_const"], LOADED["const"])
            soft_parts = {"qkv": qkv, "S": S, "T": T, "PV": PV}
            all_turns(dve, {**{(ph, n): part for ph in "af" for n, part in soft_parts.items()},
                ("a", "ln0"): ln("a0", "h0"), ("a", "ln0x"): lnx("a0"), ("a", "ln1"): ln("a1", None),
                ("a", "ln1x"): lnx("a1"), ("a", "sqkv"): a_sqkv, ("a", "sST"): a_sST, ("a", "sdiv"): a_sdiv,
                ("a", "so"): ln("so", "tok_ps"), ("a", "sox"): lnx("so"), ("a", "soT"): a_soT,
                ("a", "out"): a_out, ("a", "lnm"): ln("am", "x2"), ("a", "lnmx"): lnx("am"), ("a", "m2"): a_m2,
                ("f", "ln0"): ln("f0", "hF"), ("f", "ln0x"): lnx("f0"), ("f", "ln1"): ln("f1", None),
                ("f", "ln1x"): lnx("f1"), ("f", "fproj"): f_proj, ("f", "ln2"): ln("f2", "x2"),
                ("f", "ln2x"): lnx("f2"), ("f", "logit"): f_logit,
            })

            done = [0]

            def link(ins):
                done[0] += 1
                ins.then_inc(SEM["route"], 1)
                dve.wait_ge(SEM["route"], done[0])

            lg = logits[:].rearrange("p a t e -> p (a t) e")
            for c in (X, Y):
                need(dve, f"{c.n}_lg", TURNS - 1)
            src = lg
            desc_b = desc[:].unsqueeze(1).to_broadcast([P, NT, EXPERTS])

            def per_expert(ap):
                return ap.unsqueeze(2).to_broadcast([P, NT, EXPERTS])

            for k in range(2):
                link(dve.tensor_reduce(R.m[:, k, :], src, AX, ALU.max))
                link(dve.tensor_tensor(R.eq[:], src, per_expert(R.m[:, k, :]), ALU.is_equal))
                link(dve.tensor_tensor(R.cand[:], R.eq[:], desc_b, ALU.mult))
                link(dve.tensor_reduce(R.mc[:], R.cand[:], AX, ALU.max))
                link(dve.tensor_tensor(R.first[:, k, :, :], R.cand[:], per_expert(R.mc[:]), ALU.is_equal))
                if k == 0:
                    link(dve.scalar_tensor_tensor(out=R.l2[:], in0=R.first[:, 0, :, :], scalar=-3.0e38, in1=lg,
                                                  op0=ALU.mult, op1=ALU.add))
                    src = R.l2[:]
                else:
                    for kk in range(2):
                        last = dve.tensor_copy(R.fb[:, :, :, kk, :],
                                               R.first[:, kk, :, :].rearrange("p (a t) e -> p a t e", t=TILES))
                        if kk == 0:
                            link(last)
                    last.then_inc(SEM["fbcast"], 1)
            dve.tensor_tensor(R.dm[:], R.m[:, 1, :], R.m[:, 0, :], ALU.subtract).then_inc(SEM["dm"], 1)
            dve.wait_ge(SEM["exp_d"], 1)
            link(dve.tensor_scalar(R.den[:], R.ex[:], 1.0, None, ALU.add))
            link(dve.reciprocal(R.p[:, 0, :], R.den[:]))
            link(dve.tensor_tensor(R.p[:, 1, :], R.ex[:], R.p[:, 0, :], ALU.mult))
            dve.wait_ge(SEM["rank_ps"], 1)
            link(dve.tensor_copy(R.tot[:], X.ps[:, 3, 0:64].rearrange("p (a k e) -> p a k e", a=PAIRS, k=2)))
            link(dve.memset(R.base[:, 0, 0, :], 0.0))
            for p in range(PAIRS):
                link(dve.tensor_tensor(R.base[:, p + 1, 0, :], R.base[:, p, 0, :], R.tot[:, p, 0, :], ALU.add))
            link(dve.tensor_copy(R.base[:, 0, 1, :], R.base[:, PAIRS, 0, :]))
            for p in range(PAIRS - 1):
                link(dve.tensor_tensor(R.base[:, p + 1, 1, :], R.base[:, p, 1, :], R.tot[:, p, 1, :], ALU.add))
            for t in range(TILES):
                link(dve.tensor_tensor(R.rank[:, :, t, :, :],
                                       X.ps[:, t, 0:64].rearrange("p (a k e) -> p a k e", a=PAIRS, k=2),
                                       R.base[:, 0:PAIRS, :, :], ALU.add))
            flat = "p a t k e -> p (a t k) e"
            fl4 = "p a t k -> p (a t k)"
            for k in range(2):
                link(dve.scalar_tensor_tensor(out=R.kept[:, :, :, k, :], in0=R.rank[:, :, :, k, :], scalar=float(CAP),
                                              in1=R.first[:, k, :, :].rearrange("p (a t) e -> p a t e", t=TILES),
                                              op0=ALU.is_lt, op1=ALU.mult))
            link(dve.tensor_tensor(R.slotv[:].rearrange(flat), R.rank[:].rearrange(flat),
                                   ebase[:].unsqueeze(1).to_broadcast([P, 2 * NT, EXPERTS]), ALU.add))
            link(dve.tensor_tensor(R.slotv[:].rearrange(flat), R.slotv[:].rearrange(flat),
                                   R.kept[:].rearrange(flat), ALU.mult))
            link(dve.tensor_reduce(R.slot[:].rearrange(fl4), R.slotv[:].rearrange(flat), AX, ALU.add))
            link(dve.tensor_reduce(R.ks[:].rearrange(fl4), R.kept[:].rearrange(flat), AX, ALU.add))
            for k in range(2):
                link(dve.tensor_tensor(R.wgt[:, :, :, k], R.ks[:, :, :, k],
                                       R.p[:, k, :].rearrange("p (a t) -> p a t", t=TILES), ALU.mult))
            link(dve.tensor_scalar(R.ks[:], R.ks[:], -1.0, 1.0, ALU.mult, ALU.add))
            link(dve.tensor_tensor(R.dumpv[:], R.ks[:], dump_id[:], ALU.mult))
            link(dve.tensor_tensor(R.dumpv[:], R.dumpv[:], R.slot[:], ALU.add))
            link(dve.tensor_copy(R.gidx[:], R.slot[:]))
            dve.tensor_copy(R.sidx[:], R.dumpv[:]).then_inc(SEM["slots"], 1)

            def expert(u, j):
                n = f"e{j}_"
                need(dve, n + "bp_in", u)
                need_last(dve, n + "st", u)
                for t in range(SLOT_TILES):
                    need(dve, n + "pj_ps", u, t + 1)
                    dve.tensor_tensor(ob[j][:, t, :], Y.ps[0:SLOTS, 2 + t % 2, 0:D], b_pj[j][0:SLOTS, :], ALU.add)\
                       .then_inc(SEM[n + "ob"], 1)

            for j in range(2):
                expert(0, j)
            with dve.Fori(1, EXPERTS // 2) as u:
                for j in range(2):
                    expert(u, j)

            for n in range(NT):
                p, t = n // TILES, n % TILES
                dve.wait_ge(gat[n % 4], 32 * (n // 4 + 1))
                dve.scalar_tensor_tensor(out=y_mid[:, n % 2, :], in0=g_rows[:, n % 4, 0, :], scalar=R.wgt[:, p, t, 0:1],
                                         in1=hx_all[:, p, t, :], op0=ALU.mult, op1=ALU.add).then_inc(SEM["ymid"], 1)
                dve.wait_ge(SEM["ymid"], n + 1)
                if n >= 2:
                    dve.wait_ge(ysto[n % 2], stored(n, n % 2))
                dve.scalar_tensor_tensor(out=y_out[:, n % 2, :], in0=g_rows[:, n % 4, 1, :], scalar=R.wgt[:, p, t, 1:2],
                                         in1=y_mid[:, n % 2, :], op0=ALU.mult, op1=ALU.add).then_inc(SEM["yout"], 1)

        @block.gpsimd
        def _(pool):
            fills = [(ones_row[:], 1.0), (onesb[:], 1.0), (neghalf[:], -0.5), (eps[:], EPS)]
            fills += [(c.V[:], 0.0) for c in (X, Y)]
            fills += [(c.V[:, :, :, HD:HD + 1], 1.0) for c in (X, Y)]
            fills += [(c.xnT[HALF:HALF + 1, :, :], 1.0) for c in (X, Y)]
            pool.memset(zrow, 0.0).then_inc(SEM["zero"], 1)
            pool.wait_ge(SEM["zero"], 1)
            assert len(fills) == FILLS
            for n, (buf, value) in enumerate(fills):
                pool.memset(buf, value).then_inc(ready, 1)
                pool.wait_ge(ready, n + 1)

            def rstd(name):
                def part(c, u, g):
                    i = norm_use(name, u)
                    need(pool, f"{c.n}_ln_aggr", i)
                    pool.tensor_tensor(c.ve[:], c.mv[:, :, 1], eps[:], ALU.add).then_inc(SEM[f"{c.n}_ln_rstd"], 1)
                    need(pool, f"{c.n}_ln_rstd", i, 1)
                    pool.tensor_tensor(c.rs[:], c.ve[:], neghalf[:], ALU.pow).then_inc(SEM[f"{c.n}_ln_rstd"], 1)
                return part

            def a_lnm(c, u, g):
                rstd("am")(c, u, g)
                if isinstance(u, int):
                    pool.wait_ge(SEM["ld_mlp"], LOADED["mlp"])
                need(pool, f"{c.n}_x2", 2 * u)
                pool.tensor_tensor(c.h[:], c.x2[:], c.h[:], ALU.add).then_inc(SEM[f"{c.n}_hx2"], 1)
                need(pool, f"{c.n}_hx2", u)
                pool.tensor_tensor(c.h[:], c.h[:], b_m2[:].unsqueeze(1).to_broadcast([P, TILES, D]), ALU.add)\
                    .then_inc(SEM[f"{c.n}_hs"], 1)

            def f_ln2(c, u, g):
                rstd("f2")(c, u, g)
                need(pool, f"{c.n}_x2", 2 * u + 1)
                apart(pool)
                pool.tensor_tensor(hx_all[:, pair(c, u), :, :], c.x2[:], c.h[:], ALU.add).then_inc(SEM[f"{c.n}_hx"], 1)
                need(pool, f"{c.n}_ln_out", norm_use("f2", u))
                apart(pool)
                pool.tensor_copy(xh_all[:, pair(c, u), :, :], c.xhat[:]).then_inc(SEM[f"{c.n}_xh"], 1)

            all_turns(pool, {
                ("a", "ln0"): rstd("a0"), ("a", "ln1"): rstd("a1"), ("a", "so"): rstd("so"), ("a", "lnm"): a_lnm,
                ("f", "ln0"): rstd("f0"), ("f", "ln1"): rstd("f1"), ("f", "ln2"): f_ln2,
            })
            for c in (X, Y):
                need(pool, f"{c.n}_lg", TURNS - 1)
                need(pool, f"{c.n}_xh", TURNS - 1)
            for j in range(2):
                pool.memset(xbT[j][HALF:HALF + 1, :, :], 1.0).then_inc(SEM["xb_ones"], 1)
                pool.wait_ge(SEM["xb_ones"], j + 1)
            pool.wait_ge(SEM["slots"], 1)
            pool.wait_ge(SEM["zfill"], 160)
            for n in range(NT):
                p, t = n // TILES, n % TILES
                for k in range(2):
                    pool.indirect_dma_start(out=xb_dram, out_offset=bass.IndirectOffsetOnAxis(ap=R.sidx[:, p, t, k:k + 1], axis=0),
                                            in_=xh_all[:, p, t, :], in_offset=None).then_inc(scat, 16)
            for j in range(2):
                pool.wait_ge(SEM[f"e{j}_st"], 16 * (EXPERTS // 2))
            for n in range(NT):
                p, t = n // TILES, n % TILES
                if n >= 4:
                    pool.wait_ge(SEM["yout"], n - 3)
                for k in range(2):
                    pool.indirect_dma_start(out=g_rows[:, n % 4, k, :], out_offset=None, in_=ob_dram,
                                            in_offset=bass.IndirectOffsetOnAxis(ap=R.gidx[:, p, t, k:k + 1], axis=0))\
                        .then_inc(gat[n % 4], 16)


def constants(np):
    bf = np.dtype("bfloat16")
    i_txt, j_txt = np.arange(IMG, SEQ), np.arange(IMG, SEQ)
    c = {}
    pos = np.stack([np.concatenate([np.arange(IMG), SEQ + np.arange(IMG)]),
                    IMG + np.arange(TXT), SEQ + IMG + np.arange(TXT)])
    seq = [np.concatenate([i_txt, np.arange(IMG)]), np.arange(SEQ)]
    for kind, off in (("win", -40960.0), ("full", -1e30)):
        def valid(i, j):
            ok = j <= i
            return ok & (j > i - WINDOW) if kind == "win" else ok
        txt_q = IMG + np.arange(P)[:, None]
        m = np.concatenate([valid(pos[0][:, None], pos[0][None]) & (pos[0][:, None] // SEQ == pos[0][None] // SEQ)]
                           + [valid(txt_q, s[None]) for s in seq], 1)
        c["mask_" + kind] = np.where(m, 0.0, off).astype(bf)
    t = j_txt[:, None] <= i_txt[None]
    img_k = np.arange(P)[:, None] % IMG
    c["keep01"] = np.concatenate([img_k <= np.repeat(np.stack(seq), IMG, axis=0), t, t], 1).astype(np.float32)
    c["identf"] = np.eye(P, dtype=np.float32)
    c["identb"] = np.eye(P).astype(bf)
    c["order"] = np.stack([pos[s][:, None] < pos[t][None] for s in range(TILES) for t in range(TILES)], 1).astype(bf)
    c["desc"] = np.tile(np.arange(EXPERTS, 0, -1, dtype=np.float32), (P, 1))
    c["ebase"] = np.tile(CAP * np.arange(EXPERTS, dtype=np.float32), (P, 1))
    n = np.arange(PAIRS * TILES).reshape(PAIRS, TILES)[None, :, :, None] * P + np.arange(P)[:, None, None, None]
    c["dump_id"] = (DUMP + TOKENS * np.arange(2)[None, None, None, :] + n).astype(np.float32)
    return c


def layout(np, x):
    f = {k: np.asarray(v) for k, v in x.items()}
    z = np.zeros
    o = {}
    patches = f["x"].reshape(BATCH, 3, 2 * 4, 16, 8, 16)
    patches = patches.transpose(1, 3, 5, 0, 2, 4).reshape(KT, P, PAIRS, P)
    o["xT"] = patches.transpose(2, 1, 0, 3)
    o["txt"] = f["txt"].reshape(PAIRS, 2, TXT, D).transpose(0, 2, 1, 3)
    o["w_tok"] = f["L0_tok_W"].T.reshape(KT, P, D).transpose(1, 0, 2)
    o["b_tok"] = f["L0_tok_b"].reshape(1, D)

    def biased(w, b):
        r = z((HALF + 1, 2, w.shape[1]), np.float32)
        r[0:HALF] = w.reshape(2, HALF, -1).transpose(1, 0, 2)
        r[HALF, 1] = b
        return r

    for n, key in (("attn", "L0_attn_attn_qkv"), ("ssm", "L0_attn_ssm_qkv"), ("ffn", "L0_ffn_attn_qkv")):
        w, b = f[key + "_w"], f[key + "_b"]
        full = biased(w, b)
        qk = full[:, :, 0:2 * D].reshape(HALF + 1, 2, 2, GROUPS, GH, HD).transpose(0, 1, 3, 4, 2, 5)
        o["wqk_" + n] = qk.reshape(HALF + 1, 2, GROUPS, P)
        o["wv_" + n] = full[:, :, 2 * D:]
    for n, wk, bk in (("attn", "L0_attn_attn_proj_w", "L0_attn_attn_proj_b"), ("ssm", "L0_attn_ssm_out_w", None),
                      ("ffn", "L0_ffn_attn_proj_w", "L0_ffn_attn_proj_b")):
        r = z((GROUPS, GH, 32, D), np.float32)
        r[:, :, 0:HD] = f[wk].reshape(GROUPS, GH, HD, D)
        if bk:
            r[0, 0, HD] = f[bk]
        o["wp_" + n] = r.reshape(GROUPS, P, D).transpose(1, 0, 2)
    o["b_so"] = f["L0_attn_ssm_out_b"].reshape(1, D)
    o["w_out"] = biased(f["L0_attn_out_w"], f["L0_attn_out_b"])
    o["w_m1"] = biased(f["L0_attn_mlp_w1"], f["L0_attn_mlp_b1"])
    o["w_m2"] = f["L0_attn_mlp_w2"].reshape(MT, P, D).transpose(1, 0, 2)
    o["b_m2"] = f["L0_attn_mlp_b2"].reshape(1, D)
    o["w_g"] = f["L0_ffn_w_g"].reshape(2, HALF, EXPERTS).transpose(1, 0, 2)
    norms = (("L0_attn_ln1_g", "L0_attn_ln1_b"), ("L0_attn_ssm_ln_g", "L0_attn_ssm_ln_b"),
             ("L0_attn_lnm_g", "L0_attn_lnm_b"), ("L0_ffn_ln1_w", "L0_ffn_ln1_b"), ("L0_ffn_ln2_w", "L0_ffn_ln2_b"))
    o["affine"] = np.stack([np.stack([f[k].reshape(2, HALF) for k in ab]) for ab in norms]).transpose(3, 0, 1, 2)
    o["e_fc"] = np.stack([biased(f["L0_ffn_exp_fc_w"][e], f["L0_ffn_exp_fc_b"][e, 0]) for e in range(EXPERTS)])
    o["e_pj"] = f["L0_ffn_exp_proj_w"].reshape(EXPERTS, MT, P, D).transpose(0, 2, 1, 3)
    o["e_bpj"] = f["L0_ffn_exp_proj_b"].reshape(EXPERTS, 1, D)
    return o


def kernel(**inputs):
    import numpy as np
    import concourse.bacc as bacc
    from concourse.bass_utils import run_bass_kernel_spmd as run

    nc = bacc.Bacc("TRN2", target_bir_lowering=False, num_devices=1)
    arrays = {k: np.ascontiguousarray(v) for k, v in {**constants(np), **layout(np, inputs)}.items()}
    d = Named({k: nc.dram_tensor(k + "_dram", a.shape, mybir.dt.from_np(a.dtype), kind="ExternalInput").ap()
               for k, a in arrays.items()})
    out = nc.dram_tensor("out_dram", (BATCH, SEQ, D), F32, kind="ExternalOutput").ap()
    build(nc, d, out)
    r = run(nc, [{k + "_dram": a for k, a in arrays.items()}], core_ids=[0])
    return r.results[0]["out_dram"]
```

```python
from contextlib import ExitStack

import concourse.bass as bass
from concourse import mybir

ALU = mybir.AluOpType
ACT = mybir.ActivationFunctionType
F32 = mybir.dt.float32
BF16 = mybir.dt.bfloat16
I32 = mybir.dt.int32
AX = mybir.AxisListType.X

P = 128
D = 192
HALF = 96
HEADS, HD = 12, 16
GROUPS, GH = 3, 4
BATCH, IMG, TXT = 8, 64, 128
SEQ = IMG + TXT
PAIRS, TILES = BATCH // 2, 3
STREAMS = 2
TURNS = PAIRS // STREAMS
COLS = 2 * SEQ
TOKENS = BATCH * SEQ
KT = 768 // P
HID = 4 * D
MT = HID // P
WINDOW = 64
EXPERTS = 8
CAP = 2 * 5 * TOKENS // (4 * EXPERTS)
CAP += CAP % 2
SLOT_TILES = 4
SLOTS = CAP // SLOT_TILES
EPS = 1e-5
SCALE = HD ** -0.5
ELU_EPS = 1e-4
DUMP = EXPERTS * CAP
ROWS = DUMP + 2 * TOKENS
ROW = D + 1
HOME = 1 + 2 * TOKENS
HOME_ROWS = HOME + 2 * CAP
W_FULL = SEQ + TXT + TXT
SEG = (slice(0, P), slice(P, P + SEQ), slice(P + SEQ, P + 2 * SEQ))
W_Q = P + 2 * SEQ
TURNED = (P, 2 * P, 0, 3 * P)
assert W_Q == 512
assert SLOTS <= P and CAP <= 512


class Named(dict):

    def __getattr__(self, name):
        return self[name]


TILE_AT = (P, 0, 2 * P)
IMG_COLS = (slice(TXT, SEQ), slice(SEQ, SEQ + IMG))
TXT_COLS = (slice(0, TXT), slice(SEQ + IMG, COLS))


def tile_cols(ap, t):
    return ap[:, TILE_AT[t]:TILE_AT[t] + P]


def build(nc, d, out):
    ctx = ExitStack()
    with ctx:
        def sb(name, shape, dt=F32):
            return ctx.enter_context(nc.sbuf_tensor(name, shape, dt))

        SEM, PER = {}, {}

        def sem(name, per=1):
            SEM[name] = ctx.enter_context(nc.semaphore(name))
            PER[name] = per
            return SEM[name]

        def need(eng, name, i, k=None):
            eng.wait_ge(SEM[name], i * PER[name] + (PER[name] if k is None else k))

        def need_last(eng, name, i):
            if isinstance(i, int) and i == 0:
                return
            eng.wait_ge(SEM[name], i * PER[name])

        def apart(eng):
            eng.wait_ge(SEM["setup_pool"], FILLS)

        identf = sb("identf", [P, P])
        identb = sb("identb", [P, P], BF16)
        mask = {n: sb(f"mask_{n}", [P, W_Q], BF16) for n in ("win", "full")}
        keep01 = sb("keep01", [P, W_FULL])
        order = sb("order", [P, 9, P], BF16)
        onesb = sb("onesb", [P, P], BF16)
        ones_row = sb("ones_row", [1, P])
        neghalf = sb("neghalf", [P, TILES])
        eps = sb("eps", [P, TILES])
        w_tok = sb("w_tok", [P, KT, D])
        b_tok = sb("b_tok", [1, D])
        w_qk = {n: sb(f"w_qk_{n}", [HALF + 1, 2, GROUPS, P]) for n in ("attn", "ssm", "ffn")}
        w_v = {n: sb(f"w_v_{n}", [HALF + 1, 2, D]) for n in ("attn", "ssm", "ffn")}
        w_proj = {n: sb(f"w_proj_{n}", [P, GROUPS, D]) for n in ("attn", "ssm", "ffn")}
        b_so = sb("b_so", [1, D])
        w_out = sb("w_out", [HALF + 1, 2, D])
        w_m1 = sb("w_m1", [HALF + 1, 2, HID])
        w_m2 = sb("w_m2", [P, MT, D])
        b_m2 = sb("b_m2", [P, D])
        w_g = sb("w_g", [HALF, 2, EXPERTS])
        affine = sb("affine", [HALF, 5, 2, 2])
        AFFINE = {"a1": 0, "so": 1, "am": 2, "f1": 3, "f2": 4}

        def cut(buf, at, a, b):
            return buf[:, at:at + a * b].rearrange("p (a b) -> p a b", a=a)

        SOFT = (("turned", 2), ("scaled", 2), ("S_ps", GROUPS), ("negm", GH * GROUPS),
                ("P", GROUPS * GH * TILES), ("T_ps", GROUPS * GH), ("PTd", GROUPS * GH // 2),
                ("PTa", GROUPS * GH // 2), ("rr", GROUPS), ("recb", GROUPS), ("R_ps", GROUPS), ("R", GROUPS),
                ("PV_ps", GROUPS), ("OT", GROUPS), ("qkv_ps", 2 * GROUPS), ("q", 3), ("k", 3), ("v", 3))
        SINGLE = (("x_in", 16), ("txt_in", 16), ("h0_ps", 1), ("h0", 1), ("ao_ps", 2), ("ao", 2),
                  ("s_exp", 3), ("s_relu", 3), ("s_phi", 3),
                  ("s_PT", 3), ("s_div", 3 * GROUPS),
                  ("tok_ps", 3), ("u", 2), ("x2", 3),
                  ("hx2", 1), ("hs", 1), ("m1_ps", 6), ("gelu", 6),
                  ("m2_ps", 3), ("hF", 3),
                  ("hx", 1), ("xh", 1),
                  ("lg_ps", 1), ("lg", 1))
        LAYERS = ("attn", "ssm", "ffn")
        TURNED_X = ("a1", "so", "am", "f1", "f2")
        SCALED_X = ("a1", "am", "f1", "f2")
        TOKENS_X = ("so", "out", "ffn")
        NORMS = ("a0", "a1", "so", "am", "f0", "f1", "f2")

        def stream(n, index):
            c = Named(n=n, index=index)
            c["ps"] = ctx.enter_context(nc.psum_tensor(f"ps_{n}", [P, 4, 512], F32))
            c["work"] = sb(f"work_{n}", [P, 2 * GROUPS * COLS + GH * W_Q])
            c["qT"] = cut(c.work, 0, GROUPS, COLS)
            c["kT"] = cut(c.work, GROUPS * COLS, GROUPS, COLS)
            c["PT"] = cut(c.work, 2 * GROUPS * COLS, GH, W_Q)
            c["g_work"] = sb(f"g_work_{n}", [P, MT * COLS])
            c["Pq"] = cut(c.g_work, 0, GH, W_Q)
            c["e_ssm"] = cut(c.g_work, 0, 2, COLS)
            c["r_ssm"] = c.g_work[:, 2 * COLS:3 * COLS]
            c["aoT"] = cut(c.g_work[0:HALF, :], 3 * COLS, 2, COLS)
            c["gT"] = cut(c.g_work, 0, MT, COLS)
            for name, shape in (("V", [P, TILES, HEADS, 32]),
                                ("negm", [P, GH, TILES]), ("rsum", [P, GH, TILES]), ("rr", [P, GH, TILES]),
                                ("recb", [P, TILES, GH, 32]), ("rec", [P, COLS]), ("OT", [P, GROUPS, COLS]),
                                ("xln", [P, TILES, D]), ("xhat", [P, TILES, D]),
                                ("xnT", [HALF + 1, 2, COLS]), ("xT_in", [P, KT, P]),
                                ("h", [P, TILES, D]),
                                ("x2", [P, TILES, D]),
                                ("st", [P, TILES, 6]), ("mv", [P, TILES, 2]), ("ve", [P, TILES]), ("rs", [P, TILES]), ("carrier", [P, 1])):
                c[name] = sb(f"{name}_{n}", shape)
            for s, per in SOFT + SINGLE:
                sem(f"{n}_{s}", per)
            for s, per in (("stats", TILES), ("aggr", TILES), ("rstd", 2), ("out", TILES)):
                sem(f"{n}_ln_{s}", per)
            return c

        def norms(c):
            where = {"a0": (lambda t: c.h[:, t, :], lambda t: c.xln[:, t, :]),
                     "a1": (lambda t: c.xln[:, t, :], lambda t: c.xhat[:, t, :]),
                     "so": (lambda t: c.ps[:, 1 + t, 0:D], lambda t: c.xhat[:, t, :]),
                     "am": (lambda t: c.x2[:, t, :], lambda t: c.xhat[:, t, :]),
                     "f0": (lambda t: c.h[:, t, :], lambda t: c.xln[:, t, :]),
                     "f1": (lambda t: c.xln[:, t, :], lambda t: c.xhat[:, t, :]),
                     "f2": (lambda t: c.x2[:, t, :], lambda t: c.xhat[:, t, :])}
            return {name: Named(src=where[name][0], dst=where[name][1]) for name in NORMS}

        X, Y = stream("x", 0), stream("y", 1)
        for c in (X, Y):
            c["norms"] = norms(c)
        phases = {w + ph: Named(c, phase=k, kind=("win", "full")[k], w=("attn", "ffn")[k], norm=("a1", "f1")[k])
                  for w, c in (("x", X), ("y", Y)) for k, ph in enumerate("af")}

        def use(c, u):
            return 2 * u + c.phase

        def nth(uses, which, u):
            return len(uses) * u + uses.index(which)

        def norm_use(name, u):
            return nth(NORMS, name, u)

        def pair(c, u):
            return STREAMS * u + c.index

        hx_all = sb("hx_all", [P, PAIRS, TILES, D])
        xh_all = sb("xh_all", [P, PAIRS, TILES, ROW])
        logits = sb("logits", [P, PAIRS, TILES, EXPERTS])

        FILLS = 10
        ready = sem("setup_pool")
        loads = ["const", "tok", "attn", "ssm", "mlp", "ffn"]
        LOADED = {n: 0 for n in loads}
        for n in loads:
            sem("ld_" + n)

        xb_dram = nc.dram_tensor("xb_rows", [ROWS, ROW], F32, kind="Internal").ap()
        home_dram = nc.dram_tensor("home_rows", [HOME_ROWS, D], F32, kind="Internal").ap()
        FILL_X, FILL_Y = 10, 8
        fill_x, fill_y = EXPERTS * CAP * ROW // P // FILL_X, 2 * TOKENS * D // P // FILL_Y
        zrow = X.g_work[:, 0:max(fill_x, fill_y)]
        ZFILL = 16 * (FILL_X + FILL_Y)
        R = Named()
        NT = PAIRS * TILES
        for name, shape, dt in (("m", [P, 2, NT], F32), ("eq", [P, NT, EXPERTS], F32),
                                ("cand", [P, NT, EXPERTS], F32), ("mc", [P, NT], F32),
                                ("first", [P, 2, NT, EXPERTS], F32), ("l2", [P, NT, EXPERTS], F32),
                                ("fb", [P, PAIRS, TILES, 2, EXPERTS], BF16), ("dm", [P, NT], F32), ("ex", [P, NT], F32),
                                ("den", [P, NT], F32), ("p", [P, 2, NT], F32),
                                ("base", [P, PAIRS + 1, 2, EXPERTS], F32),
                                ("rank", [P, PAIRS, TILES, 2, EXPERTS], F32),
                                ("kept", [P, PAIRS, TILES, 2, EXPERTS], F32),
                                ("slotv", [P, PAIRS, TILES, 2, EXPERTS], F32),
                                ("ks", [P, PAIRS, TILES, 2], F32), ("slot", [P, PAIRS, TILES, 2], F32),
                                ("dumpv", [P, PAIRS, TILES, 2], F32),
                                ("wgt", [P, PAIRS, TILES, 2], F32),
                                ("sidx", [P, PAIRS, TILES, 2], I32)):
            R[name] = sb("r_" + name, shape, dt)
        desc = sb("desc", [P, EXPERTS])
        ebase = sb("ebase", [P, EXPERTS])
        dump_id = sb("dump_id", [P, PAIRS, TILES, 2])
        empty_id = sb("empty_id", [P, 2, SLOT_TILES])
        home_id = sb("home_id", [P, PAIRS, TILES])
        w_fc = [sb("w_fc0", [HALF + 1, 2, HID]), w_m1]
        w_pj = [w_m2, w_tok]
        b_pj = [sb(f"b_pj{j}", [P, D]) for j in range(2)]
        xbT = [cut(Y.g_work[0:HALF + 1, :], j * 2 * CAP, 2, CAP) for j in range(2)]
        heT = cut(X.work, 0, MT, CAP)
        xb = [cut(Y.work[0:SLOTS, :], j * SLOT_TILES * ROW, SLOT_TILES, ROW) for j in range(2)]
        ob = [cut(Y.work[0:SLOTS, :], SLOT_TILES * (2 * ROW + j * D), SLOT_TILES, D) for j in range(2)]
        pool_carrier = sb("pool_carrier", [P, 2 * SLOT_TILES])
        home_f = [sb(f"home_f{j}", [SLOTS, SLOT_TILES]) for j in range(2)]
        home = [sb(f"home{j}", [SLOTS, SLOT_TILES], I32) for j in range(2)]
        g_rows = [(X, Y)[p // 2].work[:, (p % 2) * TILES * 2 * D:(p % 2 + 1) * TILES * 2 * D]
                  .rearrange("p (t k n) -> p t k n", t=TILES, k=2) for p in range(PAIRS)]
        y_out = cut(X.g_work, 0, NT, D)
        for s in ("xb_ones", "route", "dm", "exp_d", "rank_ps", "slots", "zero", "zfill", "fbcast", "ids"):
            sem(s)
        for j in range(2):
            for s, per in (("fc_in", 16), ("pj_in", 16), ("xb_in", 16), ("xbT_ps", 2), ("xbT", 2),
                           ("bp_in", 16), ("fc_ps", 6), ("he", 6), ("pj_ps", 4), ("ob", 4), ("home", 3), ("carried", SLOT_TILES), ("st", 16 * SLOT_TILES)):
                sem(f"e{j}_{s}", per)
        scat = [sem(f"scattered{j}", 16) for j in range(2)]
        gat = [sem(f"gathered{j}") for j in range(PAIRS)]
        sem("ymid")
        sem("yout")
        sem("ystored")

        def times(names, n):
            return [(name, g) for g in range(n) for name in names]

        def named(ph, some):
            return [(ph, *x) for x in some]

        soft = times(("S", "S1", "S2", "T", "T1", "PV", "PV1"), GROUPS)
        turn_steps = (
            named("a", times(("h0", "ln0", "ln0x", "ln1", "ln1x", "xT"), 1) + times(("qkv",), 3) + soft
                  + times(("aproj",), 1) + times(("sqkv",), 3) + times(("sST", "sST1", "sPV", "sdiv"), GROUPS)
                  + times(("so", "sox", "soT", "out", "lnm", "lnmx", "mT"), 1) + times(("m1",), 3) + times(("m2",), 3))
            + named("f", times(("ln0", "ln0x", "ln1", "ln1x", "xT"), 1) + times(("qkv",), 3) + soft
                    + times(("fproj", "ln2", "ln2x", "x2T", "logit"), 1)))
        WOVEN = ("yyxyyyxyxxyxyyxyxyyxxyyxxyyyxyyxxyyxxyxxyxyyyxxyyxxyyxyxyyyxyy"
                 "xxyxxxyxyxyxyyxxyxxyxxyyxxyyxxyxxyyyxxyyxxyxxyxyyyyxxxyyyyxxxx"
                 "xyxyyxyxyxxxyxxxyxxyxxyxyxyxyyxxyyxyyyxyxyxxyyxxxyxxyxxyyxyxyy")
        assert WOVEN.count("x") == len(turn_steps) and WOVEN.count("y") == len(turn_steps)

        def steps(parts, u):
            at = {w: iter(turn_steps) for w in "xy"}
            for w in WOVEN:
                ph, name, g = next(at[w])
                if (ph, name) in parts:
                    parts[ph, name](phases[w + ph], u, g)

        def all_turns(eng, parts):
            steps(parts, 0)
            with eng.Fori(1, TURNS) as u:
                steps(parts, u)

        block = ctx.enter_context(nc.Block())

        @block.sync
        def _(sp):
            def load(n, dst, src):
                LOADED[n] += 16
                sp.dma_start(dst, src).then_inc(SEM["ld_" + n], 16)

            def tokens_in(u):
                for c in (X, Y):
                    need_last(sp, f"{c.n}_h0_ps", u)
                    sp.dma_start(c.xT_in[:], d.xT[pair(c, u)]).then_inc(SEM[f"{c.n}_x_in"], 16)
                for c in (X, Y):
                    need_last(sp, f"{c.n}_hx", u)
                    sp.dma_start(c.h[:, 1:3, :], d.txt[pair(c, u)]).then_inc(SEM[f"{c.n}_txt_in"], 16)

            load("tok", w_tok[:], d.w_tok)
            load("tok", b_tok[:], d.b_tok)
            tokens_in(0)
            load("const", identf[:], d.identf)
            load("const", identb[:], d.identb)
            load("const", affine[:], d.affine)
            for n in ("win", "full"):
                load("const", mask[n][:], d["mask_" + n])
            load("const", keep01[:], d.keep01)
            load("const", order[:], d.order)
            load("const", desc[:], d.desc)
            load("const", ebase[:], d.ebase)
            load("const", dump_id[:], d.dump_id)
            load("const", home_id[:], d.home_id)
            load("const", empty_id[:], d.empty_id)
            load("attn", w_qk["attn"][:], d.wqk_attn)
            load("attn", w_v["attn"][:], d.wv_attn)
            load("attn", w_proj["attn"][:], d.wp_attn)
            load("ssm", w_qk["ssm"][:], d.wqk_ssm)
            load("ssm", w_v["ssm"][:], d.wv_ssm)
            load("ssm", w_proj["ssm"][:], d.wp_ssm)
            load("ssm", b_so[:], d.b_so)
            load("ssm", w_out[:], d.w_out)
            load("mlp", w_m1[:], d.w_m1)
            load("mlp", w_m2[:], d.w_m2)
            load("mlp", b_m2[:], d.b_m2.to_broadcast([P, D]))
            load("ffn", w_qk["ffn"][:], d.wqk_ffn)
            load("ffn", w_v["ffn"][:], d.wv_ffn)
            load("ffn", w_proj["ffn"][:], d.wp_ffn)
            load("ffn", w_g[:], d.w_g)
            sp.wait_ge(SEM["zero"], 1)
            zr = xb_dram[0:EXPERTS * CAP, :].rearrange("(k p r) n -> k p (r n)", p=P, k=FILL_X)
            zy = home_dram[1:HOME, :].rearrange("(k p r) n -> k p (r n)", p=P, k=FILL_Y)
            for k in range(FILL_X):
                sp.dma_start(zr[k], zrow[:, 0:fill_x]).then_inc(SEM["zfill"], 16)
            for k in range(FILL_Y):
                sp.dma_start(zy[k], zrow[:, 0:fill_y]).then_inc(SEM["zfill"], 16)

            for u in range(1, TURNS):
                tokens_in(u)

            def expert_in(u, j):
                need_last(sp, f"e{j}_fc_ps", u)
                sp.dma_start(w_fc[j][:], d.e_fc[2 * u + j]).then_inc(SEM[f"e{j}_fc_in"], 16)
                need_last(sp, f"e{j}_pj_ps", u)
                sp.dma_start(w_pj[j][:], d.e_pj[2 * u + j]).then_inc(SEM[f"e{j}_pj_in"], 16)
                need_last(sp, f"e{j}_ob", u)
                sp.dma_start(b_pj[j][:], d.e_bpj[2 * u + j].to_broadcast([P, D])).then_inc(SEM[f"e{j}_bp_in"], 16)

            def rows_in(u, j):
                need_last(sp, f"e{j}_xbT_ps", u)
                rows = xb_dram[0:EXPERTS * CAP, :].rearrange("(e t s) n -> e s t n", e=EXPERTS, s=SLOTS)
                sp.dma_start(xb[j], rows[2 * u + j]).then_inc(SEM[f"e{j}_xb_in"], 16)

            for c in (X, Y):
                for n in ("m1_ps", "m2_ps"):
                    need(sp, f"{c.n}_{n}", TURNS - 1)
            expert_in(0, 0)
            expert_in(0, 1)
            for j in range(2):
                sp.wait_ge(scat[j], 16 * NT)
            rows_in(0, 0)
            rows_in(0, 1)
            with sp.Fori(0, EXPERTS // 2 - 1) as u:
                for j in range(2):
                    expert_in(u + 1, j)
                    rows_in(u + 1, j)
            homes = home_dram[1:HOME, :].rearrange("(a t p k) d -> a p t k d", a=PAIRS, t=TILES, p=P)
            for j in range(2):
                need(sp, f"e{j}_st", EXPERTS // 2 - 1)
            for p in range(PAIRS):
                sp.dma_start(g_rows[p], homes[p]).then_inc(gat[p], 16)
            for p in range(PAIRS):
                sp.wait_ge(SEM["yout"], TILES * p + 1)
                for b in range(2):
                    sp.dma_start(out[2 * p + b, 0:IMG, :], y_out[b * IMG:(b + 1) * IMG, TILES * p, :]).then_inc(SEM["ystored"], 16)
                sp.wait_ge(SEM["yout"], TILES * (p + 1))
                sp.dma_start(out[2 * p:2 * p + 2, IMG:SEQ, :].rearrange("b s d -> s b d"),
                             y_out[:, TILES * p + 1:TILES * (p + 1), :]).then_inc(SEM["ystored"], 16)
            sp.wait_ge(SEM["ystored"], 16 * 3 * PAIRS)

        @block.tensor
        def _(pe):
            def mm(out_, lhsT, rhs, start=True, stop=True, skip=False):
                return pe.matmul(out_, lhsT, rhs, start=start, stop=stop, skip_group_check=skip)

            def wait_loads(*names):
                for n in names:
                    pe.wait_ge(SEM["ld_" + n], LOADED[n])

            def turn(c, norm, u):
                for s in range(2):
                    for t in range(TILES):
                        need(pe, f"{c.n}_ln_out", norm_use(norm, u), t + 1)
                        last = pe.transpose(tile_cols(c.ps[0:HALF, s, 0:COLS], t), c.xhat[:, t, s * HALF:(s + 1) * HALF],
                                            identf[:])
                    last.then_inc(SEM[f"{c.n}_turned"], 1)

            def halves(out_, w, xT, stop=True):
                mm(out_, w(0, HALF), xT(0, HALF), True, False)
                return mm(out_, w(1, HALF + 1), xT(1, HALF + 1), False, stop)

            def a_h0(c, u, g):
                if isinstance(u, int):
                    wait_loads("tok")
                    pe.wait_ge(ready, FILLS)
                need(pe, f"{c.n}_x_in", u)
                need_last(pe, f"{c.n}_lg", u)
                for k in range(KT):
                    mm(c.ps[:, 0, 0:D], c.xT_in[:, k, :], w_tok[:, k, :], k == 0, False)
                mm(c.ps[:, 0, 0:D], ones_row[:], b_tok[:], False, True).then_inc(SEM[f"{c.n}_h0_ps"], 1)

            def xT(c, u, g):
                if c.phase == 0:
                    if isinstance(u, int):
                        wait_loads("const")
                    need(pe, f"{c.n}_h0", u)
                turn(c, c.norm, u)

            def qkv(c, w, free, u, g):
                if g == 0 and isinstance(u, int):
                    wait_loads(w)
                free(2 * g)
                halves(c.ps[:, 2 * g % 4, 0:COLS], lambda s, k: w_qk[w][0:k, s, g, :],
                       lambda s, k: c.xnT[0:k, s, :]).then_inc(SEM[f"{c.n}_qkv_ps"], 1)
                free(2 * g + 1)
                halves(c.ps[:, (2 * g + 1) % 4, 0:D], lambda s, k: tile_cols(c.xnT[0:k, s, :], g),
                       lambda s, k: w_v[w][0:k, s, :]).then_inc(SEM[f"{c.n}_qkv_ps"], 1)

            def soft_qkv(c, u, g):
                i = use(c, u)
                def free(n):
                    if n == 4:
                        need(pe, f"{c.n}_q", i, 1)
                    if n == 5:
                        need(pe, f"{c.n}_v", nth(LAYERS, c.w, u), 1)
                if g == 0:
                    need(pe, f"{c.n}_scaled", nth(SCALED_X, c.norm, u))
                qkv(c, c.w, free, u, g)

            def a_sqkv(c, u, g):
                def free(n):
                    if n == 1 or n == 2:
                        need(pe, f"{c.n}_ao", u)
                    if n == 4:
                        need(pe, f"{c.n}_s_relu", u, 1)
                    if n == 5:
                        need(pe, f"{c.n}_v", nth(LAYERS, "ssm", u), 1)
                qkv(c, "ssm", free, u, g)

            def S(c, u, g):
                n = c.n
                i = use(c, u)
                if g == 0:
                    need(pe, f"{n}_q", i)
                    need(pe, f"{n}_k", nth(LAYERS, c.w, u))
                    need(pe, f"{n}_v", nth(LAYERS, c.w, u))
                else:
                    need(pe, f"{n}_OT", nth(LAYERS, c.w, u), g)
                for b in range(GH):
                    mm(c.ps[:, b, :], identb[:], mask[c.kind][:], True, True)
                scores(c, g, 0)

            def scores(c, g, t):
                keys = (slice(TXT, TXT + P), slice(0, SEQ), slice(SEQ, COLS))[t]
                for b in range(GH):
                    r = slice(32 * b, 32 * b + HD)
                    last = mm(c.ps[:, b, SEG[t]], tile_cols(c.qT[r, g, :], t), c.kT[r, g, keys], False, True, True)
                return last

            def S1(c, u, g):
                scores(c, g, 1)

            def S2(c, u, g):
                scores(c, g, 2).then_inc(SEM[f"{c.n}_S_ps"], 1)

            def T(c, u, g):
                turn_weights(c, u, g, (0, 1))

            def T1(c, u, g):
                turn_weights(c, u, g, (2, 3))

            def turn_weights(c, u, g, heads):
                n = c.n
                i = use(c, u)
                for b in heads:
                    need(pe, f"{n}_P", i, (GH * g + b + 1) * TILES)
                    for m, at in enumerate(TURNED):
                        last = pe.transpose(c.ps[:, b, m * P:(m + 1) * P], c.Pq[:, b, at:at + P], identf[:])
                    last.then_inc(SEM[f"{n}_T_ps"], 1)

            HEAD_ROWS = [slice(32 * b, 32 * b + HD) for b in range(GH)]

            def values(c, g, w, heads):
                for b in heads:
                    for s in range(2):
                        for m, (o, rows, tile, cols) in enumerate(w[s]):
                            last = mm(c.ps[32 * b:32 * b + 32, s, o], c.V[rows, tile, GH * g + b, :],
                                      c.PT[rows, b, cols], m == 0, True, True)
                return last

            ALL, LOW, HIGH = slice(0, P), slice(0, IMG), slice(IMG, P)
            TXT_0, TXT_1, IMG_1 = slice(0, TXT), slice(IMG, SEQ), slice(0, IMG)
            soft_values = (((TXT_0, ALL, 1, slice(0, P)), (slice(0, SEQ), LOW, 0, slice(P, P + SEQ))),
                           ((TXT_1, ALL, 2, slice(3 * P, 4 * P)), (TXT_1, HIGH, 0, slice(P, 2 * P)),
                            (IMG_1, HIGH, 0, slice(P + SEQ, 3 * P))))
            ssm_values = (((TXT_0, ALL, 1, slice(SEQ, SEQ + P)), (slice(0, SEQ), LOW, 0, slice(0, SEQ))),
                          ((TXT_1, ALL, 2, slice(SEQ + P, SEQ + 2 * P)), (slice(0, SEQ), HIGH, 0, slice(0, SEQ))))

            def PV(c, u, g):
                n = c.n
                i = use(c, u)
                need(pe, f"{n}_PTd", i, 2 * g + 2)
                need(pe, f"{n}_PTa", i, 2 * g + 2)
                need(pe, f"{n}_recb", i, g + 1)
                for t in range(TILES):
                    last = pe.transpose(tile_cols(c.ps[:, 2, 0:COLS], t),
                                        c.recb[:, t, :, :].rearrange("p h e -> p (h e)"), identf[:])
                last.then_inc(SEM[f"{n}_R_ps"], 1)
                values(c, g, soft_values, (0, 1))

            def PV1(c, u, g):
                values(c, g, soft_values, (2, 3)).then_inc(SEM[f"{c.n}_PV_ps"], 1)

            def a_proj(c, u, g):
                need(pe, f"{c.n}_OT", nth(LAYERS, c.w, u))
                for s in range(2):
                    for k in range(GROUPS):
                        last = mm(c.ps[0:HALF, 1 + s, 0:COLS], w_proj["attn"][:, k, s * HALF:(s + 1) * HALF],
                                  c.OT[:, k, :], k == 0, k == GROUPS - 1)
                    last.then_inc(SEM[f"{c.n}_ao_ps"], 1)

            def a_sST(c, u, g):
                if g == 0:
                    need(pe, f"{c.n}_s_phi", u)
                    need(pe, f"{c.n}_k", nth(LAYERS, "ssm", u))
                    need(pe, f"{c.n}_v", nth(LAYERS, "ssm", u))
                else:
                    need(pe, f"{c.n}_OT", nth(LAYERS, "ssm", u), g)
                for s in range(2):
                    for b, r in enumerate(HEAD_ROWS):
                        mm(c.ps[IMG * s:IMG * (s + 1), b, 0:SEQ], c.kT[r, g, IMG_COLS[s]],
                           c.qT[r, g, s * SEQ:(s + 1) * SEQ], True, True, True)

            def a_sST1(c, u, g):
                for s in range(2):
                    for b, r in enumerate(HEAD_ROWS):
                        last = mm(c.ps[:, b, SEQ + s * TXT:SEQ + (s + 1) * TXT], c.kT[r, g, TXT_COLS[s]],
                                  c.qT[r, g, TXT_COLS[s]], True, True, True)
                last.then_inc(SEM[f"{c.n}_S_ps"], 1)

            def a_sPV(c, u, g):
                need(pe, f"{c.n}_s_PT", u, g + 1)
                values(c, g, ssm_values, range(GH)).then_inc(SEM[f"{c.n}_PV_ps"], 1)

            def a_so(c, u, g):
                need(pe, f"{c.n}_OT", nth(LAYERS, "ssm", u))
                for t in range(TILES):
                    for k in range(GROUPS):
                        mm(c.ps[:, 1 + t, 0:D], tile_cols(c.OT[:, k, :], t), w_proj["ssm"][:, k, :], k == 0, False)
                    mm(c.ps[:, 1 + t, 0:D], ones_row[:], b_so[:], False, True).then_inc(SEM[f"{c.n}_tok_ps"], 1)

            def a_soT(c, u, g):
                need(pe, f"{c.n}_ln_out", norm_use("so", u))
                turn(c, "so", u)

            def a_out(c, u, g):
                need(pe, f"{c.n}_u", u)
                for t in range(TILES):
                    halves(c.ps[:, 1 + t, 0:D], lambda s, k: tile_cols(c.xnT[0:k, s, :], t),
                           lambda s, k: w_out[0:k, s, :]).then_inc(SEM[f"{c.n}_tok_ps"], 1)

            def a_mT(c, u, g):
                if isinstance(u, int):
                    wait_loads("mlp")
                turn(c, "am", u)

            def a_m1(c, u, g):
                need(pe, f"{c.n}_scaled", nth(SCALED_X, "am", u))
                for m in range(2 * g, 2 * g + 2):
                    if m >= 4:
                        need(pe, f"{c.n}_gelu", u, m - 3)
                    halves(c.ps[:, (m + 2) % 4, 0:COLS], lambda s, k: w_m1[0:k, s, m * P:(m + 1) * P],
                           lambda s, k: c.xnT[0:k, s, :]).then_inc(SEM[f"{c.n}_m1_ps"], 1)

            def a_m2(c, u, t):
                need(pe, f"{c.n}_gelu", u)
                for m in range(MT):
                    last = mm(c.ps[:, t, 0:D], tile_cols(c.gT[:, m, :], t), w_m2[:, m, :], m == 0, m == MT - 1)
                last.then_inc(SEM[f"{c.n}_m2_ps"], 1)

            def f_proj(c, u, g):
                need(pe, f"{c.n}_OT", nth(LAYERS, c.w, u))
                for t in range(TILES):
                    for k in range(GROUPS):
                        last = mm(c.ps[:, 1 + t, 0:D], tile_cols(c.OT[:, k, :], t), w_proj["ffn"][:, k, :],
                                  k == 0, k == GROUPS - 1)
                    last.then_inc(SEM[f"{c.n}_tok_ps"], 1)

            def f_x2T(c, u, g):
                turn(c, "f2", u)

            def f_logit(c, u, g):
                need(pe, f"{c.n}_scaled", nth(SCALED_X, "f2", u))
                for t in range(TILES):
                    o = c.ps[:, 2, t * EXPERTS:(t + 1) * EXPERTS]
                    for s in range(2):
                        last = mm(o, tile_cols(c.xnT[0:HALF, s, :], t), w_g[:, s, :], s == 0, s == 1)
                last.then_inc(SEM[f"{c.n}_lg_ps"], 1)

            soft_parts = {"xT": xT, "qkv": soft_qkv, "S": S, "S1": S1, "S2": S2, "T": T, "T1": T1,
                          "PV": PV, "PV1": PV1}
            all_turns(pe, {**{(ph, n): part for ph in "af" for n, part in soft_parts.items()},
                ("a", "h0"): a_h0, ("a", "aproj"): a_proj, ("a", "sqkv"): a_sqkv,
                ("a", "sST"): a_sST, ("a", "sST1"): a_sST1, ("a", "sPV"): a_sPV, ("a", "so"): a_so, ("a", "soT"): a_soT,
                ("a", "out"): a_out, ("a", "mT"): a_mT, ("a", "m1"): a_m1, ("a", "m2"): a_m2,
                ("f", "fproj"): f_proj, ("f", "x2T"): f_x2T, ("f", "logit"): f_logit,
            })

            for k, ps in enumerate((X.ps, Y.ps)):
                pe.wait_ge(SEM["fbcast"], k + 1)
                for t in range(TILES):
                    for s in range(TILES):
                        mm(ps[:, t, 0:PAIRS * EXPERTS], order[:, 3 * s + t, :], R.fb[:, :, s, k, :],
                           s == 0, s == TILES - 1)
                for s in range(TILES):
                    last = mm(ps[:, 3, 0:PAIRS * EXPERTS], onesb[:], R.fb[:, :, s, k, :], s == 0, s == TILES - 1)
                last.then_inc(SEM["rank_ps"], 1)

            def turn_rows(u, j):
                n = f"e{j}_"
                need(pe, n + "xb_in", u)
                if j == 1:
                    need(pe, "e0_xbT", u)
                else:
                    need_last(pe, "e1_xbT", u)
                for s in range(2):
                    for t in range(SLOT_TILES):
                        last = pe.transpose(X.ps[0:HALF, s, t * SLOTS:(t + 1) * SLOTS],
                                            xb[j][:, t, s * HALF:(s + 1) * HALF], identf[0:SLOTS, 0:SLOTS])
                    last.then_inc(SEM[n + "xbT_ps"], 1)

            def first_product(u, j):
                n = f"e{j}_"
                need(pe, n + "xbT", u)
                need(pe, n + "fc_in", u)
                for m in range(MT):
                    if m >= 4:
                        need(pe, n + "he", u, m - 3)
                    ps = (X.ps[:, 2 + m % 4, :] if m % 4 < 2 else Y.ps[:, m % 4 - 2, :])
                    halves(ps[:, 0:CAP], lambda s, k: w_fc[j][0:k, s, m * P:(m + 1) * P],
                           lambda s, k: xbT[j][0:k, s, :]).then_inc(SEM[n + "fc_ps"], 1)

            def second_product(u, j):
                n = f"e{j}_"
                need(pe, n + "he", u)
                need(pe, n + "pj_in", u)
                if j == 1:
                    need(pe, "e0_ob", u)
                else:
                    need_last(pe, "e1_ob", u)
                for t in range(SLOT_TILES):
                    if t >= 2:
                        need(pe, n + "ob", u, t - 1)
                    for m in range(MT):
                        last = mm(Y.ps[0:SLOTS, 2 + t % 2, 0:D], heT[:, m, t * SLOTS:(t + 1) * SLOTS],
                                  w_pj[j][:, m, :], m == 0, m == MT - 1)
                    last.then_inc(SEM[n + "pj_ps"], 1)

            def experts(u, more=True):
                first_product(u, 0)
                turn_rows(u, 1)
                second_product(u, 0)
                first_product(u, 1)
                if more:
                    turn_rows(u + 1, 0)
                second_product(u, 1)

            pe.wait_ge(SEM["slots"], 2)
            pe.wait_ge(SEM["xb_ones"], 2)
            turn_rows(0, 0)
            experts(0)
            with pe.Fori(1, EXPERTS // 2 - 1) as u:
                experts(u)
            experts(EXPERTS // 2 - 1, more=False)

        @block.scalar
        def _(act):
            def copy(dst, src):
                return act.activation(dst, src, ACT.Copy)

            def scaled(c, norm, u):
                if isinstance(u, int):
                    act.wait_ge(SEM["ld_const"], LOADED["const"])
                which = AFFINE[norm]
                for s in range(2):
                    need(act, f"{c.n}_turned", nth(TURNED_X, norm, u), s + 1)
                    act.activation(c.xnT[0:HALF, s, :], c.ps[0:HALF, s, 0:COLS], ACT.Identity,
                                   bias=affine[:, which, 1, s:s + 1], scale=affine[:, which, 0, s:s + 1])\
                       .then_inc(SEM[f"{c.n}_scaled"], 1)

            def a_h0(c, u, g):
                need(act, f"{c.n}_h0_ps", u)
                need_last(act, f"{c.n}_hx", u)
                copy(c.h[:, 0, :], c.ps[:, 0, 0:D]).then_inc(SEM[f"{c.n}_h0"], 1)

            def xT(c, u, g):
                if c.phase == 0:
                    need_last(act, f"{c.n}_lg_ps", u)
                scaled(c, c.norm, u)

            def qkv(c, u, g):
                n = c.n
                i = use(c, u)
                need(act, f"{n}_qkv_ps", nth(LAYERS, c.w, u), 2 * g + 1)
                act.activation(c.qT[:, g, :], c.ps[:, 2 * g % 4, 0:COLS], ACT.Copy, scale=SCALE ** 0.5)\
                   .then_inc(SEM[f"{n}_q"], 1)
                need(act, f"{n}_qkv_ps", nth(LAYERS, c.w, u), 2 * g + 2)
                copy(c.V[:, g, :, 0:HD], c.ps[:, (2 * g + 1) % 4, 0:D].rearrange("p (h e) -> p h e", e=HD))\
                    .then_inc(SEM[f"{n}_v"], 1)

            def S(c, u, g):
                n = c.n
                i = use(c, u)
                if isinstance(i, int):
                    act.wait_ge(SEM["zfill"], ZFILL)
                if g:
                    need(act, f"{n}_T_ps", i, GH * g)
                    need(act, f"{n}_rr", i, g)
                for b in range(GH):
                    if b % 2 == 0:
                        need(act, f"{n}_negm", i, GH * g + b + 2)
                    for t in range(TILES):
                        act.activation(c.Pq[:, b, SEG[t]], c.ps[:, b, SEG[t]], ACT.Exp,
                                       bias=c.negm[:, b, t:t + 1], accum_out=c.rsum[:, b, t:t + 1])\
                           .then_inc(SEM[f"{n}_P"], 1)

            def T(c, u, g):
                n = c.n
                i = use(c, u)
                need(act, f"{n}_T_ps", i, GH * g + 2)
                copy(c.PT[:, 1, :], c.ps[:, 1, :]).then_inc(SEM[f"{n}_PTa"], 1)

            def T1(c, u, g):
                need(act, f"{c.n}_T_ps", use(c, u), GH * g + 4)
                copy(c.PT[:, 3, :], c.ps[:, 3, :]).then_inc(SEM[f"{c.n}_PTa"], 1)

            def PV(c, u, g):
                n = c.n
                i = use(c, u)
                need(act, f"{n}_R_ps", i, g + 1)
                if g:
                    need(act, f"{n}_OT", nth(LAYERS, c.w, u), g)
                copy(c.rec[:], c.ps[:, 2, 0:COLS]).then_inc(SEM[f"{n}_R"], 1)

            def a_proj(c, u, g):
                for s in range(2):
                    need(act, f"{c.n}_ao_ps", u, s + 1)
                    act.activation(c.aoT[:, s, :], c.ps[0:HALF, 1 + s, 0:COLS], ACT.Identity,
                                   bias=affine[:, AFFINE["so"], 1, s:s + 1]).then_inc(SEM[f"{c.n}_ao"], 1)

            def a_sqkv(c, u, g):
                need(act, f"{c.n}_qkv_ps", nth(LAYERS, "ssm", u), 2 * g + 1)
                if g == 2:
                    need(act, f"{c.n}_s_phi", u, 1)
                act.activation(c.e_ssm[:, g % 2, :], c.ps[:, 2 * g % 4, 0:COLS], ACT.Exp).then_inc(SEM[f"{c.n}_s_exp"], 1)
                need(act, f"{c.n}_qkv_ps", nth(LAYERS, "ssm", u), 2 * g + 2)
                copy(c.V[:, g, :, 0:HD], c.ps[:, (2 * g + 1) % 4, 0:D].rearrange("p (h e) -> p h e", e=HD))\
                    .then_inc(SEM[f"{c.n}_v"], 1)

            def a_mT(c, u, g):
                scaled(c, "am", u)

            def a_m1(c, u, g):
                for m in range(2 * g, 2 * g + 2):
                    need(act, f"{c.n}_m1_ps", u, m + 1)
                    act.activation(c.gT[:, m, :], c.ps[:, (m + 2) % 4, 0:COLS], ACT.Gelu).then_inc(SEM[f"{c.n}_gelu"], 1)

            def f_x2T(c, u, g):
                scaled(c, "f2", u)

            soft_parts = {"xT": xT, "qkv": qkv, "S2": S, "T": T, "T1": T1, "PV": PV}
            all_turns(act, {**{(ph, n): part for ph in "af" for n, part in soft_parts.items()},
                ("a", "h0"): a_h0, ("a", "aproj"): a_proj, ("a", "sqkv"): a_sqkv, ("a", "mT"): a_mT,
                ("a", "m1"): a_m1, ("f", "x2T"): f_x2T,
            })
            act.wait_ge(SEM["dm"], 1)
            act.activation(R.ex[:], R.dm[:], ACT.Exp).then_inc(SEM["exp_d"], 1)

            def scaled_rows(u, j):
                n = f"e{j}_"
                for s in range(2):
                    need(act, n + "xbT_ps", u, s + 1)
                    act.activation(xbT[j][0:HALF, s, :], X.ps[0:HALF, s, 0:CAP], ACT.Identity,
                                   bias=affine[:, AFFINE["f2"], 1, s:s + 1], scale=affine[:, AFFINE["f2"], 0, s:s + 1])\
                       .then_inc(SEM[n + "xbT"], 1)

            def hidden(u, j):
                n = f"e{j}_"
                if j == 1:
                    need(act, "e0_pj_ps", u)
                else:
                    need_last(act, "e1_pj_ps", u)
                for m in range(MT):
                    need(act, n + "fc_ps", u, m + 1)
                    ps = (X.ps[:, 2 + m % 4, :] if m % 4 < 2 else Y.ps[:, m % 4 - 2, :])
                    act.activation(heT[:, m, :], ps[:, 0:CAP], ACT.Gelu).then_inc(SEM[n + "he"], 1)

            def experts(u, more=True):
                hidden(u, 0)
                scaled_rows(u, 1)
                hidden(u, 1)
                if more:
                    scaled_rows(u + 1, 0)

            scaled_rows(0, 0)
            experts(0)
            with act.Fori(1, EXPERTS // 2 - 1) as u:
                experts(u)
            experts(EXPERTS // 2 - 1, more=False)

        @block.vector
        def _(dve):
            def ln(name, src):
                def part(c, u, g):
                    if src == "x2":
                        need(dve, f"{c.n}_x2", 2 * u + (name == "f2"))
                    elif src == "tok_ps":
                        need(dve, f"{c.n}_tok_ps", nth(TOKENS_X, "so", u))
                    elif src:
                        need(dve, f"{c.n}_{src}", u)
                    else:
                        need(dve, f"{c.n}_ln_out", norm_use(name, u) - 1)
                    if name == "a0":
                        need(dve, f"{c.n}_txt_in", u)
                    for t in range(TILES):
                        dve.bn_stats(c.st[:, t, :], c.norms[name].src(t)).then_inc(SEM[f"{c.n}_ln_stats"], 1)
                    need(dve, f"{c.n}_ln_stats", norm_use(name, u))
                    dve.memset(c.carrier[:], 0.0)
                    for t in range(TILES):
                        dve.bn_aggr(c.mv[:, t, :], c.st[:, t, :]).then_inc(SEM[f"{c.n}_ln_aggr"], 1)
                return part

            def lnx(name):
                def part(c, u, g):
                    if name == "a1":
                        need_last(dve, f"{c.n}_xh", u)
                    need(dve, f"{c.n}_ln_rstd", norm_use(name, u))
                    for t in range(TILES):
                        dve.tensor_scalar(c.norms[name].dst(t), c.norms[name].src(t), c.mv[:, t, 0:1], c.rs[:, t:t + 1],
                                          ALU.subtract, ALU.mult).then_inc(SEM[f"{c.n}_ln_out"], 1)
                return part

            def k_under_q(c, g):
                dve.memset(c.carrier[:], 0.0)
                dve.stream_shuffle(c.kT[:, g, :], c.qT[:, g, :], list(range(HD, 2 * HD)) * 2)\
                   .then_inc(SEM[f"{c.n}_k"], 1)

            def qkv(c, u, g):
                if g:
                    need(dve, f"{c.n}_k", nth(LAYERS, c.w, u), g)
                need(dve, f"{c.n}_q", use(c, u), g + 1)
                k_under_q(c, g)

            def S(c, u, g):
                n = c.n
                i = use(c, u)
                need(dve, f"{n}_S_ps", nth(LAYERS, c.w, u), g + 1)
                if g:
                    need(dve, f"{n}_P", i, g * GH * TILES)
                for b in (slice(0, 2), slice(2, 4)):
                    dve.tensor_reduce(c.negm[:, b, 0], c.ps[:, b, SEG[0]], AX, ALU.max, negate=True)\
                       .then_inc(SEM[f"{n}_negm"], 1)
                    dve.tensor_reduce(c.negm[:, b, 1:3],
                                      c.ps[:, b, P:W_Q].rearrange("p h (t k) -> p h t k", t=2),
                                      AX, ALU.max, negate=True).then_inc(SEM[f"{n}_negm"], 1)

            def T(c, u, g):
                n = c.n
                i = use(c, u)
                need(dve, f"{n}_T_ps", i, GH * g + 1)
                dve.tensor_copy(c.PT[:, 0, :], c.ps[:, 0, :]).then_inc(SEM[f"{n}_PTd"], 1)

            def T1(c, u, g):
                n = c.n
                i = use(c, u)
                need(dve, f"{n}_P", i, (g + 1) * GH * TILES)
                dve.reciprocal(c.rr[:], c.rsum[:]).then_inc(SEM[f"{n}_rr"], 1)
                need(dve, f"{n}_rr", i, g + 1)
                if g:
                    need(dve, f"{n}_R_ps", i, g)
                dve.tensor_copy(c.recb[:], c.rr[:].rearrange("p h t -> p t h").unsqueeze(3)
                                .to_broadcast([P, TILES, GH, 32])).then_inc(SEM[f"{n}_recb"], 1)
                need(dve, f"{n}_T_ps", i, GH * g + 3)
                dve.tensor_copy(c.PT[:, 2, :], c.ps[:, 2, :]).then_inc(SEM[f"{n}_PTd"], 1)

            def PV(c, u, g):
                n = c.n
                i = use(c, u)
                need(dve, f"{n}_R", i, g + 1)
                need(dve, f"{n}_PV_ps", nth(LAYERS, c.w, u), g + 1)
                halves = "p (s k) -> p s k"
                dve.tensor_tensor(c.OT[:, g, :].rearrange(halves, s=2), c.ps[:, 0:2, 0:SEQ],
                                  c.rec[:].rearrange(halves, s=2), ALU.mult)\
                   .then_inc(SEM[f"{n}_OT"], 1)

            def a_sqkv(c, u, g):
                need(dve, f"{c.n}_s_exp", u, g + 1)
                if g:
                    need(dve, f"{c.n}_s_phi", u, g)
                dve.tensor_scalar(c.r_ssm, c.ps[:, 2 * g % 4, 0:COLS], 0.0, ELU_EPS, ALU.max, ALU.add)\
                   .then_inc(SEM[f"{c.n}_s_relu"], 1)
                need(dve, f"{c.n}_s_relu", u, g + 1)
                dve.scalar_tensor_tensor(out=c.qT[:, g, :], in0=c.e_ssm[:, g % 2, :], scalar=1.0, in1=c.r_ssm,
                                         op0=ALU.min, op1=ALU.add).then_inc(SEM[f"{c.n}_s_phi"], 1)
                need(dve, f"{c.n}_s_phi", u, g + 1)
                k_under_q(c, g)

            def a_sST(c, u, g):
                need(dve, f"{c.n}_S_ps", nth(LAYERS, "ssm", u), g + 1)
                if g:
                    need(dve, f"{c.n}_PV_ps", nth(LAYERS, "ssm", u), g)
                dve.tensor_tensor(c.PT[:, :, 0:W_FULL], c.ps[:, :, 0:W_FULL],
                                  keep01[:].unsqueeze(1).to_broadcast([P, GH, W_FULL]), ALU.mult)\
                   .then_inc(SEM[f"{c.n}_s_PT"], 1)

            def a_sdiv(c, u, g):
                if g == 0:
                    need(dve, f"{c.n}_ao", u)
                need(dve, f"{c.n}_PV_ps", nth(LAYERS, "ssm", u), g + 1)
                dve.memset(c.carrier[:], 0.0)
                rec = c.rec[:].rearrange("p (s k) -> p s k", s=2)
                o = c.ps[:, 0:2, 0:SEQ]
                dve.stream_shuffle(rec, o, [HD] * 32).then_inc(SEM[f"{c.n}_s_div"], 1)
                need(dve, f"{c.n}_s_div", u, 3 * g + 1)
                dve.tensor_scalar(c.rec[:], c.rec[:], 1e-4 / SCALE, None, ALU.add).then_inc(SEM[f"{c.n}_s_div"], 1)
                need(dve, f"{c.n}_s_div", u, 3 * g + 2)
                dve.reciprocal(c.rec[:], c.rec[:]).then_inc(SEM[f"{c.n}_s_div"], 1)
                need(dve, f"{c.n}_s_div", u, 3 * g + 3)
                dve.tensor_tensor(c.OT[:, g, :].rearrange("p (s k) -> p s k", s=2), o, rec, ALU.mult)\
                   .then_inc(SEM[f"{c.n}_OT"], 1)

            def a_soT(c, u, g):
                need(dve, f"{c.n}_ao", u)
                for s in range(2):
                    need(dve, f"{c.n}_turned", nth(TURNED_X, "so", u), s + 1)
                    dve.scalar_tensor_tensor(out=c.xnT[0:HALF, s, :], in0=c.ps[0:HALF, s, 0:COLS],
                                             scalar=affine[:, AFFINE["so"], 0, s:s + 1], in1=c.aoT[:, s, :],
                                             op0=ALU.mult, op1=ALU.add).then_inc(SEM[f"{c.n}_u"], 1)

            def a_out(c, u, g):
                for t in range(TILES):
                    need(dve, f"{c.n}_tok_ps", nth(TOKENS_X, "out", u), t + 1)
                    dve.tensor_tensor(c.x2[:, t, :], c.ps[:, 1 + t, 0:D], c.xln[:, t, :], ALU.add)\
                       .then_inc(SEM[f"{c.n}_x2"], 1)

            def a_m2(c, u, t):
                if t == 0:
                    need(dve, f"{c.n}_hs", u)
                need(dve, f"{c.n}_m2_ps", u, t + 1)
                dve.tensor_tensor(c.h[:, t, :], c.ps[:, t, 0:D], c.h[:, t, :], ALU.add).then_inc(SEM[f"{c.n}_hF"], 1)

            def f_proj(c, u, g):
                for t in range(TILES):
                    need(dve, f"{c.n}_tok_ps", nth(TOKENS_X, "ffn", u), t + 1)
                    dve.tensor_tensor(c.x2[:, t, :], c.ps[:, 1 + t, 0:D], c.xln[:, t, :], ALU.add)\
                       .then_inc(SEM[f"{c.n}_x2"], 1)

            def f_logit(c, u, g):
                need(dve, f"{c.n}_lg_ps", u)
                dve.tensor_copy(logits[:, pair(c, u), :, :], c.ps[:, 2, 0:TILES * EXPERTS]
                                .rearrange("p (t e) -> p t e", t=TILES)).then_inc(SEM[f"{c.n}_lg"], 1)

            dve.wait_ge(ready, FILLS)
            dve.wait_ge(SEM["ld_const"], LOADED["const"])
            soft_parts = {"qkv": qkv, "S2": S, "T": T, "T1": T1, "PV1": PV}
            all_turns(dve, {**{(ph, n): part for ph in "af" for n, part in soft_parts.items()},
                ("a", "ln0"): ln("a0", "h0"), ("a", "ln0x"): lnx("a0"), ("a", "ln1"): ln("a1", None),
                ("a", "ln1x"): lnx("a1"), ("a", "sqkv"): a_sqkv, ("a", "sST1"): a_sST, ("a", "sdiv"): a_sdiv,
                ("a", "so"): ln("so", "tok_ps"), ("a", "sox"): lnx("so"), ("a", "soT"): a_soT,
                ("a", "out"): a_out, ("a", "lnm"): ln("am", "x2"), ("a", "lnmx"): lnx("am"), ("a", "m2"): a_m2,
                ("f", "ln0"): ln("f0", "hF"), ("f", "ln0x"): lnx("f0"), ("f", "ln1"): ln("f1", None),
                ("f", "ln1x"): lnx("f1"), ("f", "fproj"): f_proj, ("f", "ln2"): ln("f2", "x2"),
                ("f", "ln2x"): lnx("f2"), ("f", "logit"): f_logit,
            })

            done = [0]

            def link(ins):
                done[0] += 1
                ins.then_inc(SEM["route"], 1)
                dve.wait_ge(SEM["route"], done[0])

            lg = logits[:].rearrange("p a t e -> p (a t) e")
            for c in (X, Y):
                need(dve, f"{c.n}_lg", TURNS - 1)
            desc_b = desc[:].unsqueeze(1).to_broadcast([P, NT, EXPERTS])

            def per_expert(ap):
                return ap.unsqueeze(2).to_broadcast([P, NT, EXPERTS])

            def choose(k, src):
                link(dve.tensor_reduce(R.m[:, k, :], src, AX, ALU.max))
                link(dve.tensor_tensor(R.eq[:], src, per_expert(R.m[:, k, :]), ALU.is_equal))
                link(dve.tensor_tensor(R.cand[:], R.eq[:], desc_b, ALU.mult))
                link(dve.tensor_reduce(R.mc[:], R.cand[:], AX, ALU.max))
                link(dve.tensor_tensor(R.first[:, k, :, :], R.cand[:], per_expert(R.mc[:]), ALU.is_equal))
                dve.tensor_copy(R.fb[:, :, :, k, :], R.first[:, k, :, :].rearrange("p (a t) e -> p a t e", t=TILES))\
                   .then_inc(SEM["fbcast"], 1)

            def find_slots(k, ps):
                grid = "p (a e) -> p a e"
                dve.wait_ge(SEM["rank_ps"], k + 1)
                if k == 0:
                    link(dve.memset(R.base[:, 0, 0, :], 0.0))
                else:
                    link(dve.tensor_copy(R.base[:, 0, 1, :], R.base[:, PAIRS, 0, :]))
                for p in range(PAIRS):
                    link(dve.tensor_tensor(R.base[:, p + 1, k, :], R.base[:, p, k, :],
                                           ps[:, 3, p * EXPERTS:(p + 1) * EXPERTS], ALU.add))
                for t in range(TILES):
                    link(dve.tensor_tensor(R.rank[:, :, t, k, :], ps[:, t, 0:PAIRS * EXPERTS].rearrange(grid, a=PAIRS),
                                           R.base[:, 0:PAIRS, k, :], ALU.add))
                flat, some = "p a t k e -> p (a t) k e", "p a t k -> p (a t) k"
                rank, kept, slotv = (b[:].rearrange(flat)[:, :, k, :] for b in (R.rank, R.kept, R.slotv))
                slot, ks, dumpv, dumps, sidx = (b[:].rearrange(some)[:, :, k] for b in (R.slot, R.ks, R.dumpv, dump_id, R.sidx))
                link(dve.scalar_tensor_tensor(out=kept, in0=rank, scalar=float(CAP), in1=R.first[:, k, :, :],
                                              op0=ALU.is_lt, op1=ALU.mult))
                link(dve.tensor_tensor(slotv, rank, ebase[:].unsqueeze(1).to_broadcast([P, NT, EXPERTS]), ALU.add))
                link(dve.tensor_tensor(slotv, slotv, kept, ALU.mult))
                link(dve.tensor_reduce(slot, slotv, AX, ALU.add))
                link(dve.tensor_reduce(ks, kept, AX, ALU.add))
                link(dve.tensor_scalar(dumpv, ks, -1.0, 1.0, ALU.mult, ALU.add))
                link(dve.tensor_tensor(dumpv, dumpv, dumps, ALU.mult))
                link(dve.tensor_tensor(dumpv, dumpv, slot, ALU.add))
                dve.tensor_copy(sidx, dumpv).then_inc(SEM["slots"], 1)

            ids = xh_all[:, :, :, D]
            dve.tensor_copy(ids, home_id[:]).then_inc(SEM["ids"], 1)
            choose(0, lg)
            link(dve.scalar_tensor_tensor(out=R.l2[:], in0=R.first[:, 0, :, :], scalar=-3.0e38, in1=lg,
                                          op0=ALU.mult, op1=ALU.add))
            find_slots(0, X.ps)
            choose(1, R.l2[:])
            dve.tensor_tensor(R.dm[:], R.m[:, 1, :], R.m[:, 0, :], ALU.subtract).then_inc(SEM["dm"], 1)
            find_slots(1, Y.ps)
            dve.wait_ge(SEM["exp_d"], 1)
            link(dve.tensor_scalar(R.den[:], R.ex[:], 1.0, None, ALU.add))
            link(dve.reciprocal(R.p[:, 0, :], R.den[:]))
            link(dve.tensor_tensor(R.p[:, 1, :], R.ex[:], R.p[:, 0, :], ALU.mult))
            for k in range(2):
                link(dve.tensor_tensor(R.wgt[:, :, :, k], R.ks[:, :, :, k],
                                       R.p[:, k, :].rearrange("p (a t) -> p a t", t=TILES), ALU.mult))
            for j in range(2):
                dve.wait_ge(scat[j], 16 * NT // 2)
                half = ids[:, j * PAIRS // 2:(j + 1) * PAIRS // 2, :]
                dve.tensor_scalar(half, half, 1.0, None, ALU.add).then_inc(SEM["ids"], 1)

            def expert(u, j):
                n = f"e{j}_"
                need(dve, n + "xb_in", u)
                need_last(dve, n + "st", u)
                dve.scalar_tensor_tensor(out=home_f[j][:], in0=xb[j][:, :, D], scalar=0.0, in1=empty_id[0:SLOTS, j, :],
                                         op0=ALU.is_equal, op1=ALU.mult).then_inc(SEM[n + "home"], 1)
                need(dve, n + "home", u, 1)
                dve.tensor_tensor(home_f[j][:], home_f[j][:], xb[j][:, :, D], ALU.add).then_inc(SEM[n + "home"], 1)
                need(dve, n + "home", u, 2)
                dve.tensor_copy(home[j][:], home_f[j][:]).then_inc(SEM[n + "home"], 1)
                need(dve, n + "bp_in", u)
                for t in range(SLOT_TILES):
                    need(dve, n + "pj_ps", u, t + 1)
                    dve.tensor_tensor(ob[j][:, t, :], Y.ps[0:SLOTS, 2 + t % 2, 0:D], b_pj[j][0:SLOTS, :], ALU.add)\
                       .then_inc(SEM[n + "ob"], 1)

            for j in range(2):
                expert(0, j)
            with dve.Fori(1, EXPERTS // 2) as u:
                for j in range(2):
                    expert(u, j)

            for p in range(PAIRS):
                dve.wait_ge(gat[p], 16)
                for k, done_ in enumerate(("ymid", "yout")):
                    for t in range(TILES):
                        n = TILES * p + t
                        if k == 1:
                            dve.wait_ge(SEM["ymid"], n + 1)
                        dve.scalar_tensor_tensor(out=y_out[:, n, :], in0=g_rows[p][:, t, k, :],
                                                 scalar=R.wgt[:, p, t, k:k + 1],
                                                 in1=hx_all[:, p, t, :] if k == 0 else y_out[:, n, :],
                                                 op0=ALU.mult, op1=ALU.add).then_inc(SEM[done_], 1)

        @block.gpsimd
        def _(pool):
            fills = [(ones_row[:], 1.0), (onesb[:], 1.0), (neghalf[:], -0.5), (eps[:], EPS)]
            fills += [(c.V[:], 0.0) for c in (X, Y)]
            fills += [(c.V[:, :, :, HD:HD + 1], 1.0) for c in (X, Y)]
            fills += [(c.xnT[HALF:HALF + 1, :, :], 1.0) for c in (X, Y)]
            pool.memset(zrow, 0.0).then_inc(SEM["zero"], 1)
            pool.wait_ge(SEM["zero"], 1)
            assert len(fills) == FILLS
            for n, (buf, value) in enumerate(fills):
                pool.memset(buf, value).then_inc(ready, 1)
                pool.wait_ge(ready, n + 1)

            def rstd(name):
                def part(c, u, g):
                    i = norm_use(name, u)
                    need(pool, f"{c.n}_ln_aggr", i)
                    pool.tensor_tensor(c.ve[:], c.mv[:, :, 1], eps[:], ALU.add).then_inc(SEM[f"{c.n}_ln_rstd"], 1)
                    need(pool, f"{c.n}_ln_rstd", i, 1)
                    pool.tensor_tensor(c.rs[:], c.ve[:], neghalf[:], ALU.pow).then_inc(SEM[f"{c.n}_ln_rstd"], 1)
                return part

            def a_lnm(c, u, g):
                rstd("am")(c, u, g)
                if isinstance(u, int):
                    pool.wait_ge(SEM["ld_mlp"], LOADED["mlp"])
                need(pool, f"{c.n}_x2", 2 * u)
                pool.tensor_tensor(c.h[:], c.x2[:], c.h[:], ALU.add).then_inc(SEM[f"{c.n}_hx2"], 1)
                need(pool, f"{c.n}_hx2", u)
                pool.tensor_tensor(c.h[:], c.h[:], b_m2[:].unsqueeze(1).to_broadcast([P, TILES, D]), ALU.add)\
                    .then_inc(SEM[f"{c.n}_hs"], 1)

            def f_ln2(c, u, g):
                rstd("f2")(c, u, g)
                need(pool, f"{c.n}_x2", 2 * u + 1)
                apart(pool)
                pool.tensor_tensor(hx_all[:, pair(c, u), :, :], c.x2[:], c.h[:], ALU.add).then_inc(SEM[f"{c.n}_hx"], 1)
                need(pool, f"{c.n}_ln_out", norm_use("f2", u))
                apart(pool)
                pool.tensor_copy(xh_all[:, pair(c, u), :, 0:D], c.xhat[:]).then_inc(SEM[f"{c.n}_xh"], 1)

            all_turns(pool, {
                ("a", "ln0"): rstd("a0"), ("a", "ln1"): rstd("a1"), ("a", "so"): rstd("so"), ("a", "lnm"): a_lnm,
                ("f", "ln0"): rstd("f0"), ("f", "ln1"): rstd("f1"), ("f", "ln2"): f_ln2,
            })
            for c in (X, Y):
                need(pool, f"{c.n}_lg", TURNS - 1)
                need(pool, f"{c.n}_xh", TURNS - 1)
            for j in range(2):
                pool.memset(xbT[j][HALF:HALF + 1, :, :], 1.0).then_inc(SEM["xb_ones"], 1)
                pool.wait_ge(SEM["xb_ones"], j + 1)
            pool.wait_ge(SEM["zfill"], ZFILL)
            for k in range(2):
                pool.wait_ge(SEM["slots"], k + 1)
                for n in range(NT):
                    p, t = n // TILES, n % TILES
                    half = 2 * n // NT
                    pool.wait_ge(SEM["ids"], 1 if k == 0 else 2 + half)
                    pool.indirect_dma_start(out=xb_dram, out_offset=bass.IndirectOffsetOnAxis(ap=R.sidx[:, p, t, k:k + 1], axis=0),
                                            in_=xh_all[:, p, t, :], in_offset=None).then_inc(scat[half], 16)

            def rows_home(u, j):
                need_last(pool, f"e{j}_carried", u)
                need(pool, f"e{j}_home", u)
                for t in range(SLOT_TILES):
                    need(pool, f"e{j}_ob", u, t + 1)
                    pool.tensor_tensor(pool_carrier[:, SLOT_TILES * j + t:SLOT_TILES * j + t + 1], eps[:, 0:1], eps[:, 0:1], ALU.add)\
                        .then_inc(SEM[f"e{j}_carried"], 1)
                    pool.indirect_dma_start(out=home_dram, out_offset=bass.IndirectOffsetOnAxis(ap=home[j][:, t:t + 1], axis=0),
                                            in_=ob[j][:, t, :], in_offset=None).then_inc(SEM[f"e{j}_st"], 16)

            for j in range(2):
                rows_home(0, j)
            with pool.Fori(1, EXPERTS // 2) as u:
                for j in range(2):
                    rows_home(u, j)


def constants(np):
    bf = np.dtype("bfloat16")
    i_txt, j_txt = np.arange(IMG, SEQ), np.arange(IMG, SEQ)
    c = {}
    pos = np.stack([np.concatenate([np.arange(IMG), SEQ + np.arange(IMG)]),
                    IMG + np.arange(TXT), SEQ + IMG + np.arange(TXT)])
    seq = [np.concatenate([i_txt, np.arange(IMG)]), np.arange(SEQ)]
    for kind, off in (("win", -40960.0), ("full", -1e30)):
        def valid(i, j):
            ok = j <= i
            return ok & (j > i - WINDOW) if kind == "win" else ok
        txt_q = IMG + np.arange(P)[:, None]
        m = np.concatenate([valid(pos[0][:, None], pos[0][None]) & (pos[0][:, None] // SEQ == pos[0][None] // SEQ)]
                           + [valid(txt_q, s[None]) for s in seq], 1)
        c["mask_" + kind] = np.where(m, 0.0, off).astype(bf)
    t = j_txt[:, None] <= i_txt[None]
    img_k = np.arange(P)[:, None] % IMG
    c["keep01"] = np.concatenate([img_k <= np.repeat(np.stack(seq), IMG, axis=0), t, t], 1).astype(np.float32)
    c["identf"] = np.eye(P, dtype=np.float32)
    c["identb"] = np.eye(P).astype(bf)
    c["order"] = np.stack([pos[s][:, None] < pos[t][None] for s in range(TILES) for t in range(TILES)], 1).astype(bf)
    c["desc"] = np.tile(np.arange(EXPERTS, 0, -1, dtype=np.float32), (P, 1))
    c["ebase"] = np.tile(CAP * np.arange(EXPERTS, dtype=np.float32), (P, 1))
    n = np.arange(PAIRS * TILES).reshape(PAIRS, TILES)[None, :, :, None] * P + np.arange(P)[:, None, None, None]
    c["empty_id"] = (HOME + CAP * np.arange(2)[None, :, None] + SLOTS * np.arange(SLOT_TILES)
                     + np.arange(P)[:, None, None]).astype(np.float32)
    c["home_id"] = (1 + 2 * n[..., 0]).astype(np.float32)
    c["dump_id"] = (DUMP + TOKENS * np.arange(2)[None, None, None, :] + n).astype(np.float32)
    return c


def layout(np, x):
    f = {k: np.asarray(v) for k, v in x.items()}
    z = np.zeros
    o = {}
    patches = f["x"].reshape(BATCH, 3, 2 * 4, 16, 8, 16)
    patches = patches.transpose(1, 3, 5, 0, 2, 4).reshape(KT, P, PAIRS, P)
    o["xT"] = patches.transpose(2, 1, 0, 3)
    o["txt"] = f["txt"].reshape(PAIRS, 2, TXT, D).transpose(0, 2, 1, 3)
    o["w_tok"] = f["L0_tok_W"].T.reshape(KT, P, D).transpose(1, 0, 2)
    o["b_tok"] = f["L0_tok_b"].reshape(1, D)

    def biased(w, b):
        r = z((HALF + 1, 2, w.shape[1]), np.float32)
        r[0:HALF] = w.reshape(2, HALF, -1).transpose(1, 0, 2)
        r[HALF, 1] = b
        return r

    for n, key in (("attn", "L0_attn_attn_qkv"), ("ssm", "L0_attn_ssm_qkv"), ("ffn", "L0_ffn_attn_qkv")):
        w, b = f[key + "_w"], f[key + "_b"]
        full = biased(w, b)
        qk = full[:, :, 0:2 * D].reshape(HALF + 1, 2, 2, GROUPS, GH, HD).transpose(0, 1, 3, 4, 2, 5)
        o["wqk_" + n] = qk.reshape(HALF + 1, 2, GROUPS, P)
        o["wv_" + n] = full[:, :, 2 * D:]
    for n, wk, bk in (("attn", "L0_attn_attn_proj_w", "L0_attn_attn_proj_b"), ("ssm", "L0_attn_ssm_out_w", None),
                      ("ffn", "L0_ffn_attn_proj_w", "L0_ffn_attn_proj_b")):
        r = z((GROUPS, GH, 32, D), np.float32)
        r[:, :, 0:HD] = f[wk].reshape(GROUPS, GH, HD, D)
        if bk:
            r[0, 0, HD] = f[bk]
        o["wp_" + n] = r.reshape(GROUPS, P, D).transpose(1, 0, 2)
    o["b_so"] = f["L0_attn_ssm_out_b"].reshape(1, D)
    o["w_out"] = biased(f["L0_attn_out_w"], f["L0_attn_out_b"])
    o["w_m1"] = biased(f["L0_attn_mlp_w1"], f["L0_attn_mlp_b1"])
    o["w_m2"] = f["L0_attn_mlp_w2"].reshape(MT, P, D).transpose(1, 0, 2)
    o["b_m2"] = f["L0_attn_mlp_b2"].reshape(1, D)
    o["w_g"] = f["L0_ffn_w_g"].reshape(2, HALF, EXPERTS).transpose(1, 0, 2)
    norms = (("L0_attn_ln1_g", "L0_attn_ln1_b"), ("L0_attn_ssm_ln_g", "L0_attn_ssm_ln_b"),
             ("L0_attn_lnm_g", "L0_attn_lnm_b"), ("L0_ffn_ln1_w", "L0_ffn_ln1_b"), ("L0_ffn_ln2_w", "L0_ffn_ln2_b"))
    o["affine"] = np.stack([np.stack([f[k].reshape(2, HALF) for k in ab]) for ab in norms]).transpose(3, 0, 1, 2)
    o["e_fc"] = np.stack([biased(f["L0_ffn_exp_fc_w"][e], f["L0_ffn_exp_fc_b"][e, 0]) for e in range(EXPERTS)])
    o["e_pj"] = f["L0_ffn_exp_proj_w"].reshape(EXPERTS, MT, P, D).transpose(0, 2, 1, 3)
    o["e_bpj"] = f["L0_ffn_exp_proj_b"].reshape(EXPERTS, 1, D)
    return o


def kernel(**inputs):
    import numpy as np
    import concourse.bacc as bacc
    from concourse.bass_utils import run_bass_kernel_spmd as run

    nc = bacc.Bacc("TRN2", target_bir_lowering=False, num_devices=1)
    arrays = {k: np.ascontiguousarray(v) for k, v in {**constants(np), **layout(np, inputs)}.items()}
    d = Named({k: nc.dram_tensor(k + "_dram", a.shape, mybir.dt.from_np(a.dtype), kind="ExternalInput").ap()
               for k, a in arrays.items()})
    out = nc.dram_tensor("out_dram", (BATCH, SEQ, D), F32, kind="ExternalOutput").ap()
    build(nc, d, out)
    r = run(nc, [{k + "_dram": a for k, a in arrays.items()}], core_ids=[0])
    return r.results[0]["out_dram"]
```
